# Optimizing a Trainium2 kernel written in Bass

```python
import numpy as np
import jax
import jax.numpy as jnp

def _softmax(x, axis=-1):
    return jax.nn.softmax(x, axis=axis)

def _gelu(x):
    return jax.nn.gelu(x, approximate=True)

def _silu(x):
    return jax.nn.silu(x)

def _sigmoid(x):
    return jax.nn.sigmoid(x)

def _layernorm(x, axis=-1, eps=1e-05):
    m = jnp.mean(x, axis=axis, keepdims=True)
    v = jnp.var(x, axis=axis, keepdims=True)
    return (x - m) / jnp.sqrt(v + eps)

def _scatter_add(tgt, idx, src, axis=0):
    return tgt.at[idx].add(src)

def _segment_sum(src, seg, n):
    return jax.ops.segment_sum(src, seg, n)
kernel_name = 'mk_adaln_d2_jaxref_r8_907000'

def setup_inputs(seed: int=0):
    np.random.seed(seed)
    _w = jnp.asarray

    def _L0_attn_setup():
        import math
        import jax, jax.numpy as jnp
        import numpy as np
        N_HEADS = 16
        N_KV_HEADS = 4
        HEAD_DIM = 64
        DIM = 128
        WINDOW = 16
        EPS = 0.01

        def _alibi_slopes(n_heads):
            closest = 2 ** math.floor(math.log2(n_heads))
            base = 2.0 ** (-2.0 ** (-(math.log2(closest) - 3)))
            slopes = base ** np.arange(1, closest + 1, dtype=np.float32)
            if closest < n_heads:
                eb = 2.0 ** (-2.0 ** (-(math.log2(2 * closest) - 3)))
                extra = eb ** np.arange(1, 2 * (n_heads - closest) + 1, 2, dtype=np.float32)
                slopes = np.concatenate([slopes, extra])
            return jnp.asarray(slopes[:n_heads])

        def _rmsnorm(x, w):
            xf = x.astype(jnp.float32)
            norm = jax.lax.rsqrt(jnp.mean(xf * xf, axis=-1, keepdims=True) + EPS)
            return (xf * norm).astype(x.dtype) * w
        key = jax.random.key(seed)
        ks = jax.random.split(key, 6)
        B, L = (2, 256)
        s = 1.0 / math.sqrt(DIM)
        return {'x': jax.random.normal(ks[0], (B, L, DIM), jnp.float32), 'wq': jax.random.normal(ks[1], (N_HEADS * HEAD_DIM, DIM), jnp.float32) * s, 'wk': jax.random.normal(ks[2], (N_KV_HEADS * HEAD_DIM, DIM), jnp.float32) * s, 'wv': jax.random.normal(ks[3], (N_KV_HEADS * HEAD_DIM, DIM), jnp.float32) * s, 'wo': jax.random.normal(ks[4], (DIM, N_HEADS * HEAD_DIM), jnp.float32) * s, 'q_norm_w': jnp.ones((HEAD_DIM,), jnp.float32), 'k_norm_w': jnp.ones((HEAD_DIM,), jnp.float32)}
    _L0_attn_in = _L0_attn_setup()

    def _L0_ffn_setup():
        import jax, jax.numpy as jnp
        import numpy as np
        HIDDEN = 128
        NUM_EXPERTS = 8
        TOP_K = 2
        key = jax.random.key(seed)
        k_x, k_r, k_w1, k_w2 = jax.random.split(key, 4)
        x = jax.random.normal(k_x, (4, 256, HIDDEN), dtype=jnp.float32)
        router_w = jax.random.normal(k_r, (NUM_EXPERTS, HIDDEN), dtype=jnp.float32) * HIDDEN ** (-0.5)
        w1 = jax.random.normal(k_w1, (NUM_EXPERTS, HIDDEN, 2 * HIDDEN), dtype=jnp.float32) * HIDDEN ** (-0.5)
        w2 = jax.random.normal(k_w2, (NUM_EXPERTS, 2 * HIDDEN, HIDDEN), dtype=jnp.float32) * (2 * HIDDEN) ** (-0.5)
        return {'x': x, 'router_w': router_w, 'w1': w1, 'w2': w2}
    _L0_ffn_in = _L0_ffn_setup()
    _L0_c = _w((lambda *s: np.random.randn(*s).astype(np.float32) * 0.05)(8, 128))
    _L0_wmod = _w((lambda *s: np.random.randn(*s).astype(np.float32) * 0.05)(128, 6 * 128) * 128 ** (-0.5))

    def _L1_attn_setup():
        import jax, jax.numpy as jnp
        import numpy as np
        B, S, HID = (2, 256, 128)
        H = 16
        D = HID // H
        SPARSITY = 0.9

        def _sparse_attn(x, Wq, bq, Wk, bk, Wv, bv, Wo, bo):
            b, s, hid = x.shape
            d = hid // H

            def heads(y):
                return y.reshape(b, s, H, d).transpose(0, 2, 1, 3)
            Q = heads(x @ Wq + bq)
            K = heads(x @ Wk + bk)
            V = heads(x @ Wv + bv)
            scores = jnp.einsum('bhqd,bhkd->bhqk', Q, K) / np.sqrt(d)
            k_keep = int(s * (1.0 - SPARSITY))
            vals, idx = jax.lax.top_k(scores, k_keep)
            n = b * H * s
            rows = jnp.arange(n)[:, None]
            sparse = jnp.zeros((n, s), scores.dtype).at[rows, idx.reshape(n, k_keep)].set(vals.reshape(n, k_keep)).reshape(b, H, s, s)
            attn = jax.nn.softmax(sparse, axis=-1)
            out = jnp.einsum('bhqk,bhkd->bhqd', attn, V)
            out = out.transpose(0, 2, 1, 3).reshape(b, s, hid)
            return out @ Wo + bo
        key = jax.random.key(seed)
        ks = jax.random.split(key, 5)
        sc = 1.0 / np.sqrt(HID)
        inp = {'x': jax.random.normal(ks[0], (B, S, HID), jnp.float32)}
        for i, name in enumerate(['q', 'k', 'v', 'o']):
            inp[f'W{name}'] = jax.random.normal(ks[i + 1], (HID, HID), jnp.float32) * sc
            inp[f'b{name}'] = jnp.zeros((HID,), jnp.float32)
        return inp
    _L1_attn_in = _L1_attn_setup()

    def _L1_ffn_setup():
        import jax, jax.numpy as jnp
        import numpy as np
        NUM_HEADS = 16
        TOP_K = 2
        key = jax.random.key(seed)
        ks = jax.random.split(key, 5)
        B, S, D, E = (4, 256, 128, 8)
        scale = 0.02
        return {'x': jax.random.normal(ks[0], (B, S, D), dtype=jnp.float32), 'W_qkv': jax.random.normal(ks[1], (D, 3 * D), dtype=jnp.float32) * scale, 'b_qkv': jnp.zeros((3 * D,), dtype=jnp.float32), 'W_gate': jax.random.normal(ks[2], (D, E), dtype=jnp.float32) * scale, 'b_gate': jnp.zeros((E,), dtype=jnp.float32), 'W_experts': jax.random.normal(ks[3], (E, D, D), dtype=jnp.float32) * scale, 'b_experts': jnp.zeros((E, D), dtype=jnp.float32)}
    _L1_ffn_in = _L1_ffn_setup()
    _L1_c = _w((lambda *s: np.random.randn(*s).astype(np.float32) * 0.05)(8, 128))
    _L1_wmod = _w((lambda *s: np.random.randn(*s).astype(np.float32) * 0.05)(128, 6 * 128) * 128 ** (-0.5))
    _d = {'L0_attn_x': _L0_attn_in['x'], 'L0_attn_wq': _L0_attn_in['wq'], 'L0_attn_wk': _L0_attn_in['wk'], 'L0_attn_wv': _L0_attn_in['wv'], 'L0_attn_wo': _L0_attn_in['wo'], 'L0_attn_q_norm_w': _L0_attn_in['q_norm_w'], 'L0_attn_k_norm_w': _L0_attn_in['k_norm_w'], 'L0_ffn_router_w': _L0_ffn_in['router_w'], 'L0_ffn_w1': _L0_ffn_in['w1'], 'L0_ffn_w2': _L0_ffn_in['w2'], 'L0_c': _L0_c, 'L0_wmod': _L0_wmod, 'L1_attn_Wq': _L1_attn_in['Wq'], 'L1_attn_bq': _L1_attn_in['bq'], 'L1_attn_Wk': _L1_attn_in['Wk'], 'L1_attn_bk': _L1_attn_in['bk'], 'L1_attn_Wv': _L1_attn_in['Wv'], 'L1_attn_bv': _L1_attn_in['bv'], 'L1_attn_Wo': _L1_attn_in['Wo'], 'L1_attn_bo': _L1_attn_in['bo'], 'L1_ffn_W_qkv': _L1_ffn_in['W_qkv'], 'L1_ffn_b_qkv': _L1_ffn_in['b_qkv'], 'L1_ffn_W_gate': _L1_ffn_in['W_gate'], 'L1_ffn_b_gate': _L1_ffn_in['b_gate'], 'L1_ffn_W_experts': _L1_ffn_in['W_experts'], 'L1_ffn_b_experts': _L1_ffn_in['b_experts'], 'L1_c': _L1_c, 'L1_wmod': _L1_wmod}
    _x0 = _d['L0_attn_x']
    _d['L0_attn_x'] = jax.random.normal(jax.random.fold_in(jax.random.key(seed), 1), (8, 512, 128), dtype=_x0.dtype)
    del _x0
    return _d

def reference(L0_attn_x, L0_attn_wq, L0_attn_wk, L0_attn_wv, L0_attn_wo, L0_attn_q_norm_w, L0_attn_k_norm_w, L0_ffn_router_w, L0_ffn_w1, L0_ffn_w2, L0_c, L0_wmod, L1_attn_Wq, L1_attn_bq, L1_attn_Wk, L1_attn_bk, L1_attn_Wv, L1_attn_bv, L1_attn_Wo, L1_attn_bo, L1_ffn_W_qkv, L1_ffn_b_qkv, L1_ffn_W_gate, L1_ffn_b_gate, L1_ffn_W_experts, L1_ffn_b_experts, L1_c, L1_wmod):

    def _L0_attn_ref(x, wq, wk, wv, wo, q_norm_w, k_norm_w):
        import math
        import jax, jax.numpy as jnp
        import numpy as np
        N_HEADS = 16
        N_KV_HEADS = 4
        HEAD_DIM = 64
        DIM = 128
        WINDOW = 16
        EPS = 0.01

        def _alibi_slopes(n_heads):
            closest = 2 ** math.floor(math.log2(n_heads))
            base = 2.0 ** (-2.0 ** (-(math.log2(closest) - 3)))
            slopes = base ** np.arange(1, closest + 1, dtype=np.float32)
            if closest < n_heads:
                eb = 2.0 ** (-2.0 ** (-(math.log2(2 * closest) - 3)))
                extra = eb ** np.arange(1, 2 * (n_heads - closest) + 1, 2, dtype=np.float32)
                slopes = np.concatenate([slopes, extra])
            return jnp.asarray(slopes[:n_heads])

        def _rmsnorm(x, w):
            xf = x.astype(jnp.float32)
            norm = jax.lax.rsqrt(jnp.mean(xf * xf, axis=-1, keepdims=True) + EPS)
            return (xf * norm).astype(x.dtype) * w
        B, L, _ = x.shape
        n_rep = N_HEADS // N_KV_HEADS
        q = (x @ wq.T).reshape(B, L, N_HEADS, HEAD_DIM)
        k = (x @ wk.T).reshape(B, L, N_KV_HEADS, HEAD_DIM)
        v = (x @ wv.T).reshape(B, L, N_KV_HEADS, HEAD_DIM)
        q = _rmsnorm(q, q_norm_w)
        k = _rmsnorm(k, k_norm_w)
        k = jnp.broadcast_to(k[:, :, None], (B, L, n_rep, N_KV_HEADS, HEAD_DIM)).reshape(B, L, N_HEADS, HEAD_DIM)
        v = jnp.broadcast_to(v[:, :, None], (B, L, n_rep, N_KV_HEADS, HEAD_DIM)).reshape(B, L, N_HEADS, HEAD_DIM)
        pos = jnp.arange(L)
        rel = pos[None, :] - pos[:, None]
        slopes = _alibi_slopes(N_HEADS)
        bias = slopes[:, None, None] * rel[None].astype(jnp.float32)
        masked = (rel > 0) | (rel < -WINDOW)
        bias = jnp.where(masked[None], -jnp.inf, bias)
        scale = 1.0 / math.sqrt(HEAD_DIM)
        attn = jnp.einsum('bqhd,bkhd->bhqk', q, k) * scale + bias[None]
        attn = jax.nn.softmax(attn, axis=-1)
        out = jnp.einsum('bhqk,bkhd->bqhd', attn, v).reshape(B, L, N_HEADS * HEAD_DIM)
        return out @ wo.T

    def _L0_ffn_ref(x, router_w, w1, w2):
        import jax, jax.numpy as jnp
        import numpy as np
        HIDDEN = 128
        NUM_EXPERTS = 8
        TOP_K = 2
        bsz, seq, hidden = x.shape
        tokens = x.reshape(-1, hidden)
        logits = tokens @ router_w.T
        topk_vals, topk_idx = jax.lax.top_k(logits, TOP_K)
        weights = jax.nn.softmax(topk_vals, axis=-1)
        h = jnp.einsum('td,edf->etf', tokens, w1)
        h = jax.nn.gelu(h, approximate=False)
        out_all = jnp.einsum('etf,efd->etd', h, w2)
        out_ted = jnp.transpose(out_all, (1, 0, 2))
        gathered = jnp.take_along_axis(out_ted, topk_idx[:, :, None], axis=1)
        output = jnp.sum(weights[:, :, None] * gathered, axis=1)
        return output.reshape(bsz, seq, hidden)

    def _L1_attn_ref(x, Wq, bq, Wk, bk, Wv, bv, Wo, bo):
        import jax, jax.numpy as jnp
        import numpy as np
        B, S, HID = (2, 256, 128)
        H = 16
        D = HID // H
        SPARSITY = 0.9

        def _sparse_attn(x, Wq, bq, Wk, bk, Wv, bv, Wo, bo):
            b, s, hid = x.shape
            d = hid // H

            def heads(y):
                return y.reshape(b, s, H, d).transpose(0, 2, 1, 3)
            Q = heads(x @ Wq + bq)
            K = heads(x @ Wk + bk)
            V = heads(x @ Wv + bv)
            scores = jnp.einsum('bhqd,bhkd->bhqk', Q, K) / np.sqrt(d)
            k_keep = int(s * (1.0 - SPARSITY))
            vals, idx = jax.lax.top_k(scores, k_keep)
            n = b * H * s
            rows = jnp.arange(n)[:, None]
            sparse = jnp.zeros((n, s), scores.dtype).at[rows, idx.reshape(n, k_keep)].set(vals.reshape(n, k_keep)).reshape(b, H, s, s)
            attn = jax.nn.softmax(sparse, axis=-1)
            out = jnp.einsum('bhqk,bhkd->bhqd', attn, V)
            out = out.transpose(0, 2, 1, 3).reshape(b, s, hid)
            return out @ Wo + bo
        return _sparse_attn(x, Wq, bq, Wk, bk, Wv, bv, Wo, bo)

    def _L1_ffn_ref(x, W_qkv, b_qkv, W_gate, b_gate, W_experts, b_experts):
        import jax, jax.numpy as jnp
        import numpy as np
        NUM_HEADS = 16
        TOP_K = 2
        B, S, D = x.shape
        H = NUM_HEADS
        hd = D // H
        E = W_gate.shape[-1]
        qkv = (x @ W_qkv + b_qkv).reshape(B, S, 3, H, hd)
        q, k, v = (qkv[:, :, 0], qkv[:, :, 1], qkv[:, :, 2])
        attn = jnp.einsum('bqhd,bkhd->bhqk', q, k) / jnp.sqrt(jnp.asarray(hd, x.dtype))
        attn = jax.nn.softmax(attn, axis=-1)
        attn_out = jnp.einsum('bhqk,bkhd->bqhd', attn, v).reshape(B, S, D)
        gate = jax.nn.softmax(x @ W_gate + b_gate, axis=-1)
        top_g, top_i = jax.lax.top_k(gate, TOP_K)
        combine = jnp.sum(jax.nn.one_hot(top_i, E, dtype=x.dtype) * top_g[..., None], axis=2)
        expert_out = jnp.einsum('bsd,edf->bsef', x, W_experts) + b_experts
        moe_out = jnp.einsum('bsef,bse->bsf', expert_out, combine)
        return attn_out + moe_out
    x = L0_attn_x
    mod = (_silu(L0_c) @ L0_wmod).reshape(L0_c.shape[0], 6, 1, -1)
    sa, ca, ga, sb, cb, gb = (mod[:, 0], mod[:, 1], mod[:, 2], mod[:, 3], mod[:, 4], mod[:, 5])
    ga = (2 * (ga >= 0) - 1) * jnp.maximum(jnp.abs(ga), 0.25)
    gb = (2 * (gb >= 0) - 1) * jnp.maximum(jnp.abs(gb), 0.25)
    h = _layernorm(x, axis=-1) * (1 + ca) + sa
    x = x + ga * _L0_attn_ref(h, L0_attn_wq, L0_attn_wk, L0_attn_wv, L0_attn_wo, L0_attn_q_norm_w, L0_attn_k_norm_w)
    h = _layernorm(x, axis=-1) * (1 + cb) + sb
    x = x + gb * _L0_ffn_ref(h, L0_ffn_router_w, L0_ffn_w1, L0_ffn_w2)
    mod = (_silu(L1_c) @ L1_wmod).reshape(L1_c.shape[0], 6, 1, -1)
    sa, ca, ga, sb, cb, gb = (mod[:, 0], mod[:, 1], mod[:, 2], mod[:, 3], mod[:, 4], mod[:, 5])
    ga = (2 * (ga >= 0) - 1) * jnp.maximum(jnp.abs(ga), 0.25)
    gb = (2 * (gb >= 0) - 1) * jnp.maximum(jnp.abs(gb), 0.25)
    h = _layernorm(x, axis=-1) * (1 + ca) + sa
    x = x + ga * _L1_attn_ref(h, L1_attn_Wq, L1_attn_bq, L1_attn_Wk, L1_attn_bk, L1_attn_Wv, L1_attn_bv, L1_attn_Wo, L1_attn_bo)
    h = _layernorm(x, axis=-1) * (1 + cb) + sb
    x = x + gb * _L1_ffn_ref(h, L1_ffn_W_qkv, L1_ffn_b_qkv, L1_ffn_W_gate, L1_ffn_b_gate, L1_ffn_W_experts, L1_ffn_b_experts)
    return x

_drawn_inputs = setup_inputs


def setup_inputs(seed=0):
    import zlib

    import numpy as np

    out = dict(_drawn_inputs(seed))
    spreads = {'L0_attn_q_norm_w': (1.0, 0.2),
     'L0_attn_k_norm_w': (1.0, 0.2),
     'L1_attn_bq': (0.0, 2.0),
     'L1_attn_bk': (0.0, 2.0),
     'L1_attn_bv': (0.0, 0.309),
     'L1_attn_bo': (0.0, 0.359),
     'L1_ffn_b_qkv': (0.0, 0.324),
     'L1_ffn_b_gate': (0.0, 0.8),
     'L1_ffn_b_experts': (0.0, 0.8)}
    factors = {'L1_ffn_W_qkv': 8.0, 'L1_ffn_W_gate': 5.067, 'L1_ffn_W_experts': 4.545}
    for name, (base, spread) in spreads.items():
        noise = np.random.default_rng([zlib.crc32(name.encode()), seed]).standard_normal(out[name].shape)
        drawn = base * np.exp(spread * noise) if base else spread * noise
        out[name] = jnp.asarray(drawn.astype(out[name].dtype))
    for name, factor in factors.items():
        out[name] = (out[name] * factor).astype(out[name].dtype)
    return out
```

```python
from contextlib import ExitStack

import concourse.bass as bass
from concourse import mybir

F32 = mybir.dt.float32
BF16 = mybir.dt.bfloat16
ALU = mybir.AluOpType
ACT = mybir.ActivationFunctionType
AX = mybir.AxisListType

P = 128
B = 8
S = 512
TB = S // P
HEADS = 16

HD0 = 64
KV0 = 4
PAIRS = HEADS // 2
WINDOW = 16
SUB = 32
WIN = SUB + WINDOW
SLOT = 64
EPS0 = 0.01

EX = 8
FF = 256

HD1 = 8
KEEP = int(S * (1.0 - 0.9))
LN_EPS = 1e-5
GATE_MIN = 0.25
SHIFT_IN, SCALE_IN, GATE = 0, 1, 2


class Memory:
    pass


def setup(nc, m, a, ctx):
    with ExitStack() as c:
        sb = lambda n, s, d=F32: c.enter_context(nc.sbuf_tensor(n, s, d))
        sem = lambda n: c.enter_context(nc.semaphore(n))
        x_rows = sb("x_rows", [P, B * TB, P])
        wq_rows = sb("wq_rows", [P, PAIRS, P])
        wkv_rows = sb("wkv_rows", [P, 4, P])
        wo_rows = sb("wo_rows", [P, PAIRS, P])
        small_rows = sb("small_rows", [EX, 3, P])
        wmod = sb("wmod", [P, 2, 6 * P])
        silu = sb("silu", [P, 2 * B])
        work = sb("silu_work", [P, 2 * B])
        absmod = sb("absmod", [P, 2, 6, B])
        turned = c.enter_context(nc.psum_tensor("turned", [P, 4, 512], F32))
        modp = c.enter_context(nc.psum_tensor("modp", [P, 2, 6, B], F32))
        loaded, x_loaded = sem("loaded"), sem("x_loaded")
        turn_done, turn_copied, mod_done, step, exps = (
            sem("turn_done"), sem("turn_copied"), sem("mod_done"), sem("setup_step"), sem("exp_done"))

        jobs = []
        jobs.append([(small_rows[:, i, :], EX) for i in range(3)])
        for g in range(2):
            jobs.append([(wq_rows[:, 4 * g + i, :], P) for i in range(4)])
        jobs.append([(wkv_rows[:, i, :], P) for i in range(4)])
        for g in range(2):
            jobs.append([(wo_rows[:, 4 * g + i, :], P) for i in range(4)])
        dests = [m.small_T[:, :, :].rearrange("p a b -> p (a b)"), m.wqT[:, 0:512], m.wqT[:, 512:1024], m.wkvT[:, :],
                 m.woT[:, 0:4, :].rearrange("p a b -> p (a b)"), m.woT[:, 4:8, :].rearrange("p a b -> p (a b)")]
        n_weights = len(jobs)
        for b in range(B):
            jobs.append([(x_rows[:, TB * b + i, :], P) for i in range(TB)])
            dests.append(m.xT[:, b, :])

        loads = [
            (m.ident[:, :], a["c_ident"]), (m.ident_b[:, :], a["c_ident_b"]),
            (small_rows[:, 0, :], a["L0_c"]), (small_rows[:, 1, :], a["L1_c"]),
            (small_rows[:, 2, :], a["L0_ffn_router_w"]),
            (wmod[:, 0, :], a["L0_wmod"]), (wmod[:, 1, :], a["L1_wmod"]),
            (wq_rows[:, :, :], a["L0_attn_wq"].rearrange("(g p) d -> p g d", p=P)),
            (wkv_rows[:, 0:2, :], a["L0_attn_wk"].rearrange("(g p) d -> p g d", p=P)),
            (wkv_rows[:, 2:4, :], a["L0_attn_wv"].rearrange("(g p) d -> p g d", p=P)),
            (wo_rows[:, :, :], a["L0_attn_wo"].rearrange("p (g d) -> p g d", d=P)),
            (m.qk_w[0:HD0, 0:1], a["L0_attn_q_norm_w"].rearrange("(p o) -> p o", o=1)),
            (m.qk_w[HD0:P, 0:1], a["L0_attn_q_norm_w"].rearrange("(p o) -> p o", o=1)),
            (m.qk_w[0:HD0, 1:2], a["L0_attn_k_norm_w"].rearrange("(p o) -> p o", o=1)),
            (m.qk_w[HD0:P, 1:2], a["L0_attn_k_norm_w"].rearrange("(p o) -> p o", o=1)),
        ]
        with nc.Block() as block:
            @block.sync
            def _(sp):
                for dst, src in loads:
                    sp.dma_start(dst, src).then_inc(loaded, 16)
                x_src = a["L0_attn_x"].rearrange("b (t p) d -> p (b t) d", p=P)
                for b in range(B):
                    sp.dma_start(x_rows[:, TB * b:TB * b + TB, :], x_src[:, TB * b:TB * b + TB, :]).then_inc(x_loaded, 16)

            @block.tensor
            def _(pe):
                pe.wait_ge(loaded, 16 * len(loads))
                for n, job in enumerate(jobs):
                    if n == n_weights:
                        pe.wait_ge(x_loaded, 16 * B)
                    if n == 1:
                        pe.wait_ge(step, 2)
                        for layer in range(2):
                            for j in range(6):
                                mm = pe.matmul(modp[:, layer, j, :], wmod[:, layer, j * P:(j + 1) * P],
                                               silu[:, layer * B:(layer + 1) * B], start=True, stop=True)
                        mm.then_inc(mod_done, 1)
                    if n >= 4:
                        pe.wait_ge(turn_copied, n - 3)
                    at = 0
                    for rows, k in job:
                        mm = pe.transpose(turned[:, n % 4, at:at + k], rows, m.ident[0:k, 0:k])
                        at += k
                    mm.then_inc(turn_done, 1)

            @block.scalar
            def _(act):
                act.wait_ge(turn_copied, 1)
                act.activation(work[:, :], m.small_T[:, 0:2, :].rearrange("p a b -> p (a b)"), ACT.Exp,
                               scale=-1.0).then_inc(exps, 1)

            @block.vector
            def _(dve):
                def copy(n):
                    dve.wait_ge(turn_done, n + 1)
                    width = sum(k for _, k in jobs[n])
                    dve.tensor_copy(dests[n], turned[:, n % 4, 0:width]).then_inc(turn_copied, 1)

                copy(0)
                dve.wait_ge(exps, 1)
                dve.tensor_scalar(silu[:, :], work[:, :], 1.0, None, ALU.add).then_inc(step, 1)
                dve.wait_ge(step, 1)
                dve.reciprocal(work[:, :], silu[:, :]).then_inc(exps, 1)
                dve.wait_ge(exps, 2)
                dve.tensor_tensor(silu[:, :], m.small_T[:, 0:2, :].rearrange("p a b -> p (a b)"), work[:, :],
                                  ALU.mult).then_inc(step, 1)
                for n in range(1, len(jobs)):
                    copy(n)
                dve.wait_ge(mod_done, 1)
                dve.tensor_copy(m.mod[:, :, :, :], modp[:, :, :, :]).then_inc(step, 1)
                dve.wait_ge(step, 3)
                dve.scalar_tensor_tensor(absmod[:, :, :, :].rearrange("p a b c -> p (a b c)"),
                                         m.mod[:, :, :, :].rearrange("p a b c -> p (a b c)"), -1.0,
                                         m.mod[:, :, :, :].rearrange("p a b c -> p (a b c)"),
                                         ALU.mult, ALU.max).then_inc(step, 1)
                dve.wait_ge(step, 4)
                n = 4
                for layer in range(2):
                    for j in (GATE, 3 + GATE):
                        g = m.mod[:, layer, j, :]
                        ab = absmod[:, layer, j, :]
                        dve.tensor_scalar(ab, ab, GATE_MIN, None, ALU.max).then_inc(step, 1)
                        dve.tensor_scalar(g, g, 0.0, 2.0, ALU.is_ge, ALU.mult).then_inc(step, 1)
                        n += 2
                        dve.wait_ge(step, n)
                        dve.scalar_tensor_tensor(g, g, -1.0, ab, ALU.add, ALU.mult).then_inc(step, 1)
                        n += 1
                    for j in (SCALE_IN, 3 + SCALE_IN):
                        g = m.mod[:, layer, j, :]
                        dve.tensor_scalar(g, g, 1.0, None, ALU.add).then_inc(step, 1)
                        n += 1
                dve.tensor_tensor(m.qk_w[:, 2:3], m.qk_w[:, 0:1], m.qk_w[:, 1:2], ALU.mult).then_inc(step, 1)
                n += 1
                dve.wait_ge(step, n)
                dve.tensor_scalar(m.qk_w[:, 2:3], m.qk_w[:, 2:3], float(HD0) ** -0.5, None, ALU.mult)
                dve.memset(m.hT[:, :, 0:WINDOW], 0.0)
                dve.memset(m.eps[:, 0:1], LN_EPS)
                dve.memset(m.eps[:, 1:2], EPS0)
                dve.memset(m.mean_w[:, :], 1.0 / P)


def layer_norm(nc, m, layer, part, name):
    with ExitStack() as c:
        sb = lambda n, s, d=F32: c.enter_context(nc.sbuf_tensor(name + n, s, d))
        sem = lambda n: c.enter_context(nc.semaphore(name + n))
        centered = sb("centered", [P, 2, S])
        squared = sb("squared", [P, 2, S])
        std = sb("std", [P, 2, S])
        rstd = sb("rstd", [P, 2, S])
        normed = sb("normed", [P, 2, S])
        mean_p = c.enter_context(nc.psum_tensor(name + "mean_p", [P, 2, S], F32))
        var_p = c.enter_context(nc.psum_tensor(name + "var_p", [P, 2, S], F32))
        s_mean, s_cent, s_sq, s_var, s_std, s_rstd, s_norm, s_h = map(
            sem, ("mean", "cent", "sq", "var", "std", "rstd", "norm", "h"))
        done = lambda b: b + 3
        free = lambda b: b + 1
        shift, scale = m.mod[:, layer, 3 * part + SHIFT_IN, :], m.mod[:, layer, 3 * part + SCALE_IN, :]
        with nc.Block() as block:
            @block.tensor
            def _(pe):
                pe.sem_inc(s_mean, 2)
                pe.sem_inc(s_var, 2)
                with pe.Fori(0, B // 2) as i:
                    for j in range(2):
                        b = 2 * i + j
                        pe.wait_ge(s_cent, free(b))
                        pe.matmul(mean_p[:, j, :], m.mean_w[:, :], m.xT[:, b, :], start=True, stop=True).then_inc(s_mean, 1)
                    for j in range(2):
                        b = 2 * i + j
                        pe.wait_ge(s_std, free(b))
                        pe.wait_ge(s_sq, done(b))
                        pe.matmul(var_p[:, j, :], m.mean_w[:, :], squared[:, j, :], start=True, stop=True).then_inc(s_var, 1)

            @block.scalar
            def _(act):
                act.sem_inc(s_sq, 2)
                act.sem_inc(s_std, 2)
                act.sem_inc(s_h, 2)
                with act.Fori(0, B // 2) as i:
                    for j in range(2):
                        b = 2 * i + j
                        act.wait_ge(s_cent, done(b))
                        act.wait_ge(s_var, free(b))
                        act.activation(squared[:, j, :], centered[:, j, :], ACT.Square).then_inc(s_sq, 1)
                    for j in range(2):
                        b = 2 * i + j
                        act.wait_ge(s_var, done(b))
                        act.wait_ge(s_rstd, free(b))
                        act.activation(std[:, j, :], var_p[:, j, :], ACT.Sqrt, bias=m.eps[:, 0:1]).then_inc(s_std, 1)
                    for j in range(2):
                        b = 2 * i + j
                        act.wait_ge(s_norm, done(b))
                        act.activation(m.hT[:, b, WINDOW:], normed[:, j, :], ACT.Identity, bias=shift[:, bass.ds(b, 1)],
                                       scale=scale[:, bass.ds(b, 1)]).then_inc(s_h, 1)

            @block.vector
            def _(dve):
                dve.sem_inc(s_cent, 2)
                dve.sem_inc(s_rstd, 2)
                dve.sem_inc(s_norm, 2)
                with dve.Fori(0, B // 2) as i:
                    for j in range(2):
                        b = 2 * i + j
                        dve.wait_ge(s_mean, done(b))
                        dve.wait_ge(s_sq, free(b))
                        dve.wait_ge(s_norm, free(b))
                        dve.tensor_tensor(centered[:, j, :], m.xT[:, b, :], mean_p[:, j, :], ALU.subtract).then_inc(s_cent, 1)
                    for j in range(2):
                        b = 2 * i + j
                        dve.wait_ge(s_std, done(b))
                        dve.wait_ge(s_norm, free(b))
                        dve.reciprocal(rstd[:, j, :], std[:, j, :]).then_inc(s_rstd, 1)
                    for j in range(2):
                        b = 2 * i + j
                        dve.wait_ge(s_rstd, done(b))
                        dve.wait_ge(s_cent, done(b))
                        dve.wait_ge(s_h, free(b))
                        dve.tensor_tensor(normed[:, j, :], centered[:, j, :], rstd[:, j, :], ALU.mult).then_inc(s_norm, 1)


def window_attention(nc, m, a):
    with ExitStack() as c:
        sb = lambda n, s, d=F32: c.enter_context(nc.sbuf_tensor("wa_" + n, s, d))
        pb = lambda n, s: c.enter_context(nc.psum_tensor("wa_" + n, s, F32))
        sem = lambda n: c.enter_context(nc.semaphore("wa_" + n))
        hs = sb("hs", [P, WINDOW + S + SLOT - WIN])
        q = sb("q", [P, PAIRS, S])
        qsq = sb("qsq", [P, PAIRS, S])
        k = sb("k", [P, 2, S])
        ksq = sb("ksq", [P, 2, S])
        kstd = sb("kstd", [P, 2, S])
        krstd = sb("krstd", [P, 2, S])
        kT = sb("kT", [P, 2, WINDOW + S])
        vw = sb("vw", [P, S // SUB, P])
        qstd = sb("qstd", [P, TB, 2, PAIRS])
        qrstd = sb("qrstd", [P, TB, 2, PAIRS])
        half = sb("half", [P, P + 2])
        bias = sb("bias", [P, 2, PAIRS, 2, WIN])
        sc = sb("sc", [P, 2, PAIRS, 2, WIN])
        pr = sb("pr", [P, 2, PAIRS, 2, SLOT])
        mx = sb("mx", [P, 2, PAIRS, 2])
        sm = sb("sm", [P, 2, PAIRS, 2])
        rs = sb("rs", [P, 2, PAIRS, 2])
        pT = sb("pT", [P, PAIRS, P])
        ao = sb("ao", [P, PAIRS, S])
        bank = pb("bank", [P, 2, S])
        sp = pb("sp", [P, 2, S])
        tp = pb("tp", [P, PAIRS, P])
        op = pb("op", [P, PAIRS, P])
        (s_const, s_zero, s_hs, s_use, s_free, s_vfree, s_kr, s_k, s_qr, s_S, s_mult, s_bias, s_max, s_sub, s_exp, s_sum,
         s_rs, s_p, s_t, s_pT, s_pv, s_ao, s_x, s_pass) = map(sem, (
             "const", "zero", "hs", "use", "free", "vfree", "kr", "k", "qr", "S", "mult", "bias", "max", "sub", "exp",
             "sum", "rs", "p", "t", "pT", "pv", "ao", "x", "pass"))
        Q0, K0, V0, M0, RQ, Y = 0, PAIRS, PAIRS + 2, PAIRS + 6, PAIRS + 8, PAIRS + 9
        USES = PAIRS + 10
        READ = USES - 1
        wv = m.wkvT[:, 2 * P:].rearrange("p (a par d) -> p par a d", par=2, d=HD0)

        with nc.Block() as block:
            @block.sync
            def _(sp_):
                sp_.dma_start(half[:, :], a["c_half"]).then_inc(s_const, 16)
                sp_.dma_start(bias[:, :, :, :, :], a["c_bias"]).then_inc(s_const, 16)

            @block.gpsimd
            def _(pool):
                pool.memset(hs[:, WINDOW + S:], 0.0).then_inc(s_zero, 1)
                pool.memset(kT[:, :, 0:WINDOW], 0.0).then_inc(s_zero, 1)
                pool.memset(pr[:, :, :, :, :], 0.0).then_inc(s_zero, 1)
                with pool.Fori(0, B) as b:
                    pool.wait_ge(s_vfree, b)
                    pool.tensor_copy(hs[:, 0:WINDOW + S], m.hT[:, b, :]).then_inc(s_hs, 1)

            @block.tensor
            def _(pe):
                pe.wait_ge(s_const, 32)
                pe.wait_ge(s_zero, 3)
                with pe.Fori(0, B) as b:
                    def to(n):
                        if n == 1:
                            pe.wait_ge(s_x, b)
                            pe.wait_ge(s_free, READ * b)
                        else:
                            pe.wait_ge(s_free, READ * b + max(n - 1, 0))
                        return bank[:, n % 2, :]

                    pe.wait_ge(s_hs, b + 1)
                    for g in range(PAIRS):
                        o = to(Q0 + g)
                        pe.matmul(o, m.wqT[:, g * P:(g + 1) * P], hs[:, WINDOW:WINDOW + S],
                                  start=True, stop=True).then_inc(s_use, 1)
                    for g in range(2):
                        o = to(K0 + g)
                        pe.matmul(o, m.wkvT[:, g * P:(g + 1) * P], hs[:, WINDOW:WINDOW + S],
                                  start=True, stop=True).then_inc(s_use, 1)
                    for g in range(4):
                        o = to(V0 + g)
                        for w in range(4):
                            at = (4 * g + w) * SUB
                            for par in range(2):
                                mm = pe.matmul(o[SLOT * par:SLOT * par + SLOT, w * P:(w + 1) * P], hs[:, at:at + SLOT],
                                               wv[:, par, :, :], start=True, stop=True)
                        mm.then_inc(s_use, 1)
                    for g in range(2):
                        o = to(M0 + g)
                        pe.matmul(o, half[:, 0:P], ksq[:, g, :], start=True, stop=True).then_inc(s_use, 1)
                    o = to(RQ)[:, 0:TB * HEADS].rearrange("p (t par g) -> p t par g", t=TB, par=2)
                    for t in range(TB):
                        for g in range(PAIRS):
                            mm = pe.matmul(o[:, t, :, g], qsq[:, g, t * P:(t + 1) * P], half[:, P:P + 2],
                                           start=True, stop=True)
                            if t == 0 and g == 0:
                                mm.then_inc(s_vfree, 1)
                    mm.then_inc(s_use, 1)

                    def scores(t):
                        if t == 0:
                            pe.wait_ge(s_k, b + 1)
                        pe.wait_ge(s_mult, TB * b + t)
                        pe.sem_inc(s_pass, 1)
                        for par in range(2):
                            for g in range(PAIRS):
                                for j in range(P // SUB):
                                    at = t * P + SUB * j
                                    mm = pe.matmul(sp[SUB * j:SUB * j + SUB, par, g * WIN:(g + 1) * WIN],
                                                   q[SLOT * par:SLOT * par + SLOT, g, at:at + SUB],
                                                   kT[SLOT * par:SLOT * par + SLOT, g % 2, at:at + WIN],
                                                   start=True, stop=True)
                        mm.then_inc(s_S, 1)

                    def values(t):
                        n = TB * b + t
                        pe.wait_ge(s_p, n + 1)
                        pe.wait_ge(s_pT, n)
                        for g in range(PAIRS):
                            mm = pe.transpose(tp[:, g, :], pr[:, t % 2, g, :, :].rearrange("p a k -> p (a k)"), m.ident[:, :])
                        mm.then_inc(s_t, 1)
                        pe.wait_ge(s_pT, n + 1)
                        pe.wait_ge(s_ao, n)
                        pe.sem_inc(s_pass, 1)
                        for g in range(PAIRS):
                            for j in range(P // SUB):
                                for par in range(2):
                                    rows = slice(SLOT * par, SLOT * par + SLOT)
                                    mm = pe.matmul(op[rows, g, SUB * j:SUB * j + SUB],
                                                   vw[rows, 4 * t + j, (g % 2) * HD0:(g % 2 + 1) * HD0],
                                                   pT[rows, g, SUB * j:SUB * j + SUB], start=True, stop=True)
                        mm.then_inc(s_pv, 1)

                    scores(0)
                    for t in range(TB):
                        if t + 1 < TB:
                            scores(t + 1)
                        values(t)
                    o = to(Y)
                    pe.wait_ge(s_ao, TB * (b + 1))
                    for g in range(PAIRS):
                        mm = pe.matmul(o, m.woT[:, g, :], ao[:, g, :], start=(g == 0), stop=(g == PAIRS - 1))
                    mm.then_inc(s_use, 1)

            @block.scalar
            def _(act):
                with act.Fori(0, B) as b:
                    def use(n):
                        act.wait_ge(s_use, USES * b + n + 1)
                        return bank[:, n % 2, :]

                    for g in range(PAIRS):
                        o = use(Q0 + g)
                        act.activation(q[:, g, :], o, ACT.Copy)
                        act.activation(qsq[:, g, :], o, ACT.Square).then_inc(s_free, 1)
                    for g in range(2):
                        o = use(K0 + g)
                        act.activation(k[:, g, :], o, ACT.Copy)
                        act.activation(ksq[:, g, :], o, ACT.Square).then_inc(s_free, 1)
                    for g in range(4):
                        o = use(V0 + g)
                        act.activation(vw[:, 4 * g:4 * g + 4, :].rearrange("p a b -> p (a b)"), o, ACT.Copy).then_inc(s_free, 1)
                    for g in range(2):
                        o = use(M0 + g)
                        act.activation(kstd[:, g, :], o, ACT.Sqrt, bias=m.eps[:, 1:2]).then_inc(s_free, 1)
                    o = use(RQ)
                    act.activation(qstd[:, :, :, :].rearrange("p t a g -> p (t a g)"), o[:, 0:TB * HEADS], ACT.Sqrt,
                                   bias=m.eps[:, 1:2]).then_inc(s_free, 1)

                    def exp(t):
                        act.wait_ge(s_sub, TB * b + t + 1)
                        act.activation(pr[:, t % 2, :, :, 0:WIN].rearrange("p g a k -> p (g a) k"),
                                       sc[:, t % 2, :, :, :].rearrange("p g a k -> p (g a) k"), ACT.Exp).then_inc(s_exp, 1)

                    exp(0)
                    for t in range(TB):
                        if t + 1 < TB:
                            if t >= 1:
                                act.wait_ge(s_t, TB * b + t)
                            exp(t + 1)
                        act.wait_ge(s_t, TB * b + t + 1)
                        act.activation(pT[:, :, :], tp[:, :, :], ACT.Copy).then_inc(s_pT, 1)
                        act.wait_ge(s_pv, TB * b + t + 1)
                        act.activation(ao[:, :, t * P:(t + 1) * P], op[:, :, :], ACT.Copy).then_inc(s_ao, 1)

            @block.vector
            def _(dve):
                dve.wait_ge(s_const, 32)
                with dve.Fori(0, B) as b:
                    dve.wait_ge(s_free, READ * b + M0 + 2)
                    dve.reciprocal(krstd[:, :, :], kstd[:, :, :]).then_inc(s_kr, 1)
                    dve.wait_ge(s_kr, b + 1)
                    for g in range(2):
                        ins = dve.scalar_tensor_tensor(kT[:, g, WINDOW:], k[:, g, :], m.qk_w[:, 2:3], krstd[:, g, :],
                                                       ALU.mult, ALU.mult)
                    ins.then_inc(s_k, 1)
                    dve.wait_ge(s_free, READ * b + RQ + 1)
                    dve.reciprocal(qrstd[:, :, :, :], qstd[:, :, :, :]).then_inc(s_qr, 1)
                    dve.wait_ge(s_qr, b + 1)

                    def logits(t):
                        n, i = TB * b + t, t % 2
                        dve.wait_ge(s_S, n + 1)
                        s_ = sc[:, i, :, :, :].rearrange("p g a k -> p a g k")
                        for par in range(2):
                            ins = dve.tensor_tensor(s_[:, par], sp[:, par, 0:PAIRS * WIN].rearrange("p (g k) -> p g k", g=PAIRS),
                                                    qrstd[:, t, par, :].unsqueeze(2).to_broadcast([P, PAIRS, WIN]), ALU.mult)
                        ins.then_inc(s_mult, 1)
                        dve.wait_ge(s_mult, n + 1)
                        flat = sc[:, i, :, :, :].rearrange("p g a k -> p (g a k)")
                        dve.tensor_tensor(flat, flat, bias[:, 0 if t == 0 else 1, :, :, :].rearrange("p g a k -> p (g a k)"),
                                          ALU.add).then_inc(s_bias, 1)
                        dve.wait_ge(s_bias, n + 1)
                        rows = sc[:, i, :, :, :].rearrange("p g a k -> p (g a) k")
                        m_ = mx[:, i, :, :].rearrange("p g a -> p (g a)")
                        dve.tensor_reduce(m_, rows, AX.X, ALU.max).then_inc(s_max, 1)
                        dve.wait_ge(s_max, n + 1)
                        dve.tensor_tensor(rows, rows, m_.unsqueeze(2).to_broadcast([P, HEADS, WIN]),
                                          ALU.subtract).then_inc(s_sub, 1)

                    def normalise(t):
                        n, i = TB * b + t, t % 2
                        rows = pr[:, i, :, :, 0:WIN].rearrange("p g a k -> p (g a) k")
                        s_ = sm[:, i, :, :].rearrange("p g a -> p (g a)")
                        r_ = rs[:, i, :, :].rearrange("p g a -> p (g a)")
                        dve.wait_ge(s_exp, n + 1)
                        dve.tensor_reduce(s_, rows, AX.X, ALU.add).then_inc(s_sum, 1)
                        dve.wait_ge(s_sum, n + 1)
                        dve.reciprocal(r_, s_).then_inc(s_rs, 1)
                        dve.wait_ge(s_rs, n + 1)
                        dve.tensor_tensor(rows, rows, r_.unsqueeze(2).to_broadcast([P, HEADS, WIN]), ALU.mult).then_inc(s_p, 1)

                    logits(0)
                    for t in range(TB):
                        if t + 1 < TB:
                            logits(t + 1)
                        normalise(t)
                    dve.wait_ge(s_use, USES * b + Y + 1)
                    dve.scalar_tensor_tensor(m.xT[:, b, :], bank[:, Y % 2, :], m.mod[:, 0, GATE, bass.ds(b, 1)], m.xT[:, b, :],
                                             ALU.mult, ALU.add).then_inc(s_x, 1)


SPLIT_Q = (0, 0, 0, 1, 1, 2)
SPLIT_K = (0, 1, 2, 0, 1, 0)
GROUPS = len(SPLIT_Q)
ROWS = GROUPS * HD1
QUAD = 4
QUADS = HEADS // QUAD
COL = 32
VW = HD1 + 1
LOW = -3.0e38


def head_attention(nc, m, a, sparse):
    tag = "sp_" if sparse else "de_"
    with ExitStack() as c:
        sb = lambda n, s, d=F32: c.enter_context(nc.sbuf_tensor(tag + n, s, d))
        pb = lambda n, s: c.enter_context(nc.psum_tensor(tag + n, s, F32))
        sem = lambda n: c.enter_context(nc.semaphore(tag + n))
        KINDS = 2 if sparse else 1
        STAT = 3 * KINDS
        K_SIDES = 2 if sparse else 1
        scratch = nc.dram_tensor(tag + "scratch", (B, 2, HEADS, ROWS, S), BF16, kind="Internal").ap()

        hs = sb("hs", [P, S])
        w_q, w_k, w_v, w_o = (sb(n, [P, P]) for n in ("w_q", "w_k", "w_v", "w_o"))
        cols = sb("cols", [P, 3])
        bq = sb("bq", [P, 1])
        bv = sb("bv", [P, P])
        ones = sb("ones", [P, P])
        qk = sb("qk", [P, 2, S])
        rest = sb("rest", [P, 2, S])
        part = sb("part", [P, 3, 2, S], BF16)
        v = sb("v", [P, TB, HEADS, COL])
        stack_q = sb("stack_q", [P, 2, 2, S], BF16)
        stack_k = sb("stack_k", [P, 2, K_SIDES, 2, S], BF16)
        stat = sb("stat", [P, 2, TB, QUAD, KINDS])
        stat_rest = sb("stat_rest", [P, TB, QUAD, KINDS])
        stat_part = sb("stat_part", [P, TB, QUAD, KINDS, 3], BF16)
        statT = sb("statT", [QUAD * STAT, 2, S], BF16)
        e = sb("e", [P, 2, 2, S])
        u_sb = sb("u_sb", [P, KINDS, S])
        zr = sb("zr", [P, TB, QUAD, 1])
        tok = sb("tok", [P, TB, P])
        if sparse:
            work = sb("work", [P, 2, S])
            m8 = sb("m8", [P, 2, 7, 8])
            sumv = sb("sumv", [P, HEADS, COL])
            vrest = sb("vrest", [P, 2, TB, P])
            vpart = sb("vpart", [P, TB, HEADS, COL], BF16)
            vp2 = sb("vp2", [P, TB, P], BF16)
            mask = sb("mask", [P, 2, QUAD, S], BF16)
            w = sb("w", [P, 2, QUAD, S])
            floor = sb("floor", [P, 2, TB, QUAD])
            tot = sb("tot", [P, TB, QUAD, VW])
            tot2 = sb("tot2", [P, TB, QUAD, VW])
            aT = sb("aT", [P, S])
            y = sb("y", [P, S])
        bank = pb("bank", [P, 2, S])
        h_p = pb("h_p", [P, 2, S])
        g_p = pb("g_p", [P, 2, S]) if sparse else None
        u_p = [pb(f"u_p{i}", [P, S]) for i in range(KINDS)]

        (s_load, s_one, s_hs, s_use, s_f0, s_f1, s_qk, s_split, s_vone, s_wr, s_ld, s_st, s_sp, s_hp, s_exp, s_pv, s_u,
         s_kd, s_fin, s_sg, s_pass) = map(sem, ("load", "one", "hs", "use", "free0", "free1", "qk", "split", "vone", "wr", "ld",
                                          "st", "sp", "hp", "exp", "pv", "u", "kd", "fin", "sg", "pass"))
        s_v, s_top, s_fl, s_gp, s_mk, s_w, s_tok, s_rel = (
            map(sem, ("v", "top", "fl", "gp", "mk", "w", "tok", "rel")) if sparse else [None] * 8)
        s_bank = (s_f0, s_f1)

        uses = ["q", "k", "v", "vs"] if sparse else ["q", "k", "v", "v2"]
        plan = [("A",)]
        for s in range(QUAD):
            plan.append(("Q", 0, s))
        plan.append(("T", 0))
        for r in range(QUADS):
            for s in range(QUAD):
                if r + 1 < QUADS:
                    plan.append(("Q", r + 1, s))
                plan.append(("K", r, s))
            if r + 1 < QUADS:
                plan.append(("T", r + 1))
            plan.append(("F", r))
        if sparse:
            plan.append(("Y",))
        for it in plan:
            if it[0] == "Q":
                uses += [("S", it[1], it[2], t) for t in range(TB)]
            if it[0] == "T":
                uses.append(("T", it[1]))
            if it[0] == "F":
                uses += [("F", it[1], k) for k in range(KINDS)]
            if it[0] == "Y":
                uses += ["aT", "y"]
        index = {u: n for n, u in enumerate(uses)}
        USES = len(uses)
        assert USES % 2 == 0
        CHUNK2 = QUADS * TB * 2
        CHUNKS = QUADS * TB
        TOPS = HEADS * TB // 2 * 13

        def used(eng, b, u):
            n = index[u]
            eng.wait_ge(s_use, USES * b + n + 1)
            return bank[:, n % 2, :]

        def freed(u):
            return s_bank[index[u] % 2]

        def released(eng, b, u):
            n = index[u]
            eng.wait_ge(s_bank[n % 2], (USES // 2) * b + n // 2 + 1)

        wname = "L1_attn_" if sparse else "L1_ffn_"
        if sparse:
            srcs = [(w_q, a["L1_attn_Wq"]), (w_k, a["L1_attn_Wk"]), (w_v, a["L1_attn_Wv"]), (w_o, a["L1_attn_Wo"])]
            bias = [a["L1_attn_bq"], a["L1_attn_bk"], a["L1_attn_bo"], a["L1_attn_bv"]]
        else:
            wqkv, bqkv = a["L1_ffn_W_qkv"], a["L1_ffn_b_qkv"]
            srcs = [(w_q, wqkv[:, 0:P]), (w_k, wqkv[:, P:2 * P]), (w_v, wqkv[:, 2 * P:])]
            bias = [bqkv[0:P], bqkv[P:2 * P], None, bqkv[2 * P:]]
        loads = [(d[:, :], s) for d, s in srcs]
        loads += [(cols[:, i:i + 1], bias[i].rearrange("(p o) -> p o", o=1)) for i in range(3) if bias[i] is not None]
        loads.append((bv[:, :], bias[3].rearrange("(o d) -> o d", o=1).to_broadcast([P, P])))
        for slot in range(2):
            for side in range(K_SIDES):
                for par in range(2):
                    loads.append((stack_k[64 * par + ROWS:64 * par + ROWS + STAT, slot, side, :, :],
                                  a["c_stat2" if sparse else "c_stat1"][:, side, :, :]))

        with nc.Block() as block:
            @block.sync
            def _(sp):
                for dst, src in loads:
                    sp.dma_start(dst, src).then_inc(s_load, 16)
                with sp.Fori(0, B) as b:
                    sp.wait_ge(s_split, 2 * b + 2)
                    sp.sem_inc(s_pass, 1)
                    for side, groups in ((0, SPLIT_Q), (1, SPLIT_K)):
                        for j, k in enumerate(groups):
                            sp.dma_start(scratch[b, side, :, HD1 * j:HD1 * j + HD1, :], part[:, k, side, :]).then_inc(s_wr, 16)
                    sp.wait_ge(s_wr, 2 * GROUPS * 16 * (b + 1))
                    sp.sem_inc(s_pass, 1)

                    def load(r):
                        sl = r % 2
                        for par in range(2):
                            rows = slice(64 * par, 64 * par + ROWS)
                            heads = slice(QUAD * r + par, QUAD * r + QUAD, 2)
                            sp.dma_start(stack_q[rows, sl, :, :],
                                         scratch[b, 0, heads, :, :].rearrange("h r s -> r h s")).then_inc(s_ld, 16)
                            for side in range(K_SIDES):
                                sp.dma_start(stack_k[rows, sl, side, :, :],
                                             scratch[b, 1, heads, :, :].rearrange("h r s -> r h s")).then_inc(s_ld, 16)

                    for r in range(QUADS):
                        if r == 0:
                            sp.wait_ge(s_kd, QUADS * b)
                            sp.sem_inc(s_pass, 1)
                            load(0)
                            load(1)
                        released(sp, b, ("T", r))
                        for i in range(QUAD):
                            par, p = i % 2, i // 2
                            sp.dma_start(stack_q[64 * par + ROWS:64 * par + ROWS + STAT, r % 2, p, :],
                                         statT[STAT * i:STAT * i + STAT, r % 2, :]).then_inc(s_st, 16)
                        if r + 2 < QUADS:
                            sp.wait_ge(s_kd, QUADS * b + r + 1)
                            sp.sem_inc(s_pass, 1)
                            load(r + 2)
            LD = 2 * (1 + K_SIDES) * 16

            @block.gpsimd
            def _(pool):
                pool.memset(v[:, :, :, :], 0.0).then_inc(s_one, 1)
                pool.memset(ones[:, :], 1.0).then_inc(s_one, 1)
                if sparse:
                    pool.memset(vpart[:, :, :, :], 0.0).then_inc(s_one, 1)
                    pool.sem_inc(s_w, 2)
                pool.wait_ge(s_one, 1)
                pool.memset(v[:, :, :, HD1:VW], 1.0).then_inc(s_vone, 1)
                if sparse:
                    pool.wait_ge(s_one, 3)
                    pool.memset(vpart[:, :, :, HD1:VW], 1.0).then_inc(s_vone, 1)
                with pool.Fori(0, B) as b:
                    for it in plan:
                        if it[0] == "A":
                            pool.wait_ge(s_kd, QUADS * b)
                            pool.tensor_copy(hs[:, :], m.hT[:, b, WINDOW:]).then_inc(s_hs, 1)
                        if it[0] == "K" and sparse:
                            _, r, ch = it
                            for p in range(2):
                                n = CHUNK2 * b + (r * TB + ch) * 2 + p
                                pool.wait_ge(s_exp, n + 1)
                                pool.wait_ge(s_mk, n + 1)
                                pool.tensor_tensor(w[:, ch % 2, 2 * p:2 * p + 2, :], mask[:, ch % 2, 2 * p:2 * p + 2, :],
                                                   e[:, p, :, :], ALU.mult).then_inc(s_w, 1)

            @block.tensor
            def _(pe):
                pe.wait_ge(s_load, 16 * len(loads))
                pe.wait_ge(s_one, 2)
                pe.wait_ge(s_vone, KINDS)
                pe.sem_inc(s_pv, 2)
                with pe.Fori(0, B) as b:
                    def to(u):
                        n = index[u]
                        pe.wait_ge(s_bank[n % 2], (USES // 2) * b + n // 2)
                        return bank[:, n % 2, :]

                    for it in plan:
                        if it[0] == "A":
                            pe.wait_ge(s_hs, b + 1)
                            o = to("q")
                            pe.matmul(o, w_q[:, :], hs[:, :], start=True, stop=True).then_inc(s_use, 1)
                            o = to("k")
                            pe.matmul(o, w_k[:, :], hs[:, :], start=True, stop=True).then_inc(s_use, 1)
                            o = to("v")
                            for t in range(TB):
                                if t == TB // 2 and not sparse:
                                    mm.then_inc(s_use, 1)
                                    o = to("v2")
                                mm = pe.matmul(o[:, t * P:(t + 1) * P], hs[:, t * P:(t + 1) * P], w_v[:, :],
                                               start=True, stop=True)
                            mm.then_inc(s_use, 1)
                            if sparse:
                                o = to("vs")
                                released(pe, b, "v")
                                for t in range(TB):
                                    mm = pe.matmul(o, ones[:, :], v[:, t, :, :].rearrange("p h d -> p (h d)"),
                                                   start=(t == 0), stop=(t == TB - 1))
                                mm.then_inc(s_use, 1)
                        if it[0] == "Q":
                            _, r, i = it
                            par, p, sl = i % 2, i // 2, r % 2
                            rows = slice(64 * par, 64 * par + ROWS)
                            if i == 0:
                                pe.wait_ge(s_ld, LD * (QUADS * b + (r + 1 if r else 2)))
                            for t in range(TB):
                                o = to(("S", r, i, t))
                                pe.matmul(o, stack_q[rows, sl, p, t * P:(t + 1) * P], stack_k[rows, sl, 0, p, :],
                                          start=True, stop=True).then_inc(s_use, 1)
                        if it[0] == "T":
                            r = it[1]
                            o = to(("T", r)).bitcast(BF16)
                            pe.wait_ge(s_sp, QUADS * b + r + 1)
                            for t in range(TB):
                                mm = pe.transpose(o[0:QUAD * STAT, t * P:(t + 1) * P],
                                                  stat_part[:, t, :, :, :].rearrange("p i k j -> p (i k j)"),
                                                  m.ident_b[:, :])
                            mm.then_inc(s_use, 1)
                        if it[0] == "K":
                            _, r, ch = it
                            if ch == 0:
                                pe.wait_ge(s_st, 16 * QUAD * (QUADS * b + r + 1))
                            for p in range(2):
                                n = CHUNK2 * b + (r * TB + ch) * 2 + p
                                for side, dst, freeby, s_done in ((0, h_p, s_exp, s_hp), (1, g_p, s_mk, s_gp))[:K_SIDES]:
                                    pe.wait_ge(freeby, n)
                                    for par in range(2):
                                        rows = slice(64 * par, 64 * par + ROWS + STAT)
                                        mm = pe.matmul(dst[:, par, :], stack_k[rows, r % 2, side, p, ch * P:(ch + 1) * P],
                                                       stack_q[rows, r % 2, p, :], start=True, stop=True)
                                    mm.then_inc(s_done, 1)

                            def values(ch):
                                kc = CHUNKS * b + r * TB + ch
                                if ch == 0:
                                    pe.wait_ge(s_u, QUADS * b + r)
                                if sparse:
                                    pe.wait_ge(s_w, CHUNK2 * b + (r * TB + ch) * 2 + 2 + 2)
                                else:
                                    pe.wait_ge(s_exp, CHUNK2 * b + (r * TB + ch) * 2 + 2)
                                for i in range(QUAD):
                                    rhs = w[:, ch % 2, i, :] if sparse else e[:, i // 2, i % 2, :]
                                    mm = pe.matmul(u_p[0][COL * i:COL * i + COL, :], v[:, ch, QUAD * r + i, :], rhs,
                                                   start=(ch == 0), stop=(ch == TB - 1))
                                if sparse:
                                    for i in range(QUAD):
                                        mm = pe.matmul(u_p[1][COL * i:COL * i + COL, :], vpart[:, ch, QUAD * r + i, :],
                                                       mask[:, ch % 2, i, :], start=(ch == 0), stop=(ch == TB - 1))
                                mm.then_inc(s_pv, 1)

                            if sparse:
                                if ch >= 1:
                                    values(ch - 1)
                                if ch == TB - 1:
                                    values(ch)
                            else:
                                values(ch)
                        if it[0] == "F":
                            r = it[1]
                            for k in range(KINDS):
                                o = to(("F", r, k))
                                pe.wait_ge(s_u, QUADS * b + r + 1)
                                for t in range(TB):
                                    mm = pe.transpose(o[:, t * P:(t + 1) * P], u_sb[:, k, t * P:(t + 1) * P], m.ident[:, :])
                                    if k == 0 and t == 0:
                                        mm.then_inc(s_kd, 1)
                                mm.then_inc(s_use, 1)
                        if it[0] == "Y":
                            o = to("aT")
                            pe.wait_ge(s_tok, QUADS * (b + 1))
                            for t in range(TB):
                                mm = pe.transpose(o[:, t * P:(t + 1) * P], tok[:, t, :], m.ident[:, :])
                            mm.then_inc(s_use, 1)
                            o = to("y")
                            released(pe, b, "aT")
                            pe.matmul(o, w_o[:, :], aT[:, :], start=True, stop=True).then_inc(s_use, 1)

            @block.scalar
            def _(act):
                act.wait_ge(s_load, 16 * len(loads))
                act.activation(bq[:, :], cols[:, 0:1], ACT.Copy, scale=float(HD1) ** -0.5).then_inc(s_qk, 1)
                act.wait_ge(s_qk, 1)
                with act.Fori(0, B) as b:
                    for it in plan:
                        if it[0] == "A":
                            act.wait_ge(s_split, 2 * b)
                            o = used(act, b, "q")
                            act.activation(qk[:, 0, :], o, ACT.Identity, bias=bq[:, 0:1],
                                           scale=float(HD1) ** -0.5).then_inc(freed("q"), 1)
                            o = used(act, b, "k")
                            act.activation(qk[:, 1, :], o, ACT.Identity, bias=cols[:, 1:2]).then_inc(freed("k"), 1)
                            act.wait_ge(freed("k"), (USES // 2) * b + index["k"] // 2 + 1)
                            act.wait_ge(freed("q"), (USES // 2) * b + index["q"] // 2 + 1)
                            act.wait_ge(s_wr, 2 * GROUPS * 16 * b)
                            act.activation(part[:, 0, :, :], qk[:, :, :], ACT.Copy).then_inc(s_qk, 1)
                            act.wait_ge(s_split, 2 * b + 1)
                            act.activation(part[:, 1, :, :], rest[:, :, :], ACT.Copy).then_inc(s_qk, 1)
                        if it[0] == "T":
                            r = it[1]
                            n = QUADS * b + r
                            if sparse:
                                act.wait_ge(s_sp, n + 1)
                                act.activation(floor[:, r % 2, :, :], stat[:, r % 2, :, :, 1], ACT.Exp).then_inc(s_fl, 1)
                            o = used(act, b, ("T", r)).bitcast(BF16)
                            act.activation(statT[:, r % 2, :], o[0:QUAD * STAT, 0:S], ACT.Copy).then_inc(freed(("T", r)), 1)
                        if it[0] == "K":
                            _, r, ch = it
                            for p in range(2):
                                n = CHUNK2 * b + (r * TB + ch) * 2 + p
                                act.wait_ge(s_hp, n + 1)
                                if sparse:
                                    act.wait_ge(s_w, n + 1)
                                else:
                                    act.wait_ge(s_pv, CHUNKS * b + r * TB + ch + 2)
                                act.activation(e[:, p, :, :], h_p[:, :, :], ACT.Exp).then_inc(s_exp, 1)
                        if it[0] == "F":
                            r = it[1]
                            act.wait_ge(s_pv, CHUNKS * b + r * TB + TB + 2)
                            for k in range(KINDS):
                                ins = act.activation(u_sb[:, k, :], u_p[k][:, :], ACT.Copy)
                            ins.then_inc(s_u, 1)
                        if it[0] == "Y":
                            o = used(act, b, "aT")
                            act.activation(aT[:, :], o, ACT.Copy).then_inc(freed("aT"), 1)

            @block.vector
            def _(dve):
                dve.wait_ge(s_load, 16 * len(loads))
                dve.wait_ge(s_one, 2 + sparse)
                dve.wait_ge(s_vone, KINDS)

                def settled():
                    dve.sem_inc(s_rel, 1)

                with dve.Fori(0, B) as b:
                    count = {s_top: 0, s_sg: 0, s_fin: 0}
                    per = {s_top: HEADS * TB // 2 * 28 if sparse else HEADS * TB, s_sg: 3 * QUADS,
                           s_fin: (5 if sparse else 1) * QUADS}

                    def did(ins, s_):
                        count[s_] += 1
                        ins.then_inc(s_, 1)

                    def wait_own(s_, back=0):
                        dve.wait_ge(s_, per[s_] * b + count[s_] - back)

                    for it in plan:
                        if it[0] == "A":
                            dve.wait_ge(s_qk, 2 * b + 2)
                            dve.tensor_tensor(rest[:, :, :], qk[:, :, :], part[:, 0, :, :], ALU.subtract).then_inc(s_split, 1)
                            dve.wait_ge(s_qk, 2 * b + 3)
                            dve.wait_ge(s_split, 2 * b + 1)
                            dve.tensor_tensor(part[:, 2, :, :], rest[:, :, :], part[:, 1, :, :], ALU.subtract).then_inc(s_split, 1)
                            vh = v[:, :, :, 0:HD1]
                            bvb = bv[:, :].unsqueeze(1).to_broadcast([P, TB, P])
                            if not sparse:
                                for k, u in enumerate(("v", "v2")):
                                    half = slice(k * TB // 2, (k + 1) * TB // 2)
                                    o = used(dve, b, u)
                                    dve.tensor_tensor(vh[:, half], o[:, half.start * P:half.stop * P].rearrange("p (t h d) -> p t h d", t=TB // 2, d=HD1),
                                                      bvb[:, half].rearrange("p t (h d) -> p t h d", d=HD1), ALU.add).then_inc(freed(u), 1)
                            else:
                                o = used(dve, b, "v")
                                dve.tensor_tensor(vh, o.rearrange("p (t h d) -> p t h d", t=TB, d=HD1),
                                                  bvb.rearrange("p t (h d) -> p t h d", d=HD1), ALU.add).then_inc(freed("v"), 1)
                                released(dve, b, "v")
                                vp = [vpart[:, :, :, VW * k:VW * k + HD1] for k in range(3)]
                                vr = [vrest[:, k, :, :].rearrange("p t (h d) -> p t h d", d=HD1) for k in range(2)]
                                dve.tensor_copy(vp[0], vh).then_inc(s_v, 1)
                                dve.wait_ge(s_v, 4 * b + 1)
                                dve.tensor_tensor(vr[0], vh, vp[0], ALU.subtract).then_inc(s_v, 1)
                                dve.wait_ge(s_v, 4 * b + 2)
                                dve.tensor_copy(vp[1], vr[0]).then_inc(s_v, 1)
                                dve.wait_ge(s_v, 4 * b + 3)
                                dve.tensor_tensor(vp[2], vr[0], vp[1], ALU.subtract).then_inc(s_v, 1)
                                o = used(dve, b, "vs")
                                dve.tensor_copy(sumv[:, :, :].rearrange("p h d -> p (h d)"), o).then_inc(freed("vs"), 1)
                        if it[0] == "Q" and not sparse:
                            _, r, i = it
                            for t in range(TB):
                                o = used(dve, b, ("S", r, i, t))
                                dve.tensor_reduce(stat[:, r % 2, t, i, :], o, AX.X, ALU.max, negate=True).then_inc(freed(("S", r, i, t)), 1)
                        if it[0] == "Q" and sparse:
                            _, r, i = it
                            for t0 in range(0, TB, 2):
                                tiles = [used(dve, b, ("S", r, i, t0 + u)) for u in range(2)]
                                for k in range(7):
                                    if k == 0:
                                        wait_own(s_top)
                                    if k:
                                        if k == 1:
                                            for u in range(2):
                                                released(dve, b, ("S", r, i, t0 + u))
                                        else:
                                            wait_own(s_top)
                                    settled()
                                    for u in range(2):
                                        did(dve.max(m8[:, u, k, :], work[:, u, :] if k else tiles[u]), s_top)
                                    if k == 6:
                                        break
                                    wait_own(s_top)
                                    settled()
                                    for u in range(2):
                                        ins = dve.match_replace(work[:, u, :], m8[:, u, k, :], work[:, u, :] if k else tiles[u], LOW)
                                        if k:
                                            did(ins, s_top)
                                        else:
                                            ins.then_inc(freed(("S", r, i, t0 + u)), 1)
                                wait_own(s_top)
                                last = KEEP - 1 - 48
                                for u in range(2):
                                    st = stat[:, r % 2, t0 + u, i, :]
                                    did(dve.tensor_scalar(st[:, 0:1], m8[:, u, 6, last:last + 1], m8[:, u, 6, last + 1:last + 2],
                                                          -0.5, ALU.add, ALU.mult), s_top)
                                    did(dve.tensor_scalar(st[:, 1:2], m8[:, u, 0, 0:1], 0.0, -1.0, ALU.max, ALU.mult), s_top)
                        if it[0] == "T":
                            r = it[1]
                            if sparse:
                                wait_own(s_top)
                            else:
                                released(dve, b, ("S", r, QUAD - 1, TB - 1))
                                released(dve, b, ("S", r, QUAD - 1, TB - 2))
                            if r:
                                used(dve, b, ("T", r - 1))
                            st, sr = stat[:, r % 2, :, :, :], stat_rest[:, :, :, :]
                            pt = [stat_part[:, :, :, :, k] for k in range(3)]
                            did(dve.tensor_copy(pt[0], st), s_sg)
                            wait_own(s_sg)
                            did(dve.tensor_tensor(sr, st, pt[0], ALU.subtract), s_sg)
                            wait_own(s_sg)
                            did(dve.tensor_copy(pt[1], sr), s_sg)
                            wait_own(s_sg)
                            dve.tensor_tensor(pt[2], sr, pt[1], ALU.subtract).then_inc(s_sp, 1)
                        if it[0] == "K" and sparse:
                            _, r, ch = it
                            for p in range(2):
                                n = CHUNK2 * b + (r * TB + ch) * 2 + p
                                dve.wait_ge(s_gp, n + 1)
                                dve.wait_ge(s_pv, CHUNKS * b + r * TB + ch + 1)
                                dve.tensor_scalar(mask[:, ch % 2, 2 * p:2 * p + 2, :], g_p[:, :, :], 0.0, None,
                                                  ALU.is_ge).then_inc(s_mk, 1)
                        if it[0] == "F":
                            r = it[1]
                            uT = used(dve, b, ("F", r, 0)).rearrange("p (t i c) -> p t i c", t=TB, i=QUAD)
                            if not sparse:
                                if r:
                                    released(dve, b, ("F", r - 1, 0))
                                did(dve.reciprocal(zr[:, :, :, :], uT[:, :, :, HD1:VW]), s_fin)
                                wait_own(s_fin)
                                dst = m.attn[:, b, :, QUAD * r * HD1:QUAD * (r + 1) * HD1].rearrange("p t (i d) -> p t i d", d=HD1)
                                dve.tensor_tensor(dst, uT[:, :, :, 0:HD1], zr[:, :, :, :].to_broadcast([P, TB, QUAD, HD1]),
                                                  ALU.mult).then_inc(freed(("F", r, 0)), 1)
                                if r == QUADS - 1:
                                    released(dve, b, ("F", r, 0))
                            else:
                                mT = used(dve, b, ("F", r, 1)).rearrange("p (t i c) -> p t i c", t=TB, i=QUAD)
                                did(dve.tensor_copy(tot[:, :, :, :], mT[:, :, :, 0:VW]), s_fin)
                                wait_own(s_fin)
                                did(dve.tensor_tensor(tot2[:, :, :, :], mT[:, :, :, VW:2 * VW], tot[:, :, :, :], ALU.add), s_fin)
                                wait_own(s_fin)
                                dve.tensor_tensor(tot[:, :, :, :], mT[:, :, :, 2 * VW:3 * VW], tot2[:, :, :, :],
                                                  ALU.add).then_inc(freed(("F", r, 1)), 1)
                                released(dve, b, ("F", r, 1))
                                sv = sumv[:, QUAD * r:QUAD * (r + 1), 0:VW].unsqueeze(1).to_broadcast([P, TB, QUAD, VW])
                                did(dve.tensor_tensor(tot2[:, :, :, :], sv, tot[:, :, :, :], ALU.subtract), s_fin)
                                wait_own(s_fin)
                                dve.wait_ge(s_fl, QUADS * b + r + 1)
                                fl = floor[:, r % 2, :, :].unsqueeze(3).to_broadcast([P, TB, QUAD, VW])
                                did(dve.tensor_tensor(tot[:, :, :, :], tot2[:, :, :, :], fl, ALU.mult), s_fin)
                                wait_own(s_fin)
                                dve.tensor_tensor(tot2[:, :, :, :], uT[:, :, :, 0:VW], tot[:, :, :, :],
                                                  ALU.add).then_inc(freed(("F", r, 0)), 1)
                                released(dve, b, ("F", r, 0))
                                did(dve.reciprocal(zr[:, :, :, :], tot2[:, :, :, HD1:VW]), s_fin)
                                wait_own(s_fin)
                                dst = tok[:, :, QUAD * r * HD1:QUAD * (r + 1) * HD1].rearrange("p t (i d) -> p t i d", d=HD1)
                                dve.tensor_tensor(dst, tot2[:, :, :, 0:HD1], zr[:, :, :, :].to_broadcast([P, TB, QUAD, HD1]),
                                                  ALU.mult).then_inc(s_tok, 1)
                        if it[0] == "Y":
                            o = used(dve, b, "y")
                            dve.tensor_scalar(y[:, :], o, cols[:, 2:3], m.mod[:, 1, GATE, bass.ds(b, 1)], ALU.add,
                                              ALU.mult).then_inc(freed("y"), 1)
                            released(dve, b, "y")
                            dve.tensor_tensor(m.xT[:, b, :], m.xT[:, b, :], y[:, :], ALU.add)
                assert all(count[s_] == per[s_] for s_ in (s_sg, s_fin) + ((s_top,) if sparse else ()))


def experts(nc, m, a, gelu):
    tag = "ge_" if gelu else "li_"
    layer = 0 if gelu else 1
    with ExitStack() as c:
        sb = lambda n, s, d=F32: c.enter_context(nc.sbuf_tensor(tag + n, s, d))
        pb = lambda n, s: c.enter_context(nc.psum_tensor(tag + n, s, F32))
        sem = lambda n: c.enter_context(nc.semaphore(tag + n))
        hs = sb("hs", [P, 2, S])
        lg = sb("lg", [P, TB, EX])
        m8 = sb("m8", [P, TB, 8])
        sh = sb("sh", [P, TB, EX])
        ex = sb("ex", [P, TB, EX])
        mk = sb("mk", [P, TB, EX])
        exm = sb("exm", [P, TB, EX])
        tot = sb("tot", [P, TB])
        inv = sb("inv", [P, TB])
        share = sb("share", [P, TB, EX])
        acc = sb("acc", [P, TB, P])
        STAGE = EX if gelu else 2
        if gelu:
            w1 = sb("w1", [P, EX, FF])
            w2 = sb("w2", [P, EX, 2, P])
            act_ = sb("act", [P, 2, 2, S])
            gate_w = m.small_T[:, 2, :]
            up_p = pb("up_p", [P, 2, 2, S])
            loads = [(w1[:, :, :], a["L0_ffn_w1"].rearrange("e p f -> p e f")),
                     ] + [(w2[:, :, k, :], a["L0_ffn_w2"][:, k * P:(k + 1) * P, :].rearrange("e p f -> p e f")) for k in range(2)]
            NOUT = EX
        else:
            wexp = sb("wexp", [P, EX, P])
            gw = sb("gw", [P, EX])
            gb = sb("gb", [P, EX])
            bexp = sb("bexp", [EX, P])
            shareT = sb("shareT", [EX, S])
            gate_w = gw[:, :]
            loads = [(wexp[:, :, :], a["L1_ffn_W_experts"].rearrange("e p f -> p e f")),
                     (gw[:, :], a["L1_ffn_W_gate"]), (bexp[:, :], a["L1_ffn_b_experts"]),
                     (gb[:, :], a["L1_ffn_b_gate"].rearrange("(o d) -> o d", o=1).to_broadcast([P, EX]))]
            NOUT = 2 * TB
        out_p = pb("out_p", [P, 2, S])
        lg_p = pb("lg_p", [P, S])
        y_p = pb("y_p", [P, S])
        (s_load, s_hs, s_lg, s_out, s_g, s_ex, s_acc, s_tr, s_x, s_free, s_norm, s_pass) = map(
            sem, ("load", "hs", "lg", "out", "g", "ex", "acc", "tr", "x", "free", "norm", "pass"))
        if gelu:
            s_up, s_act = sem("up"), sem("act")
        else:
            s_sh, s_shT = sem("sh"), sem("shT")
        G = 9 if gelu else 10
        ACC = EX * TB

        with nc.Block() as block:
            @block.sync
            def _(sp):
                for dst, src in loads:
                    sp.dma_start(dst, src).then_inc(s_load, 16)

            @block.gpsimd
            def _(pool):
                with pool.Fori(0, B // 2) as i:
                    for j in range(2):
                        b = 2 * i + j
                        pool.wait_ge(s_free, b + 1)
                        pool.tensor_copy(hs[:, j, :], m.hT[:, b, WINDOW:]).then_inc(s_hs, 1)

            @block.tensor
            def _(pe):
                pe.sem_inc(s_free, 2)
                pe.wait_ge(s_load, 16 * len(loads))
                with pe.Fori(0, B // 2) as i:
                    for j in range(2):
                        b = 2 * i + j
                        pe.wait_ge(s_hs, b + 1)
                        pe.wait_ge(s_g, G * b)
                        for t in range(TB):
                            mm = pe.matmul(lg_p[:, t * EX:(t + 1) * EX], hs[:, j, t * P:(t + 1) * P], gate_w,
                                           start=True, stop=True)
                        mm.then_inc(s_lg, 1)
                        if gelu:
                            def up(e):
                                n = EX * b + e
                                if e >= 2:
                                    pe.wait_ge(s_act, n - 1)
                                for k in range(2):
                                    mm = pe.matmul(up_p[:, e % 2, k, :], w1[:, e, k * P:(k + 1) * P], hs[:, j, :],
                                                   start=True, stop=True)
                                mm.then_inc(s_up, 1)

                            up(0)
                            for e in range(EX):
                                n = EX * b + e
                                if e + 1 < EX:
                                    up(e + 1)
                                pe.wait_ge(s_act, n + 1)
                                if e >= 2:
                                    pe.wait_ge(s_acc, ACC * b + TB * (e - 1))
                                else:
                                    pe.wait_ge(s_acc, ACC * b)
                                for t in range(TB):
                                    for k in range(2):
                                        mm = pe.matmul(out_p[:, e % 2, t * P:(t + 1) * P], act_[:, e % 2, k, t * P:(t + 1) * P],
                                                       w2[:, e, k, :], start=(k == 0), stop=(k == 1))
                                mm.then_inc(s_out, 1)
                        else:
                            for n in range(NOUT):
                                t, k = n // 2, n % 2
                                if n >= 2:
                                    pe.wait_ge(s_acc, ACC * b + EX // 2 * (n - 1))
                                else:
                                    pe.wait_ge(s_acc, ACC * b)
                                pe.matmul(out_p[:, n % 2, :], hs[:, j, t * P:(t + 1) * P],
                                          wexp[:, 4 * k:4 * k + 4, :].rearrange("p e f -> p (e f)"),
                                          start=True, stop=True).then_inc(s_out, 1)
                            pe.wait_ge(s_g, G * (b + 1))
                            for t in range(TB):
                                mm = pe.transpose(lg_p[0:EX, t * P:(t + 1) * P], share[:, t, :], m.ident[:, :])
                            mm.then_inc(s_sh, 1)
                        pe.wait_ge(s_acc, ACC * (b + 1))
                        pe.wait_ge(s_x, b)
                        for t in range(TB):
                            mm = pe.matmul(y_p[:, t * P:(t + 1) * P], acc[:, t, :], m.ident[:, :],
                                           start=True, stop=gelu)
                            if t == 0:
                                mm.then_inc(s_free, 1)
                            if not gelu:
                                if t == 0:
                                    pe.wait_ge(s_shT, b + 1)
                                mm = pe.matmul(y_p[:, t * P:(t + 1) * P], bexp[:, :], shareT[:, t * P:(t + 1) * P],
                                               start=False, stop=True)
                        mm.then_inc(s_tr, 1)

            @block.scalar
            def _(act):
                with act.Fori(0, B // 2) as i:
                    for j in range(2):
                        b = 2 * i + j
                        act.wait_ge(s_g, G * b + (6 if gelu else 7))
                        act.activation(ex[:, :, :], sh[:, :, :], ACT.Exp).then_inc(s_ex, 1)
                        if gelu:
                            for e in range(EX):
                                n = EX * b + e
                                act.wait_ge(s_up, n + 1)
                                if e >= 2:
                                    act.wait_ge(s_out, n - 1)
                                act.activation(act_[:, e % 2, :, :], up_p[:, e % 2, :, :], ACT.Gelu).then_inc(s_act, 1)
                        else:
                            act.wait_ge(s_sh, b + 1)
                            act.activation(shareT[:, :], lg_p[0:EX, :], ACT.Copy).then_inc(s_shT, 1)

            @block.vector
            def _(dve):
                dve.wait_ge(s_load, 16 * len(loads))
                with dve.Fori(0, B // 2) as i:
                    for j in range(2):
                        b = 2 * i + j
                        g = [0]

                        def did(ins):
                            g[0] += 1
                            ins.then_inc(s_g, 1)

                        def wait_own():
                            dve.wait_ge(s_g, G * b + g[0])

                        flat = lambda x: x[:, :, :].rearrange("p t e -> p (t e)")
                        dve.wait_ge(s_lg, b + 1)
                        if not gelu:
                            dve.wait_ge(s_shT, b)
                        did(dve.tensor_copy(flat(lg), lg_p[:, 0:TB * EX]))
                        wait_own()
                        if not gelu:
                            did(dve.tensor_tensor(lg[:, :, :], lg[:, :, :], gb[:, :].unsqueeze(1).to_broadcast([P, TB, EX]), ALU.add))
                            wait_own()
                        dve.sem_inc(s_pass, 1)
                        for t in range(TB):
                            did(dve.max(m8[:, t, :], lg[:, t, :]))
                        wait_own()
                        did(dve.tensor_tensor(sh[:, :, :], lg[:, :, :], m8[:, :, 0:1].to_broadcast([P, TB, EX]), ALU.subtract))
                        did(dve.tensor_tensor(mk[:, :, :], lg[:, :, :], m8[:, :, 1:2].to_broadcast([P, TB, EX]), ALU.is_ge))
                        wait_own()
                        dve.wait_ge(s_ex, b + 1)
                        did(dve.tensor_tensor(exm[:, :, :], ex[:, :, :], mk[:, :, :], ALU.mult))
                        wait_own()
                        dve.tensor_reduce(tot[:, :], (exm if gelu else ex)[:, :, :], AX.X, ALU.add).then_inc(s_norm, 1)
                        dve.wait_ge(s_norm, 2 * b + 1)
                        dve.reciprocal(inv[:, :], tot[:, :]).then_inc(s_norm, 1)
                        dve.wait_ge(s_norm, 2 * b + 2)
                        if not gelu:
                            dve.wait_ge(s_sh, b)
                        did(dve.tensor_tensor(share[:, :, :], exm[:, :, :], inv[:, :].unsqueeze(2).to_broadcast([P, TB, EX]), ALU.mult))
                        wait_own()
                        assert g[0] == G, g[0]
                        first = 0
                        if not gelu:
                            dve.wait_ge(s_tr, b)
                        if gelu:
                            order = [(e, e, t) for e in range(EX) for t in range(TB)]
                            dve.wait_ge(s_tr, b)
                        else:
                            order = [(2 * t + e // 4, e, t) for t in range(TB) for e in range(EX)]
                        last = {}
                        for n, (use, e, t) in enumerate(order):
                            dve.wait_ge(s_out, NOUT * b + use + 1)
                            o = out_p[:, use % 2, (t * P if gelu else (e % 4) * P):][:, 0:P]
                            sc = share[:, t, e:e + 1]
                            if e == 0 and gelu:
                                ins = dve.tensor_scalar(acc[:, t, :], o, sc, None, ALU.mult)
                            else:
                                if t in last:
                                    dve.wait_ge(s_acc, ACC * b + last[t] + 1)
                                ins = dve.scalar_tensor_tensor(acc[:, t, :], o, sc, acc[:, t, :] if t in last else m.attn[:, b, t, :],
                                                               ALU.mult, ALU.add)
                            ins.then_inc(s_acc, 1)
                            last[t] = n
                        dve.wait_ge(s_tr, b + 1)
                        dve.scalar_tensor_tensor(m.xT[:, b, :], y_p[:, :], m.mod[:, layer, 3 + GATE, bass.ds(b, 1)], m.xT[:, b, :],
                                                 ALU.mult, ALU.add).then_inc(s_x, 1)


def store(nc, m, a, out):
    with ExitStack() as c:
        sem = lambda n: c.enter_context(nc.semaphore("st_" + n))
        rows = c.enter_context(nc.sbuf_tensor("st_rows", [P, B, TB, P], F32))
        turned = c.enter_context(nc.psum_tensor("st_turned", [P, 4, S], F32))
        s_t, s_c, s_o = sem("t"), sem("c"), sem("o")
        with nc.Block() as block:
            @block.tensor
            def _(pe):
                for b in range(B):
                    if b >= 4:
                        pe.wait_ge(s_c, b - 3)
                    for t in range(TB):
                        mm = pe.transpose(turned[:, b % 4, t * P:(t + 1) * P], m.xT[:, b, t * P:(t + 1) * P], m.ident[:, :])
                    mm.then_inc(s_t, 1)

            @block.vector
            def _(dve):
                for b in range(B):
                    dve.wait_ge(s_t, b + 1)
                    dve.tensor_copy(rows[:, b, :, :].rearrange("p t d -> p (t d)"), turned[:, b % 4, :]).then_inc(s_c, 1)

            @block.sync
            def _(sp):
                for b in range(B):
                    sp.wait_ge(s_c, b + 1)
                    sp.dma_start(out[b].rearrange("(t p) d -> p t d", p=P), rows[:, b, :, :]).then_inc(s_o, 16)
                sp.wait_ge(s_o, 16 * B)


def program(nc, a, out, upto=99, dump=None):
    m = Memory()
    with ExitStack() as ctx:
        sb = lambda n, s, d=F32: ctx.enter_context(nc.sbuf_tensor(n, s, d))
        m.ident = sb("ident", [P, P])
        m.ident_b = sb("ident_b", [P, P], BF16)
        m.attn = sb("attn", [P, B, TB, P])
        m.mean_w = sb("mean_w", [P, P])
        m.xT = sb("xT", [P, B, S])
        m.hT = sb("hT", [P, B, WINDOW + S])
        m.small_T = sb("small_T", [P, 3, EX])
        m.wqT = sb("wqT", [P, HEADS * HD0])
        m.wkvT = sb("wkvT", [P, 2 * KV0 * HD0])
        m.woT = sb("woT", [P, PAIRS, P])
        m.mod = sb("mod", [P, 2, 6, B])
        m.qk_w = sb("qk_w", [P, 3])
        m.eps = sb("eps", [P, 2])
        setup(nc, m, a, ctx)
        layer_norm(nc, m, 0, 0, "ln0_")
        if upto >= 1:
            window_attention(nc, m, a)
        if upto >= 2:
            layer_norm(nc, m, 0, 1, "ln1_")
            experts(nc, m, a, True)
        if upto >= 3:
            layer_norm(nc, m, 1, 0, "ln2_")
            head_attention(nc, m, a, True)
        if upto >= 4:
            layer_norm(nc, m, 1, 1, "ln3_")
            head_attention(nc, m, a, False)
            experts(nc, m, a, False)
            if out is not None:
                store(nc, m, a, out)
        if dump:
            dump(nc, m, ctx)


def constants():
    import numpy as np
    bf16 = mybir.dt.np(BF16)
    out = {"c_ident": np.eye(P, dtype=np.float32), "c_ident_b": np.eye(P).astype(bf16)}
    stat2 = np.zeros((6, 2, 2, S))
    stat2[3:6, 0] = 1.0
    stat2[0:3, 1] = 1.0
    out["c_stat2"] = stat2.astype(bf16)
    out["c_stat1"] = np.ones((3, 1, 2, S)).astype(bf16)
    half = np.zeros((P, P + 2), np.float32)
    for i in range(2):
        half[HD0 * i:HD0 * (i + 1), HD0 * i:HD0 * (i + 1)] = 1.0 / HD0
        half[HD0 * i:HD0 * (i + 1), P + i] = 1.0 / HD0
    out["c_half"] = half
    query, key = np.arange(P)[:, None], np.arange(WIN)[None, :]
    rel = key - WINDOW - query % SUB
    slopes = (2.0 ** (-0.5)) ** np.arange(1, HEADS + 1, dtype=np.float32)
    table = np.zeros((P, 2, HEADS, WIN), np.float32)
    for first in range(2):
        masked = (rel > 0) | (rel < -WINDOW)
        if first == 0:
            masked = masked | (query + rel < 0)
        for h in range(HEADS):
            table[:, first, h] = np.where(masked, -1e30, slopes[h] * rel.astype(np.float32))
    out["c_bias"] = table.reshape(P, 2, PAIRS, 2, WIN)
    return out


def kernel(**inputs):
    import numpy as _np
    import concourse.bacc as _bacc
    from concourse.bass_utils import run_bass_kernel_spmd as _run

    nc = _bacc.Bacc("TRN2", target_bir_lowering=False, num_devices=1)
    arrays, aps = {}, {}
    for name, x in list(inputs.items()) + list(constants().items()):
        x = _np.ascontiguousarray(x)
        arrays[f"in_{name}_dram"] = x
        aps[name] = nc.dram_tensor(f"in_{name}_dram", x.shape, mybir.dt.from_np(x.dtype), kind="ExternalInput").ap()
    out = nc.dram_tensor("out_dram", (B, S, P), F32, kind="ExternalOutput").ap()
    program(nc, aps, out)
    r = _run(nc, [arrays], core_ids=[0])
    return r.results[0]["out_dram"]
```

```python
from contextlib import ExitStack

import concourse.bass as bass
from concourse import mybir

F32 = mybir.dt.float32
BF16 = mybir.dt.bfloat16
ALU = mybir.AluOpType
ACT = mybir.ActivationFunctionType
AX = mybir.AxisListType

P = 128
B = 8
S = 512
TB = S // P
HEADS = 16

HD0 = 64
KV0 = 4
PAIRS = HEADS // 2
WINDOW = 16
SUB = 32
WIN = SUB + WINDOW
SLOT = 64
EPS0 = 0.01

EX = 8
FF = 256

HD1 = 8
KEEP = int(S * (1.0 - 0.9))
LN_EPS = 1e-5
GATE_MIN = 0.25
SHIFT_IN, SCALE_IN, GATE = 0, 1, 2


class Memory:
    pass


def setup(nc, m, a, ctx):
    with ExitStack() as c:
        sb = lambda n, s, d=F32: c.enter_context(nc.sbuf_tensor(n, s, d))
        sem = lambda n: nc.alloc_semaphore(n)
        x_rows = sb("x_rows", [P, B * TB, P])
        wq_rows = sb("wq_rows", [P, PAIRS, P])
        wkv_rows = sb("wkv_rows", [P, 4, P])
        wo_rows = sb("wo_rows", [P, PAIRS, P])
        small_rows = sb("small_rows", [EX, 3, P])
        wmod = sb("wmod", [P, 2, 6 * P])
        silu = sb("silu", [P, 2 * B])
        work = sb("silu_work", [P, 2 * B])
        absmod = sb("absmod", [P, 2, 6, B])
        turned = c.enter_context(nc.psum_tensor("turned", [P, 4, 512], F32))
        modp = c.enter_context(nc.psum_tensor("modp", [P, 2, 6, B], F32))
        loaded, x_loaded = sem("loaded"), sem("x_loaded")
        turn_done, turn_copied, mod_done, step, exps = (
            sem("turn_done"), sem("turn_copied"), sem("mod_done"), sem("setup_step"), sem("exp_done"))

        jobs = []
        jobs.append([(small_rows[:, i, :], EX) for i in range(3)])
        for g in range(2):
            jobs.append([(wq_rows[:, 4 * g + i, :], P) for i in range(4)])
        jobs.append([(wkv_rows[:, i, :], P) for i in range(4)])
        for g in range(2):
            jobs.append([(wo_rows[:, 4 * g + i, :], P) for i in range(4)])
        dests = [m.small_T[:, :, :].rearrange("p a b -> p (a b)"), m.wqT[:, 0:512], m.wqT[:, 512:1024], m.wkvT[:, :],
                 m.woT[:, 0:4, :].rearrange("p a b -> p (a b)"), m.woT[:, 4:8, :].rearrange("p a b -> p (a b)")]
        n_weights = len(jobs)
        for b in range(B):
            jobs.append([(x_rows[:, TB * b + i, :], P) for i in range(TB)])
            dests.append(m.xT[:, b, :])

        loads = [
            (m.ident[:, :], a["c_ident"]), (m.ident_b[:, :], a["c_ident_b"]),
            (small_rows[:, 0, :], a["L0_c"]), (small_rows[:, 1, :], a["L1_c"]),
            (small_rows[:, 2, :], a["L0_ffn_router_w"]),
            (wmod[:, 0, :], a["L0_wmod"]), (wmod[:, 1, :], a["L1_wmod"]),
            (wq_rows[:, :, :], a["L0_attn_wq"].rearrange("(g p) d -> p g d", p=P)),
            (wkv_rows[:, 0:2, :], a["L0_attn_wk"].rearrange("(g p) d -> p g d", p=P)),
            (wkv_rows[:, 2:4, :], a["L0_attn_wv"].rearrange("(g p) d -> p g d", p=P)),
            (wo_rows[:, :, :], a["L0_attn_wo"].rearrange("p (g d) -> p g d", d=P)),
            (m.qk_w[0:HD0, 0:1], a["L0_attn_q_norm_w"].rearrange("(p o) -> p o", o=1)),
            (m.qk_w[HD0:P, 0:1], a["L0_attn_q_norm_w"].rearrange("(p o) -> p o", o=1)),
            (m.qk_w[0:HD0, 1:2], a["L0_attn_k_norm_w"].rearrange("(p o) -> p o", o=1)),
            (m.qk_w[HD0:P, 1:2], a["L0_attn_k_norm_w"].rearrange("(p o) -> p o", o=1)),
        ]
        with nc.Block() as block:
            @block.sync
            def _(sp):
                for dst, src in loads:
                    sp.dma_start(dst, src).then_inc(loaded, 16)
                x_src = a["L0_attn_x"].rearrange("b (t p) d -> p (b t) d", p=P)
                for b in range(B):
                    sp.dma_start(x_rows[:, TB * b:TB * b + TB, :], x_src[:, TB * b:TB * b + TB, :]).then_inc(x_loaded, 16)

            @block.tensor
            def _(pe):
                pe.wait_ge(loaded, 16 * len(loads))
                for n, job in enumerate(jobs):
                    if n == n_weights:
                        pe.wait_ge(x_loaded, 16 * B)
                    if n == 1:
                        pe.wait_ge(step, 2)
                        for layer in range(2):
                            for j in range(6):
                                mm = pe.matmul(modp[:, layer, j, :], wmod[:, layer, j * P:(j + 1) * P],
                                               silu[:, layer * B:(layer + 1) * B], start=True, stop=True)
                        mm.then_inc(mod_done, 1)
                    if n >= 4:
                        pe.wait_ge(turn_copied, n - 3)
                    at = 0
                    for rows, k in job:
                        mm = pe.transpose(turned[:, n % 4, at:at + k], rows, m.ident[0:k, 0:k])
                        at += k
                    mm.then_inc(turn_done, 1)

            @block.scalar
            def _(act):
                act.wait_ge(turn_copied, 1)
                act.activation(work[:, :], m.small_T[:, 0:2, :].rearrange("p a b -> p (a b)"), ACT.Exp,
                               scale=-1.0).then_inc(exps, 1)

            @block.vector
            def _(dve):
                def copy(n):
                    dve.wait_ge(turn_done, n + 1)
                    width = sum(k for _, k in jobs[n])
                    dve.tensor_copy(dests[n], turned[:, n % 4, 0:width]).then_inc(turn_copied, 1)

                copy(0)
                dve.wait_ge(exps, 1)
                dve.tensor_scalar(silu[:, :], work[:, :], 1.0, None, ALU.add).then_inc(step, 1)
                dve.wait_ge(step, 1)
                dve.reciprocal(work[:, :], silu[:, :]).then_inc(exps, 1)
                dve.wait_ge(exps, 2)
                dve.tensor_tensor(silu[:, :], m.small_T[:, 0:2, :].rearrange("p a b -> p (a b)"), work[:, :],
                                  ALU.mult).then_inc(step, 1)
                for n in range(1, len(jobs)):
                    copy(n)
                dve.wait_ge(mod_done, 1)
                dve.tensor_copy(m.mod[:, :, :, :], modp[:, :, :, :]).then_inc(step, 1)
                dve.wait_ge(step, 3)
                dve.scalar_tensor_tensor(absmod[:, :, :, :].rearrange("p a b c -> p (a b c)"),
                                         m.mod[:, :, :, :].rearrange("p a b c -> p (a b c)"), -1.0,
                                         m.mod[:, :, :, :].rearrange("p a b c -> p (a b c)"),
                                         ALU.mult, ALU.max).then_inc(step, 1)
                dve.wait_ge(step, 4)
                n = 4
                for layer in range(2):
                    for j in (GATE, 3 + GATE):
                        g = m.mod[:, layer, j, :]
                        ab = absmod[:, layer, j, :]
                        dve.tensor_scalar(ab, ab, GATE_MIN, None, ALU.max).then_inc(step, 1)
                        dve.tensor_scalar(g, g, 0.0, 2.0, ALU.is_ge, ALU.mult).then_inc(step, 1)
                        n += 2
                        dve.wait_ge(step, n)
                        dve.scalar_tensor_tensor(g, g, -1.0, ab, ALU.add, ALU.mult).then_inc(step, 1)
                        n += 1
                    for j in (SCALE_IN, 3 + SCALE_IN):
                        g = m.mod[:, layer, j, :]
                        dve.tensor_scalar(g, g, 1.0, None, ALU.add).then_inc(step, 1)
                        n += 1
                dve.tensor_tensor(m.qk_w[:, 2:3], m.qk_w[:, 0:1], m.qk_w[:, 1:2], ALU.mult).then_inc(step, 1)
                n += 1
                dve.wait_ge(step, n)
                dve.tensor_scalar(m.qk_w[:, 2:3], m.qk_w[:, 2:3], float(HD0) ** -0.5, None, ALU.mult)
                dve.memset(m.hT[:, :, 0:WINDOW], 0.0)
                dve.memset(m.eps[:, 0:1], LN_EPS)
                dve.memset(m.eps[:, 1:2], EPS0)
                dve.memset(m.mean_w[:, :], 1.0 / P)


def layer_norm(nc, m, layer, part, name):
    with ExitStack() as c:
        sb = lambda n, s, d=F32: c.enter_context(nc.sbuf_tensor(name + n, s, d))
        sem = lambda n: nc.alloc_semaphore(name + n)
        centered = sb("centered", [P, 2, S])
        squared = sb("squared", [P, 2, S])
        std = sb("std", [P, 2, S])
        rstd = sb("rstd", [P, 2, S])
        normed = sb("normed", [P, 2, S])
        mean_p = c.enter_context(nc.psum_tensor(name + "mean_p", [P, 2, S], F32))
        var_p = c.enter_context(nc.psum_tensor(name + "var_p", [P, 2, S], F32))
        s_mean, s_cent, s_sq, s_var, s_std, s_rstd, s_norm, s_h = map(
            sem, ("mean", "cent", "sq", "var", "std", "rstd", "norm", "h"))
        done = lambda b: b + 3
        free = lambda b: b + 1
        shift, scale = m.mod[:, layer, 3 * part + SHIFT_IN, :], m.mod[:, layer, 3 * part + SCALE_IN, :]
        with nc.Block() as block:
            @block.tensor
            def _(pe):
                pe.sem_inc(s_mean, 2)
                pe.sem_inc(s_var, 2)
                with pe.Fori(0, B // 2) as i:
                    for j in range(2):
                        b = 2 * i + j
                        pe.wait_ge(s_cent, free(b))
                        pe.matmul(mean_p[:, j, :], m.mean_w[:, :], m.xT[:, b, :], start=True, stop=True).then_inc(s_mean, 1)
                    for j in range(2):
                        b = 2 * i + j
                        pe.wait_ge(s_std, free(b))
                        pe.wait_ge(s_sq, done(b))
                        pe.matmul(var_p[:, j, :], m.mean_w[:, :], squared[:, j, :], start=True, stop=True).then_inc(s_var, 1)

            @block.scalar
            def _(act):
                act.sem_inc(s_sq, 2)
                act.sem_inc(s_std, 2)
                act.sem_inc(s_h, 2)
                with act.Fori(0, B // 2) as i:
                    for j in range(2):
                        b = 2 * i + j
                        act.wait_ge(s_cent, done(b))
                        act.wait_ge(s_var, free(b))
                        act.activation(squared[:, j, :], centered[:, j, :], ACT.Square).then_inc(s_sq, 1)
                    for j in range(2):
                        b = 2 * i + j
                        act.wait_ge(s_var, done(b))
                        act.wait_ge(s_rstd, free(b))
                        act.activation(std[:, j, :], var_p[:, j, :], ACT.Sqrt, bias=m.eps[:, 0:1]).then_inc(s_std, 1)
                    for j in range(2):
                        b = 2 * i + j
                        act.wait_ge(s_norm, done(b))
                        act.activation(m.hT[:, b, WINDOW:], normed[:, j, :], ACT.Identity, bias=shift[:, bass.ds(b, 1)],
                                       scale=scale[:, bass.ds(b, 1)]).then_inc(s_h, 1)

            @block.vector
            def _(dve):
                dve.sem_inc(s_cent, 2)
                dve.sem_inc(s_rstd, 2)
                dve.sem_inc(s_norm, 2)
                with dve.Fori(0, B // 2) as i:
                    for j in range(2):
                        b = 2 * i + j
                        dve.wait_ge(s_mean, done(b))
                        dve.wait_ge(s_sq, free(b))
                        dve.wait_ge(s_norm, free(b))
                        dve.tensor_tensor(centered[:, j, :], m.xT[:, b, :], mean_p[:, j, :], ALU.subtract).then_inc(s_cent, 1)
                    for j in range(2):
                        b = 2 * i + j
                        dve.wait_ge(s_std, done(b))
                        dve.wait_ge(s_norm, free(b))
                        dve.reciprocal(rstd[:, j, :], std[:, j, :]).then_inc(s_rstd, 1)
                    for j in range(2):
                        b = 2 * i + j
                        dve.wait_ge(s_rstd, done(b))
                        dve.wait_ge(s_cent, done(b))
                        dve.wait_ge(s_h, free(b))
                        dve.tensor_tensor(normed[:, j, :], centered[:, j, :], rstd[:, j, :], ALU.mult).then_inc(s_norm, 1)


def window_attention(nc, m, a):
    with ExitStack() as c:
        sb = lambda n, s, d=F32: c.enter_context(nc.sbuf_tensor("wa_" + n, s, d))
        pb = lambda n, s: c.enter_context(nc.psum_tensor("wa_" + n, s, F32))
        sem = lambda n: nc.alloc_semaphore("wa_" + n)
        hs = sb("hs", [P, WINDOW + S + SLOT - WIN])
        q = sb("q", [P, PAIRS, S])
        qsq = sb("qsq", [P, PAIRS, S])
        k = sb("k", [P, 2, S])
        ksq = sb("ksq", [P, 2, S])
        kstd = sb("kstd", [P, 2, S])
        krstd = sb("krstd", [P, 2, S])
        kT = sb("kT", [P, 2, WINDOW + S])
        vw = sb("vw", [P, S // SUB, P])
        qstd = sb("qstd", [P, TB, 2, PAIRS])
        qrstd = sb("qrstd", [P, TB, 2, PAIRS])
        half = sb("half", [P, P + 2])
        bias = sb("bias", [P, 2, PAIRS, 2, WIN])
        sc = sb("sc", [P, 2, PAIRS, 2, WIN])
        pr = sb("pr", [P, 2, PAIRS, 2, SLOT])
        mx = sb("mx", [P, 2, PAIRS, 2])
        sm = sb("sm", [P, 2, PAIRS, 2])
        rs = sb("rs", [P, 2, PAIRS, 2])
        pT = sb("pT", [P, PAIRS, P])
        ao = sb("ao", [P, PAIRS, S])
        bank = pb("bank", [P, 2, S])
        sp = pb("sp", [P, 2, S])
        tp = pb("tp", [P, PAIRS, P])
        op = pb("op", [P, PAIRS, P])
        (s_const, s_zero, s_hs, s_use, s_free, s_vfree, s_kr, s_k, s_qr, s_S, s_mult, s_bias, s_max, s_sub, s_exp, s_sum,
         s_rs, s_p, s_t, s_pT, s_pv, s_ao, s_x, s_pass) = map(sem, (
             "const", "zero", "hs", "use", "free", "vfree", "kr", "k", "qr", "S", "mult", "bias", "max", "sub", "exp",
             "sum", "rs", "p", "t", "pT", "pv", "ao", "x", "pass"))
        Q0, K0, V0, M0, RQ, Y = 0, PAIRS, PAIRS + 2, PAIRS + 6, PAIRS + 8, PAIRS + 9
        USES = PAIRS + 10
        READ = USES - 1
        wv = m.wkvT[:, 2 * P:].rearrange("p (a par d) -> p par a d", par=2, d=HD0)

        with nc.Block() as block:
            @block.sync
            def _(sp_):
                sp_.dma_start(half[:, :], a["c_half"]).then_inc(s_const, 16)
                sp_.dma_start(bias[:, :, :, :, :], a["c_bias"]).then_inc(s_const, 16)

            @block.gpsimd
            def _(pool):
                pool.memset(hs[:, WINDOW + S:], 0.0).then_inc(s_zero, 1)
                pool.memset(kT[:, :, 0:WINDOW], 0.0).then_inc(s_zero, 1)
                pool.memset(pr[:, :, :, :, :], 0.0).then_inc(s_zero, 1)
                with pool.Fori(0, B) as b:
                    pool.wait_ge(s_vfree, b)
                    pool.tensor_copy(hs[:, 0:WINDOW + S], m.hT[:, b, :]).then_inc(s_hs, 1)

            @block.tensor
            def _(pe):
                pe.wait_ge(s_const, 32)
                pe.wait_ge(s_zero, 3)
                with pe.Fori(0, B) as b:
                    def to(n):
                        if n == 1:
                            pe.wait_ge(s_x, b)
                            pe.wait_ge(s_free, READ * b)
                        else:
                            pe.wait_ge(s_free, READ * b + max(n - 1, 0))
                        return bank[:, n % 2, :]

                    pe.wait_ge(s_hs, b + 1)
                    for g in range(PAIRS):
                        o = to(Q0 + g)
                        pe.matmul(o, m.wqT[:, g * P:(g + 1) * P], hs[:, WINDOW:WINDOW + S],
                                  start=True, stop=True).then_inc(s_use, 1)
                    for g in range(2):
                        o = to(K0 + g)
                        pe.matmul(o, m.wkvT[:, g * P:(g + 1) * P], hs[:, WINDOW:WINDOW + S],
                                  start=True, stop=True).then_inc(s_use, 1)
                    for g in range(4):
                        o = to(V0 + g)
                        for w in range(4):
                            at = (4 * g + w) * SUB
                            for par in range(2):
                                mm = pe.matmul(o[SLOT * par:SLOT * par + SLOT, w * P:(w + 1) * P], hs[:, at:at + SLOT],
                                               wv[:, par, :, :], start=True, stop=True)
                        mm.then_inc(s_use, 1)
                    for g in range(2):
                        o = to(M0 + g)
                        pe.matmul(o, half[:, 0:P], ksq[:, g, :], start=True, stop=True).then_inc(s_use, 1)
                    o = to(RQ)[:, 0:TB * HEADS].rearrange("p (t par g) -> p t par g", t=TB, par=2)
                    for t in range(TB):
                        for g in range(PAIRS):
                            mm = pe.matmul(o[:, t, :, g], qsq[:, g, t * P:(t + 1) * P], half[:, P:P + 2],
                                           start=True, stop=True)
                            if t == 0 and g == 0:
                                mm.then_inc(s_vfree, 1)
                    mm.then_inc(s_use, 1)

                    def scores(t):
                        if t == 0:
                            pe.wait_ge(s_k, b + 1)
                        pe.wait_ge(s_mult, TB * b + t)
                        pe.sem_inc(s_pass, 1)
                        for par in range(2):
                            for g in range(PAIRS):
                                for j in range(P // SUB):
                                    at = t * P + SUB * j
                                    mm = pe.matmul(sp[SUB * j:SUB * j + SUB, par, g * WIN:(g + 1) * WIN],
                                                   q[SLOT * par:SLOT * par + SLOT, g, at:at + SUB],
                                                   kT[SLOT * par:SLOT * par + SLOT, g % 2, at:at + WIN],
                                                   start=True, stop=True)
                        mm.then_inc(s_S, 1)

                    def values(t):
                        n = TB * b + t
                        pe.wait_ge(s_p, n + 1)
                        pe.wait_ge(s_pT, n)
                        for g in range(PAIRS):
                            mm = pe.transpose(tp[:, g, :], pr[:, t % 2, g, :, :].rearrange("p a k -> p (a k)"), m.ident[:, :])
                        mm.then_inc(s_t, 1)
                        pe.wait_ge(s_pT, n + 1)
                        pe.wait_ge(s_ao, n)
                        pe.sem_inc(s_pass, 1)
                        for g in range(PAIRS):
                            for j in range(P // SUB):
                                for par in range(2):
                                    rows = slice(SLOT * par, SLOT * par + SLOT)
                                    mm = pe.matmul(op[rows, g, SUB * j:SUB * j + SUB],
                                                   vw[rows, 4 * t + j, (g % 2) * HD0:(g % 2 + 1) * HD0],
                                                   pT[rows, g, SUB * j:SUB * j + SUB], start=True, stop=True)
                        mm.then_inc(s_pv, 1)

                    scores(0)
                    for t in range(TB):
                        if t + 1 < TB:
                            scores(t + 1)
                        values(t)
                    o = to(Y)
                    pe.wait_ge(s_ao, TB * (b + 1))
                    for g in range(PAIRS):
                        mm = pe.matmul(o, m.woT[:, g, :], ao[:, g, :], start=(g == 0), stop=(g == PAIRS - 1))
                    mm.then_inc(s_use, 1)

            @block.scalar
            def _(act):
                with act.Fori(0, B) as b:
                    def use(n):
                        act.wait_ge(s_use, USES * b + n + 1)
                        return bank[:, n % 2, :]

                    for g in range(PAIRS):
                        o = use(Q0 + g)
                        act.activation(q[:, g, :], o, ACT.Copy)
                        act.activation(qsq[:, g, :], o, ACT.Square).then_inc(s_free, 1)
                    for g in range(2):
                        o = use(K0 + g)
                        act.activation(k[:, g, :], o, ACT.Copy)
                        act.activation(ksq[:, g, :], o, ACT.Square).then_inc(s_free, 1)
                    for g in range(4):
                        o = use(V0 + g)
                        act.activation(vw[:, 4 * g:4 * g + 4, :].rearrange("p a b -> p (a b)"), o, ACT.Copy).then_inc(s_free, 1)
                    for g in range(2):
                        o = use(M0 + g)
                        act.activation(kstd[:, g, :], o, ACT.Sqrt, bias=m.eps[:, 1:2]).then_inc(s_free, 1)
                    o = use(RQ)
                    act.activation(qstd[:, :, :, :].rearrange("p t a g -> p (t a g)"), o[:, 0:TB * HEADS], ACT.Sqrt,
                                   bias=m.eps[:, 1:2]).then_inc(s_free, 1)

                    def exp(t):
                        act.wait_ge(s_sub, TB * b + t + 1)
                        act.activation(pr[:, t % 2, :, :, 0:WIN].rearrange("p g a k -> p (g a) k"),
                                       sc[:, t % 2, :, :, :].rearrange("p g a k -> p (g a) k"), ACT.Exp).then_inc(s_exp, 1)

                    exp(0)
                    for t in range(TB):
                        if t + 1 < TB:
                            if t >= 1:
                                act.wait_ge(s_t, TB * b + t)
                            exp(t + 1)
                        act.wait_ge(s_t, TB * b + t + 1)
                        act.activation(pT[:, :, :], tp[:, :, :], ACT.Copy).then_inc(s_pT, 1)
                        act.wait_ge(s_pv, TB * b + t + 1)
                        act.activation(ao[:, :, t * P:(t + 1) * P], op[:, :, :], ACT.Copy).then_inc(s_ao, 1)

            @block.vector
            def _(dve):
                dve.wait_ge(s_const, 32)
                with dve.Fori(0, B) as b:
                    dve.wait_ge(s_free, READ * b + M0 + 2)
                    dve.reciprocal(krstd[:, :, :], kstd[:, :, :]).then_inc(s_kr, 1)
                    dve.wait_ge(s_kr, b + 1)
                    for g in range(2):
                        ins = dve.scalar_tensor_tensor(kT[:, g, WINDOW:], k[:, g, :], m.qk_w[:, 2:3], krstd[:, g, :],
                                                       ALU.mult, ALU.mult)
                    ins.then_inc(s_k, 1)
                    dve.wait_ge(s_free, READ * b + RQ + 1)
                    dve.reciprocal(qrstd[:, :, :, :], qstd[:, :, :, :]).then_inc(s_qr, 1)
                    dve.wait_ge(s_qr, b + 1)

                    def logits(t):
                        n, i = TB * b + t, t % 2
                        dve.wait_ge(s_S, n + 1)
                        s_ = sc[:, i, :, :, :].rearrange("p g a k -> p a g k")
                        for par in range(2):
                            ins = dve.tensor_tensor(s_[:, par], sp[:, par, 0:PAIRS * WIN].rearrange("p (g k) -> p g k", g=PAIRS),
                                                    qrstd[:, t, par, :].unsqueeze(2).to_broadcast([P, PAIRS, WIN]), ALU.mult)
                        ins.then_inc(s_mult, 1)
                        dve.wait_ge(s_mult, n + 1)
                        flat = sc[:, i, :, :, :].rearrange("p g a k -> p (g a k)")
                        dve.tensor_tensor(flat, flat, bias[:, 0 if t == 0 else 1, :, :, :].rearrange("p g a k -> p (g a k)"),
                                          ALU.add).then_inc(s_bias, 1)
                        dve.wait_ge(s_bias, n + 1)
                        rows = sc[:, i, :, :, :].rearrange("p g a k -> p (g a) k")
                        m_ = mx[:, i, :, :].rearrange("p g a -> p (g a)")
                        dve.tensor_reduce(m_, rows, AX.X, ALU.max).then_inc(s_max, 1)
                        dve.wait_ge(s_max, n + 1)
                        dve.tensor_tensor(rows, rows, m_.unsqueeze(2).to_broadcast([P, HEADS, WIN]),
                                          ALU.subtract).then_inc(s_sub, 1)

                    def normalise(t):
                        n, i = TB * b + t, t % 2
                        rows = pr[:, i, :, :, 0:WIN].rearrange("p g a k -> p (g a) k")
                        s_ = sm[:, i, :, :].rearrange("p g a -> p (g a)")
                        r_ = rs[:, i, :, :].rearrange("p g a -> p (g a)")
                        dve.wait_ge(s_exp, n + 1)
                        dve.tensor_reduce(s_, rows, AX.X, ALU.add).then_inc(s_sum, 1)
                        dve.wait_ge(s_sum, n + 1)
                        dve.reciprocal(r_, s_).then_inc(s_rs, 1)
                        dve.wait_ge(s_rs, n + 1)
                        dve.tensor_tensor(rows, rows, r_.unsqueeze(2).to_broadcast([P, HEADS, WIN]), ALU.mult).then_inc(s_p, 1)

                    logits(0)
                    for t in range(TB):
                        if t + 1 < TB:
                            logits(t + 1)
                        normalise(t)
                    dve.wait_ge(s_use, USES * b + Y + 1)
                    dve.scalar_tensor_tensor(m.xT[:, b, :], bank[:, Y % 2, :], m.mod[:, 0, GATE, bass.ds(b, 1)], m.xT[:, b, :],
                                             ALU.mult, ALU.add).then_inc(s_x, 1)


SPLIT_Q = (0, 0, 0, 1, 1, 2)
SPLIT_K = (0, 1, 2, 0, 1, 0)
GROUPS = len(SPLIT_Q)
ROWS = GROUPS * HD1
QUAD = 4
QUADS = HEADS // QUAD
COL = 32
VW = HD1 + 1
LOW = -3.0e38


def head_attention(nc, m, a, sparse):
    tag = "sp_" if sparse else "de_"
    with ExitStack() as c:
        sb = lambda n, s, d=F32: c.enter_context(nc.sbuf_tensor(tag + n, s, d))
        pb = lambda n, s: c.enter_context(nc.psum_tensor(tag + n, s, F32))
        sem = lambda n: nc.alloc_semaphore(tag + n)
        KINDS = 2 if sparse else 1
        STAT = 3 * KINDS
        K_SIDES = 2 if sparse else 1
        scratch = nc.dram_tensor(tag + "scratch", (B, 2, HEADS, ROWS, S), BF16, kind="Internal").ap()

        hs = sb("hs", [P, S])
        w_q, w_k, w_v, w_o = (sb(n, [P, P]) for n in ("w_q", "w_k", "w_v", "w_o"))
        cols = sb("cols", [P, 3])
        bq = sb("bq", [P, 1])
        bv = sb("bv", [P, P])
        ones = sb("ones", [P, P])
        qk = sb("qk", [P, 2, S])
        rest = sb("rest", [P, 2, S])
        part = sb("part", [P, 3, 2, S], BF16)
        v = sb("v", [P, TB, HEADS, COL])
        stack_q = sb("stack_q", [P, 2, 2, S], BF16)
        stack_k = sb("stack_k", [P, 2, K_SIDES, 2, S], BF16)
        stat = sb("stat", [P, 2, TB, QUAD, KINDS])
        stat_rest = sb("stat_rest", [P, TB, QUAD, KINDS])
        stat_part = sb("stat_part", [P, TB, QUAD, KINDS, 3], BF16)
        statT = sb("statT", [QUAD * STAT, 2, S], BF16)
        e = sb("e", [P, 2, 2, S])
        u_sb = sb("u_sb", [P, KINDS, S])
        zr = sb("zr", [P, TB, QUAD, 1])
        tok = sb("tok", [P, TB, P])
        if sparse:
            work = sb("work", [P, 2, S])
            m8 = sb("m8", [P, 2, 7, 8])
            sumv = sb("sumv", [P, HEADS, COL])
            vrest = sb("vrest", [P, 2, TB, P])
            vpart = sb("vpart", [P, TB, HEADS, COL], BF16)
            vp2 = sb("vp2", [P, TB, P], BF16)
            mask = sb("mask", [P, 2, QUAD, S], BF16)
            w = sb("w", [P, 2, QUAD, S])
            floor = sb("floor", [P, 2, TB, QUAD])
            tot = sb("tot", [P, TB, QUAD, VW])
            tot2 = sb("tot2", [P, TB, QUAD, VW])
            aT = sb("aT", [P, S])
            y = sb("y", [P, S])
        bank = pb("bank", [P, 2, S])
        h_p = pb("h_p", [P, 2, S])
        g_p = pb("g_p", [P, 2, S]) if sparse else None
        u_p = [pb(f"u_p{i}", [P, S]) for i in range(KINDS)]

        (s_load, s_one, s_hs, s_use, s_f0, s_f1, s_qk, s_split, s_vone, s_wr, s_ld, s_st, s_sp, s_hp, s_exp, s_pv, s_u,
         s_kd, s_fin, s_sg, s_pass) = map(sem, ("load", "one", "hs", "use", "free0", "free1", "qk", "split", "vone", "wr", "ld",
                                          "st", "sp", "hp", "exp", "pv", "u", "kd", "fin", "sg", "pass"))
        s_v, s_top, s_fl, s_gp, s_mk, s_w, s_tok, s_rel = (
            map(sem, ("v", "top", "fl", "gp", "mk", "w", "tok", "rel")) if sparse else [None] * 8)
        s_bank = (s_f0, s_f1)

        uses = ["q", "k", "v", "vs"] if sparse else ["q", "k", "v", "v2"]
        plan = [("A",)]
        for s in range(QUAD):
            plan.append(("Q", 0, s))
        plan.append(("T", 0))
        for r in range(QUADS):
            for s in range(QUAD):
                if r + 1 < QUADS:
                    plan.append(("Q", r + 1, s))
                plan.append(("K", r, s))
            if r + 1 < QUADS:
                plan.append(("T", r + 1))
            plan.append(("F", r))
        if sparse:
            plan.append(("Y",))
        for it in plan:
            if it[0] == "Q":
                uses += [("S", it[1], it[2], t) for t in range(TB)]
            if it[0] == "T":
                uses.append(("T", it[1]))
            if it[0] == "F":
                uses += [("F", it[1], k) for k in range(KINDS)]
            if it[0] == "Y":
                uses += ["aT", "y"]
        index = {u: n for n, u in enumerate(uses)}
        USES = len(uses)
        assert USES % 2 == 0
        CHUNK2 = QUADS * TB * 2
        CHUNKS = QUADS * TB
        TOPS = HEADS * TB // 2 * 13

        def used(eng, b, u):
            n = index[u]
            eng.wait_ge(s_use, USES * b + n + 1)
            return bank[:, n % 2, :]

        def freed(u):
            return s_bank[index[u] % 2]

        def released(eng, b, u):
            n = index[u]
            eng.wait_ge(s_bank[n % 2], (USES // 2) * b + n // 2 + 1)

        wname = "L1_attn_" if sparse else "L1_ffn_"
        if sparse:
            srcs = [(w_q, a["L1_attn_Wq"]), (w_k, a["L1_attn_Wk"]), (w_v, a["L1_attn_Wv"]), (w_o, a["L1_attn_Wo"])]
            bias = [a["L1_attn_bq"], a["L1_attn_bk"], a["L1_attn_bo"], a["L1_attn_bv"]]
        else:
            wqkv, bqkv = a["L1_ffn_W_qkv"], a["L1_ffn_b_qkv"]
            srcs = [(w_q, wqkv[:, 0:P]), (w_k, wqkv[:, P:2 * P]), (w_v, wqkv[:, 2 * P:])]
            bias = [bqkv[0:P], bqkv[P:2 * P], None, bqkv[2 * P:]]
        loads = [(d[:, :], s) for d, s in srcs]
        loads += [(cols[:, i:i + 1], bias[i].rearrange("(p o) -> p o", o=1)) for i in range(3) if bias[i] is not None]
        loads.append((bv[:, :], bias[3].rearrange("(o d) -> o d", o=1).to_broadcast([P, P])))
        for slot in range(2):
            for side in range(K_SIDES):
                for par in range(2):
                    loads.append((stack_k[64 * par + ROWS:64 * par + ROWS + STAT, slot, side, :, :],
                                  a["c_stat2" if sparse else "c_stat1"][:, side, :, :]))

        with nc.Block() as block:
            @block.sync
            def _(sp):
                for dst, src in loads:
                    sp.dma_start(dst, src).then_inc(s_load, 16)
                with sp.Fori(0, B) as b:
                    sp.wait_ge(s_split, 2 * b + 2)
                    sp.sem_inc(s_pass, 1)
                    for side, groups in ((0, SPLIT_Q), (1, SPLIT_K)):
                        for j, k in enumerate(groups):
                            sp.dma_start(scratch[b, side, :, HD1 * j:HD1 * j + HD1, :], part[:, k, side, :]).then_inc(s_wr, 16)
                    sp.wait_ge(s_wr, 2 * GROUPS * 16 * (b + 1))
                    sp.sem_inc(s_pass, 1)

                    def load(r):
                        sl = r % 2
                        for par in range(2):
                            rows = slice(64 * par, 64 * par + ROWS)
                            heads = slice(QUAD * r + par, QUAD * r + QUAD, 2)
                            sp.dma_start(stack_q[rows, sl, :, :],
                                         scratch[b, 0, heads, :, :].rearrange("h r s -> r h s")).then_inc(s_ld, 16)
                            for side in range(K_SIDES):
                                sp.dma_start(stack_k[rows, sl, side, :, :],
                                             scratch[b, 1, heads, :, :].rearrange("h r s -> r h s")).then_inc(s_ld, 16)

                    for r in range(QUADS):
                        if r == 0:
                            sp.wait_ge(s_kd, QUADS * b)
                            sp.sem_inc(s_pass, 1)
                            load(0)
                            load(1)
                        released(sp, b, ("T", r))
                        for i in range(QUAD):
                            par, p = i % 2, i // 2
                            sp.dma_start(stack_q[64 * par + ROWS:64 * par + ROWS + STAT, r % 2, p, :],
                                         statT[STAT * i:STAT * i + STAT, r % 2, :]).then_inc(s_st, 16)
                        if r + 2 < QUADS:
                            sp.wait_ge(s_kd, QUADS * b + r + 1)
                            sp.sem_inc(s_pass, 1)
                            load(r + 2)
            LD = 2 * (1 + K_SIDES) * 16

            @block.gpsimd
            def _(pool):
                pool.memset(v[:, :, :, :], 0.0).then_inc(s_one, 1)
                pool.memset(ones[:, :], 1.0).then_inc(s_one, 1)
                if sparse:
                    pool.memset(vpart[:, :, :, :], 0.0).then_inc(s_one, 1)
                    pool.sem_inc(s_w, 2)
                pool.wait_ge(s_one, 1)
                pool.memset(v[:, :, :, HD1:VW], 1.0).then_inc(s_vone, 1)
                if sparse:
                    pool.wait_ge(s_one, 3)
                    pool.memset(vpart[:, :, :, HD1:VW], 1.0).then_inc(s_vone, 1)
                with pool.Fori(0, B) as b:
                    for it in plan:
                        if it[0] == "A":
                            pool.wait_ge(s_kd, QUADS * b)
                            pool.tensor_copy(hs[:, :], m.hT[:, b, WINDOW:]).then_inc(s_hs, 1)
                        if it[0] == "K" and sparse:
                            _, r, ch = it
                            for p in range(2):
                                n = CHUNK2 * b + (r * TB + ch) * 2 + p
                                pool.wait_ge(s_exp, n + 1)
                                pool.wait_ge(s_mk, n + 1)
                                pool.tensor_tensor(w[:, ch % 2, 2 * p:2 * p + 2, :], mask[:, ch % 2, 2 * p:2 * p + 2, :],
                                                   e[:, p, :, :], ALU.mult).then_inc(s_w, 1)

            @block.tensor
            def _(pe):
                pe.wait_ge(s_load, 16 * len(loads))
                pe.wait_ge(s_one, 2)
                pe.wait_ge(s_vone, KINDS)
                pe.sem_inc(s_pv, 2)
                with pe.Fori(0, B) as b:
                    def to(u):
                        n = index[u]
                        pe.wait_ge(s_bank[n % 2], (USES // 2) * b + n // 2)
                        return bank[:, n % 2, :]

                    for it in plan:
                        if it[0] == "A":
                            pe.wait_ge(s_hs, b + 1)
                            o = to("q")
                            pe.matmul(o, w_q[:, :], hs[:, :], start=True, stop=True).then_inc(s_use, 1)
                            o = to("k")
                            pe.matmul(o, w_k[:, :], hs[:, :], start=True, stop=True).then_inc(s_use, 1)
                            o = to("v")
                            for t in range(TB):
                                if t == TB // 2 and not sparse:
                                    mm.then_inc(s_use, 1)
                                    o = to("v2")
                                mm = pe.matmul(o[:, t * P:(t + 1) * P], hs[:, t * P:(t + 1) * P], w_v[:, :],
                                               start=True, stop=True)
                            mm.then_inc(s_use, 1)
                            if sparse:
                                o = to("vs")
                                released(pe, b, "v")
                                for t in range(TB):
                                    mm = pe.matmul(o, ones[:, :], v[:, t, :, :].rearrange("p h d -> p (h d)"),
                                                   start=(t == 0), stop=(t == TB - 1))
                                mm.then_inc(s_use, 1)
                        if it[0] == "Q":
                            _, r, i = it
                            par, p, sl = i % 2, i // 2, r % 2
                            rows = slice(64 * par, 64 * par + ROWS)
                            if i == 0:
                                pe.wait_ge(s_ld, LD * (QUADS * b + (r + 1 if r else 2)))
                            for t in range(TB):
                                o = to(("S", r, i, t))
                                pe.matmul(o, stack_q[rows, sl, p, t * P:(t + 1) * P], stack_k[rows, sl, 0, p, :],
                                          start=True, stop=True).then_inc(s_use, 1)
                        if it[0] == "T":
                            r = it[1]
                            o = to(("T", r)).bitcast(BF16)
                            pe.wait_ge(s_sp, QUADS * b + r + 1)
                            for t in range(TB):
                                mm = pe.transpose(o[0:QUAD * STAT, t * P:(t + 1) * P],
                                                  stat_part[:, t, :, :, :].rearrange("p i k j -> p (i k j)"),
                                                  m.ident_b[:, :])
                            mm.then_inc(s_use, 1)
                        if it[0] == "K":
                            _, r, ch = it
                            if ch == 0:
                                pe.wait_ge(s_st, 16 * QUAD * (QUADS * b + r + 1))
                            for p in range(2):
                                n = CHUNK2 * b + (r * TB + ch) * 2 + p
                                for side, dst, freeby, s_done in ((0, h_p, s_exp, s_hp), (1, g_p, s_mk, s_gp))[:K_SIDES]:
                                    pe.wait_ge(freeby, n)
                                    for par in range(2):
                                        rows = slice(64 * par, 64 * par + ROWS + STAT)
                                        mm = pe.matmul(dst[:, par, :], stack_k[rows, r % 2, side, p, ch * P:(ch + 1) * P],
                                                       stack_q[rows, r % 2, p, :], start=True, stop=True)
                                    mm.then_inc(s_done, 1)

                            def values(ch):
                                kc = CHUNKS * b + r * TB + ch
                                if ch == 0:
                                    pe.wait_ge(s_u, QUADS * b + r)
                                if sparse:
                                    pe.wait_ge(s_w, CHUNK2 * b + (r * TB + ch) * 2 + 2 + 2)
                                else:
                                    pe.wait_ge(s_exp, CHUNK2 * b + (r * TB + ch) * 2 + 2)
                                for i in range(QUAD):
                                    rhs = w[:, ch % 2, i, :] if sparse else e[:, i // 2, i % 2, :]
                                    mm = pe.matmul(u_p[0][COL * i:COL * i + COL, :], v[:, ch, QUAD * r + i, :], rhs,
                                                   start=(ch == 0), stop=(ch == TB - 1))
                                if sparse:
                                    for i in range(QUAD):
                                        mm = pe.matmul(u_p[1][COL * i:COL * i + COL, :], vpart[:, ch, QUAD * r + i, :],
                                                       mask[:, ch % 2, i, :], start=(ch == 0), stop=(ch == TB - 1))
                                mm.then_inc(s_pv, 1)

                            if sparse:
                                if ch >= 1:
                                    values(ch - 1)
                                if ch == TB - 1:
                                    values(ch)
                            else:
                                values(ch)
                        if it[0] == "F":
                            r = it[1]
                            for k in range(KINDS):
                                o = to(("F", r, k))
                                pe.wait_ge(s_u, QUADS * b + r + 1)
                                for t in range(TB):
                                    mm = pe.transpose(o[:, t * P:(t + 1) * P], u_sb[:, k, t * P:(t + 1) * P], m.ident[:, :])
                                    if k == 0 and t == 0:
                                        mm.then_inc(s_kd, 1)
                                mm.then_inc(s_use, 1)
                        if it[0] == "Y":
                            o = to("aT")
                            pe.wait_ge(s_tok, QUADS * (b + 1))
                            for t in range(TB):
                                mm = pe.transpose(o[:, t * P:(t + 1) * P], tok[:, t, :], m.ident[:, :])
                            mm.then_inc(s_use, 1)
                            o = to("y")
                            released(pe, b, "aT")
                            pe.matmul(o, w_o[:, :], aT[:, :], start=True, stop=True).then_inc(s_use, 1)

            @block.scalar
            def _(act):
                act.wait_ge(s_load, 16 * len(loads))
                act.activation(bq[:, :], cols[:, 0:1], ACT.Copy, scale=float(HD1) ** -0.5).then_inc(s_qk, 1)
                act.wait_ge(s_qk, 1)
                with act.Fori(0, B) as b:
                    for it in plan:
                        if it[0] == "A":
                            act.wait_ge(s_split, 2 * b)
                            o = used(act, b, "q")
                            act.activation(qk[:, 0, :], o, ACT.Identity, bias=bq[:, 0:1],
                                           scale=float(HD1) ** -0.5).then_inc(freed("q"), 1)
                            o = used(act, b, "k")
                            act.activation(qk[:, 1, :], o, ACT.Identity, bias=cols[:, 1:2]).then_inc(freed("k"), 1)
                            act.wait_ge(freed("k"), (USES // 2) * b + index["k"] // 2 + 1)
                            act.wait_ge(freed("q"), (USES // 2) * b + index["q"] // 2 + 1)
                            act.wait_ge(s_wr, 2 * GROUPS * 16 * b)
                            act.activation(part[:, 0, :, :], qk[:, :, :], ACT.Copy).then_inc(s_qk, 1)
                            act.wait_ge(s_split, 2 * b + 1)
                            act.activation(part[:, 1, :, :], rest[:, :, :], ACT.Copy).then_inc(s_qk, 1)
                        if it[0] == "T":
                            r = it[1]
                            n = QUADS * b + r
                            if sparse:
                                act.wait_ge(s_sp, n + 1)
                                act.activation(floor[:, r % 2, :, :], stat[:, r % 2, :, :, 1], ACT.Exp).then_inc(s_fl, 1)
                            o = used(act, b, ("T", r)).bitcast(BF16)
                            act.activation(statT[:, r % 2, :], o[0:QUAD * STAT, 0:S], ACT.Copy).then_inc(freed(("T", r)), 1)
                        if it[0] == "K":
                            _, r, ch = it
                            for p in range(2):
                                n = CHUNK2 * b + (r * TB + ch) * 2 + p
                                act.wait_ge(s_hp, n + 1)
                                if sparse:
                                    act.wait_ge(s_w, n + 1)
                                else:
                                    act.wait_ge(s_pv, CHUNKS * b + r * TB + ch + 2)
                                act.activation(e[:, p, :, :], h_p[:, :, :], ACT.Exp).then_inc(s_exp, 1)
                        if it[0] == "F":
                            r = it[1]
                            act.wait_ge(s_pv, CHUNKS * b + r * TB + TB + 2)
                            for k in range(KINDS):
                                ins = act.activation(u_sb[:, k, :], u_p[k][:, :], ACT.Copy)
                            ins.then_inc(s_u, 1)
                        if it[0] == "Y":
                            o = used(act, b, "aT")
                            act.activation(aT[:, :], o, ACT.Copy).then_inc(freed("aT"), 1)

            @block.vector
            def _(dve):
                dve.wait_ge(s_load, 16 * len(loads))
                dve.wait_ge(s_one, 2 + sparse)
                dve.wait_ge(s_vone, KINDS)

                def settled():
                    dve.sem_inc(s_rel, 1)

                with dve.Fori(0, B) as b:
                    count = {s_top: 0, s_sg: 0, s_fin: 0}
                    per = {s_top: HEADS * TB // 2 * 28 if sparse else HEADS * TB, s_sg: 3 * QUADS,
                           s_fin: (5 if sparse else 1) * QUADS}

                    def did(ins, s_):
                        count[s_] += 1
                        ins.then_inc(s_, 1)

                    def wait_own(s_, back=0):
                        dve.wait_ge(s_, per[s_] * b + count[s_] - back)

                    for it in plan:
                        if it[0] == "A":
                            dve.wait_ge(s_qk, 2 * b + 2)
                            dve.tensor_tensor(rest[:, :, :], qk[:, :, :], part[:, 0, :, :], ALU.subtract).then_inc(s_split, 1)
                            dve.wait_ge(s_qk, 2 * b + 3)
                            dve.wait_ge(s_split, 2 * b + 1)
                            dve.tensor_tensor(part[:, 2, :, :], rest[:, :, :], part[:, 1, :, :], ALU.subtract).then_inc(s_split, 1)
                            vh = v[:, :, :, 0:HD1]
                            bvb = bv[:, :].unsqueeze(1).to_broadcast([P, TB, P])
                            if not sparse:
                                for k, u in enumerate(("v", "v2")):
                                    half = slice(k * TB // 2, (k + 1) * TB // 2)
                                    o = used(dve, b, u)
                                    dve.tensor_tensor(vh[:, half], o[:, half.start * P:half.stop * P].rearrange("p (t h d) -> p t h d", t=TB // 2, d=HD1),
                                                      bvb[:, half].rearrange("p t (h d) -> p t h d", d=HD1), ALU.add).then_inc(freed(u), 1)
                            else:
                                o = used(dve, b, "v")
                                dve.tensor_tensor(vh, o.rearrange("p (t h d) -> p t h d", t=TB, d=HD1),
                                                  bvb.rearrange("p t (h d) -> p t h d", d=HD1), ALU.add).then_inc(freed("v"), 1)
                                released(dve, b, "v")
                                vp = [vpart[:, :, :, VW * k:VW * k + HD1] for k in range(3)]
                                vr = [vrest[:, k, :, :].rearrange("p t (h d) -> p t h d", d=HD1) for k in range(2)]
                                dve.tensor_copy(vp[0], vh).then_inc(s_v, 1)
                                dve.wait_ge(s_v, 4 * b + 1)
                                dve.tensor_tensor(vr[0], vh, vp[0], ALU.subtract).then_inc(s_v, 1)
                                dve.wait_ge(s_v, 4 * b + 2)
                                dve.tensor_copy(vp[1], vr[0]).then_inc(s_v, 1)
                                dve.wait_ge(s_v, 4 * b + 3)
                                dve.tensor_tensor(vp[2], vr[0], vp[1], ALU.subtract).then_inc(s_v, 1)
                                o = used(dve, b, "vs")
                                dve.tensor_copy(sumv[:, :, :].rearrange("p h d -> p (h d)"), o).then_inc(freed("vs"), 1)
                        if it[0] == "Q" and not sparse:
                            _, r, i = it
                            for t in range(TB):
                                o = used(dve, b, ("S", r, i, t))
                                dve.tensor_reduce(stat[:, r % 2, t, i, :], o, AX.X, ALU.max, negate=True).then_inc(freed(("S", r, i, t)), 1)
                        if it[0] == "Q" and sparse:
                            _, r, i = it
                            for t0 in range(0, TB, 2):
                                tiles = [used(dve, b, ("S", r, i, t0 + u)) for u in range(2)]
                                for k in range(7):
                                    if k == 0:
                                        wait_own(s_top)
                                    if k:
                                        if k == 1:
                                            for u in range(2):
                                                released(dve, b, ("S", r, i, t0 + u))
                                        else:
                                            wait_own(s_top)
                                    settled()
                                    for u in range(2):
                                        did(dve.max(m8[:, u, k, :], work[:, u, :] if k else tiles[u]), s_top)
                                    if k == 6:
                                        break
                                    wait_own(s_top)
                                    settled()
                                    for u in range(2):
                                        ins = dve.match_replace(work[:, u, :], m8[:, u, k, :], work[:, u, :] if k else tiles[u], LOW)
                                        if k:
                                            did(ins, s_top)
                                        else:
                                            ins.then_inc(freed(("S", r, i, t0 + u)), 1)
                                wait_own(s_top)
                                last = KEEP - 1 - 48
                                for u in range(2):
                                    st = stat[:, r % 2, t0 + u, i, :]
                                    did(dve.tensor_scalar(st[:, 0:1], m8[:, u, 6, last:last + 1], m8[:, u, 6, last + 1:last + 2],
                                                          -0.5, ALU.add, ALU.mult), s_top)
                                    did(dve.tensor_scalar(st[:, 1:2], m8[:, u, 0, 0:1], 0.0, -1.0, ALU.max, ALU.mult), s_top)
                        if it[0] == "T":
                            r = it[1]
                            if sparse:
                                wait_own(s_top)
                            else:
                                released(dve, b, ("S", r, QUAD - 1, TB - 1))
                                released(dve, b, ("S", r, QUAD - 1, TB - 2))
                            if r:
                                used(dve, b, ("T", r - 1))
                            st, sr = stat[:, r % 2, :, :, :], stat_rest[:, :, :, :]
                            pt = [stat_part[:, :, :, :, k] for k in range(3)]
                            did(dve.tensor_copy(pt[0], st), s_sg)
                            wait_own(s_sg)
                            did(dve.tensor_tensor(sr, st, pt[0], ALU.subtract), s_sg)
                            wait_own(s_sg)
                            did(dve.tensor_copy(pt[1], sr), s_sg)
                            wait_own(s_sg)
                            dve.tensor_tensor(pt[2], sr, pt[1], ALU.subtract).then_inc(s_sp, 1)
                        if it[0] == "K" and sparse:
                            _, r, ch = it
                            for p in range(2):
                                n = CHUNK2 * b + (r * TB + ch) * 2 + p
                                dve.wait_ge(s_gp, n + 1)
                                dve.wait_ge(s_pv, CHUNKS * b + r * TB + ch + 1)
                                dve.tensor_scalar(mask[:, ch % 2, 2 * p:2 * p + 2, :], g_p[:, :, :], 0.0, None,
                                                  ALU.is_ge).then_inc(s_mk, 1)
                        if it[0] == "F":
                            r = it[1]
                            uT = used(dve, b, ("F", r, 0)).rearrange("p (t i c) -> p t i c", t=TB, i=QUAD)
                            if not sparse:
                                if r:
                                    released(dve, b, ("F", r - 1, 0))
                                did(dve.reciprocal(zr[:, :, :, :], uT[:, :, :, HD1:VW]), s_fin)
                                wait_own(s_fin)
                                dst = m.attn[:, b, :, QUAD * r * HD1:QUAD * (r + 1) * HD1].rearrange("p t (i d) -> p t i d", d=HD1)
                                dve.tensor_tensor(dst, uT[:, :, :, 0:HD1], zr[:, :, :, :].to_broadcast([P, TB, QUAD, HD1]),
                                                  ALU.mult).then_inc(freed(("F", r, 0)), 1)
                                if r == QUADS - 1:
                                    released(dve, b, ("F", r, 0))
                            else:
                                mT = used(dve, b, ("F", r, 1)).rearrange("p (t i c) -> p t i c", t=TB, i=QUAD)
                                did(dve.tensor_copy(tot[:, :, :, :], mT[:, :, :, 0:VW]), s_fin)
                                wait_own(s_fin)
                                did(dve.tensor_tensor(tot2[:, :, :, :], mT[:, :, :, VW:2 * VW], tot[:, :, :, :], ALU.add), s_fin)
                                wait_own(s_fin)
                                dve.tensor_tensor(tot[:, :, :, :], mT[:, :, :, 2 * VW:3 * VW], tot2[:, :, :, :],
                                                  ALU.add).then_inc(freed(("F", r, 1)), 1)
                                released(dve, b, ("F", r, 1))
                                sv = sumv[:, QUAD * r:QUAD * (r + 1), 0:VW].unsqueeze(1).to_broadcast([P, TB, QUAD, VW])
                                did(dve.tensor_tensor(tot2[:, :, :, :], sv, tot[:, :, :, :], ALU.subtract), s_fin)
                                wait_own(s_fin)
                                dve.wait_ge(s_fl, QUADS * b + r + 1)
                                fl = floor[:, r % 2, :, :].unsqueeze(3).to_broadcast([P, TB, QUAD, VW])
                                did(dve.tensor_tensor(tot[:, :, :, :], tot2[:, :, :, :], fl, ALU.mult), s_fin)
                                wait_own(s_fin)
                                dve.tensor_tensor(tot2[:, :, :, :], uT[:, :, :, 0:VW], tot[:, :, :, :],
                                                  ALU.add).then_inc(freed(("F", r, 0)), 1)
                                released(dve, b, ("F", r, 0))
                                did(dve.reciprocal(zr[:, :, :, :], tot2[:, :, :, HD1:VW]), s_fin)
                                wait_own(s_fin)
                                dst = tok[:, :, QUAD * r * HD1:QUAD * (r + 1) * HD1].rearrange("p t (i d) -> p t i d", d=HD1)
                                dve.tensor_tensor(dst, tot2[:, :, :, 0:HD1], zr[:, :, :, :].to_broadcast([P, TB, QUAD, HD1]),
                                                  ALU.mult).then_inc(s_tok, 1)
                        if it[0] == "Y":
                            o = used(dve, b, "y")
                            dve.tensor_scalar(y[:, :], o, cols[:, 2:3], m.mod[:, 1, GATE, bass.ds(b, 1)], ALU.add,
                                              ALU.mult).then_inc(freed("y"), 1)
                            released(dve, b, "y")
                            dve.tensor_tensor(m.xT[:, b, :], m.xT[:, b, :], y[:, :], ALU.add)
                assert all(count[s_] == per[s_] for s_ in (s_sg, s_fin) + ((s_top,) if sparse else ()))


def wait(eng, sem, value):
    if not (isinstance(value, int) and value <= 0):
        eng.wait_ge(sem, value)


def project_sparse(nc, m, a):
    with ExitStack() as c:
        sb = lambda n, s, d=F32: c.enter_context(nc.sbuf_tensor("pj_" + n, s, d))
        pb = lambda n: c.enter_context(nc.psum_tensor("pj_" + n, [P, S], F32))
        sem = lambda n: nc.alloc_semaphore("pj_" + n)
        hs = sb("hs", [P, 2, S])
        w_q, w_k, w_v = (sb(n, [P, P]) for n in ("w_q", "w_k", "w_v"))
        cols = sb("cols", [P, 2])
        bq = sb("bq", [P, 1])
        bv = sb("bv", [P, P])
        ones = sb("ones", [P, P])
        block = sb("block", [P, P])
        heads = sb("heads", [P, HEADS])
        qkc = sb("qkc", [P, 2, 3, S])
        ksum = sb("ksum", [P, 2, 1])
        kbar = sb("kbar", [P, 2, 1])
        kbar_h = sb("kbar_h", [P, 2, HEADS])
        rest = sb("rest", [P, 2, 3, S])
        part = sb("part", [P, 2, 3, 3, S], BF16)
        v = sb("v", [P, 2, QUADS, TB, QUAD, COL])
        vrest = sb("vrest", [P, 2, 2, QUADS, TB, QUAD, HD1])
        vpart = sb("vpart", [P, 2, QUADS, TB, QUAD, COL], BF16)
        kT = sb("kT", [P, 2, TB, P])
        cov = sb("cov", [P, 2, P])
        z = sb("z", [P, 2, S])
        q_p, k_p, v_p, vs_p, kt_p, cov_p, y_p, st_p = (pb(n) for n in ("q_p", "k_p", "v_p", "vs_p", "kt_p", "cov_p", "y_p", "st_p"))
        names = ("load", "zero", "ones", "bq", "hs", "pq", "pk", "pv", "q", "k", "kbar", "kc", "p0", "rest", "p1", "p2", "wr0", "wr1",
                 "v", "vp", "vw0", "vw1", "vs", "sv", "kt", "kts", "cov", "covs", "y", "z", "st", "mean", "var", "sd", "kh", "split", "pass")
        (s_load, s_zero, s_ones, s_bq, s_hs, s_pq, s_pk, s_pv, s_q, s_k, s_kbar, s_kc, s_p0, s_rest, s_p1, s_p2, s_wr0, s_wr1,
         s_v, s_vp, s_vw0, s_vw1, s_vs, s_sv, s_kt, s_kts, s_cov, s_covs, s_y, s_z, s_st, s_mean, s_var, s_sd, s_kh, s_split,
         s_pass) = map(sem, names)
        s_wr, s_vw = (s_wr0, s_wr1), (s_vw0, s_vw1)
        WR = 3 * GROUPS * 16
        loads = [(w_q[:, :], a["L1_attn_Wq"]), (w_k[:, :], a["L1_attn_Wk"]), (w_v[:, :], a["L1_attn_Wv"]),
                 (cols[:, 0:1], a["L1_attn_bq"].rearrange("(p o) -> p o", o=1)),
                 (cols[:, 1:2], a["L1_attn_bk"].rearrange("(p o) -> p o", o=1)),
                 (bv[:, :], a["L1_attn_bv"].rearrange("(o d) -> o d", o=1).to_broadcast([P, P])),
                 (block[:, :], a["c_block"]), (heads[:, :], a["c_heads"])]

        def batches(eng, emit):
            for j in range(2):
                emit(j, j, 0)
            with eng.Fori(1, B // 2) as i:
                for j in range(2):
                    emit(2 * i + j, j, i)

        with nc.Block() as blk:
            @blk.sync
            def _(sp):
                for dst, src in loads:
                    sp.dma_start(dst, src).then_inc(s_load, 16)

                def emit(b, j, pair):
                    wait(sp, s_p2, b + 1)
                    sp.sem_inc(s_pass, 1)
                    for kind, groups in ((0, SPLIT_Q), (1, SPLIT_K), (2, SPLIT_K)):
                        for n, k in enumerate(groups):
                            sp.dma_start(m.parts[b, kind, :, HD1 * n:HD1 * n + HD1, :], part[:, j, k, kind, :]).then_inc(s_wr[j], 16)
                    wait(sp, s_vp, b + 1)
                    sp.sem_inc(s_pass, 1)
                    sp.dma_start(m.v_store[b].rearrange("q p n -> p q n"),
                                 v[:, j, :, :, :, :].rearrange("p q t i c -> p q (t i c)")).then_inc(s_vw[j], 16)
                    sp.dma_start(m.vp_store[b].rearrange("q p n -> p q n"),
                                 vpart[:, j, :, :, :, :].rearrange("p q t i c -> p q (t i c)")).then_inc(s_vw[j], 16)

                batches(sp, emit)
                for j in range(2):
                    sp.wait_ge(s_wr[j], WR * B // 2)
                    sp.wait_ge(s_vw[j], 32 * B // 2)

            @blk.gpsimd
            def _(pool):
                pool.memset(v[:, :, :, :, :, :], 0.0).then_inc(s_zero, 1)
                pool.memset(vpart[:, :, :, :, :, :], 0.0).then_inc(s_zero, 1)
                pool.memset(ones[:, :], 1.0).then_inc(s_ones, 1)
                pool.wait_ge(s_zero, 2)
                pool.memset(v[:, :, :, :, :, HD1:VW], 1.0).then_inc(s_ones, 1)
                pool.memset(vpart[:, :, :, :, :, HD1:VW], 1.0).then_inc(s_ones, 1)

                def emit(b, j, pair):
                    wait(pool, s_pv, b - 1)
                    pool.sem_inc(s_pass, 1)
                    pool.tensor_copy(hs[:, j, :], m.hT[:, b, WINDOW:]).then_inc(s_hs, 1)

                batches(pool, emit)

            @blk.tensor
            def _(pe):
                pe.wait_ge(s_load, 16 * len(loads))
                pe.wait_ge(s_ones, 3)

                def emit(b, j, pair):
                    wait(pe, s_hs, b + 1)
                    wait(pe, s_q, b)
                    pe.matmul(q_p[:, :], w_q[:, :], hs[:, j, :], start=True, stop=True).then_inc(s_pq, 1)
                    wait(pe, s_k, b)
                    pe.matmul(k_p[:, :], w_k[:, :], hs[:, j, :], start=True, stop=True).then_inc(s_pk, 1)
                    wait(pe, s_v, b)
                    for t in range(TB):
                        mm = pe.matmul(v_p[:, t * P:(t + 1) * P], hs[:, j, t * P:(t + 1) * P], w_v[:, :], start=True, stop=True)
                    mm.then_inc(s_pv, 1)
                    wait(pe, s_kc, b + 1)
                    wait(pe, s_kts, b)
                    for t in range(TB):
                        mm = pe.transpose(kt_p[:, t * P:(t + 1) * P], qkc[:, j, 2, t * P:(t + 1) * P], m.ident[:, :])
                    mm.then_inc(s_kt, 1)
                    wait(pe, s_v, b + 1)
                    wait(pe, s_sv, b)
                    for t in range(TB):
                        mm = pe.matmul(vs_p[:, :], ones[:, :], v[:, j, :, t, :, :], start=(t == 0), stop=(t == TB - 1))
                    mm.then_inc(s_vs, 1)
                    wait(pe, s_kts, b + 1)
                    wait(pe, s_covs, b)
                    for t in range(TB):
                        mm = pe.matmul(cov_p[:, 0:P], kT[:, j, t, :], kT[:, j, t, :], start=(t == 0), stop=(t == TB - 1))
                    mm.then_inc(s_cov, 1)
                    wait(pe, s_covs, b + 1)
                    wait(pe, s_z, b)
                    pe.matmul(y_p[:, :], cov[:, j, :], qkc[:, j, 0, :], start=True, stop=True).then_inc(s_y, 1)
                    wait(pe, s_z, b + 1)
                    wait(pe, s_kh, b + 1)
                    wait(pe, s_mean, b)
                    wait(pe, s_var, b)
                    for t in range(TB):
                        at = slice(t * P, (t + 1) * P)
                        pe.matmul(st_p[:, t * HEADS:(t + 1) * HEADS], z[:, j, at], heads[:, :], start=True, stop=True)
                        mm = pe.matmul(st_p[:, (TB + t) * HEADS:(TB + t + 1) * HEADS], qkc[:, j, 0, at], kbar_h[:, j, :],
                                       start=True, stop=True)
                    mm.then_inc(s_st, 1)

                batches(pe, emit)

            @blk.scalar
            def _(act):
                act.wait_ge(s_load, 16 * len(loads))
                act.activation(bq[:, :], cols[:, 0:1], ACT.Copy, scale=float(HD1) ** -0.5).then_inc(s_bq, 1)
                act.wait_ge(s_bq, 1)

                def emit(b, j, pair):
                    wait(act, s_pq, b + 1)
                    wait(act, s_st, b - 1)
                    wait(act, s_rest, b - 1)
                    act.activation(qkc[:, j, 0, :], q_p[:, :], ACT.Identity, bias=bq[:, 0:1],
                                   scale=float(HD1) ** -0.5).then_inc(s_q, 1)
                    wait(act, s_pk, b + 1)
                    act.activation(qkc[:, j, 1, :], k_p[:, :], ACT.Identity, bias=cols[:, 1:2],
                                   accum_out=ksum[:, j, :]).then_inc(s_k, 1)
                    wait(act, s_kc, b + 1)
                    wait(act, s_q, b + 1)
                    wait(act, s_k, b + 1)
                    wait(act, s_wr[j], WR * pair)
                    act.activation(part[:, j, 0, :, :], qkc[:, j, :, :], ACT.Copy).then_inc(s_p0, 1)
                    wait(act, s_kt, b + 1)
                    wait(act, s_cov, b - 1)
                    act.activation(kT[:, j, :, :], kt_p[:, :].rearrange("p (t d) -> p t d", t=TB), ACT.Copy).then_inc(s_kts, 1)
                    wait(act, s_rest, b + 1)
                    act.activation(part[:, j, 1, :, :], rest[:, j, :, :], ACT.Copy).then_inc(s_p1, 1)
                    wait(act, s_st, b + 1)
                    wait(act, s_var, b + 1)
                    act.activation(m.mean[:, b, :].rearrange("p (h t) -> p t h", t=TB),
                                   st_p[:, TB * HEADS:2 * TB * HEADS].rearrange("p (t h) -> p t h", t=TB),
                                   ACT.Copy).then_inc(s_mean, 1)

                batches(act, emit)
                act.wait_ge(s_var, B)
                act.activation(m.sd[:, :, :], m.sd[:, :, :], ACT.Sqrt).then_inc(s_sd, 1)

            @blk.vector
            def _(dve):
                dve.wait_ge(s_load, 16 * len(loads))
                dve.wait_ge(s_ones, 3)

                def emit(b, j, pair):
                    wait(dve, s_k, b + 1)
                    wait(dve, s_kh, b - 1)
                    dve.tensor_scalar(kbar[:, j, :], ksum[:, j, :], 1.0 / S, None, ALU.mult).then_inc(s_kbar, 1)
                    wait(dve, s_kbar, b + 1)
                    wait(dve, s_cov, b - 1)
                    dve.tensor_scalar(qkc[:, j, 2, :], qkc[:, j, 1, :], kbar[:, j, 0:1], None, ALU.subtract).then_inc(s_kc, 1)
                    wait(dve, s_st, b - 1)
                    dve.tensor_scalar(kbar_h[:, j, :], heads[:, :], kbar[:, j, 0:1], None, ALU.mult).then_inc(s_kh, 1)
                    wait(dve, s_pv, b + 1)
                    wait(dve, s_vw[j], 32 * pair)
                    for r in range(QUADS):
                        ins = dve.tensor_tensor(v[:, j, r, :, :, 0:HD1],
                                                v_p[:, :].rearrange("p (t q i d) -> p q t i d", t=TB, q=QUADS, i=QUAD)[:, r],
                                                bv[:, r * COL:(r + 1) * COL].rearrange("p (i d) -> p i d", i=QUAD).unsqueeze(1)
                                                .to_broadcast([P, TB, QUAD, HD1]), ALU.add)
                    ins.then_inc(s_v, 1)
                    wait(dve, s_p0, b + 1)
                    dve.tensor_tensor(rest[:, j, :, :], qkc[:, j, :, :], part[:, j, 0, :, :], ALU.subtract).then_inc(s_rest, 1)
                    wait(dve, s_cov, b + 1)
                    wait(dve, s_y, b - 1)
                    dve.tensor_tensor(cov[:, j, :], cov_p[:, 0:P], block[:, :], ALU.mult).then_inc(s_covs, 1)
                    wait(dve, s_v, b + 1)
                    flat = lambda x: x.rearrange("p q t i d -> p (q t i) d")
                    vh = flat(v[:, j, :, :, :, :])[:, :, 0:HD1]
                    vp = [flat(vpart[:, j, :, :, :, :])[:, :, VW * k:VW * k + HD1] for k in range(3)]
                    vr = [flat(vrest[:, j, k, :, :, :, :]) for k in range(1)]
                    dve.tensor_copy(vp[0], vh).then_inc(s_split, 1)
                    wait(dve, s_split, 3 * b + 1)
                    dve.tensor_tensor(vr[0], vh, vp[0], ALU.subtract).then_inc(s_split, 1)
                    wait(dve, s_split, 3 * b + 2)
                    dve.tensor_copy(vp[1], vr[0]).then_inc(s_split, 1)
                    wait(dve, s_split, 3 * b + 3)
                    dve.tensor_tensor(vp[2], vr[0], vp[1], ALU.subtract).then_inc(s_vp, 1)
                    wait(dve, s_y, b + 1)
                    wait(dve, s_st, b - 1)
                    dve.tensor_tensor(z[:, j, :], y_p[:, :], qkc[:, j, 0, :], ALU.mult).then_inc(s_z, 1)
                    wait(dve, s_p1, b + 1)
                    dve.tensor_tensor(part[:, j, 2, :, :], rest[:, j, :, :], part[:, j, 1, :, :], ALU.subtract).then_inc(s_p2, 1)
                    wait(dve, s_vs, b + 1)
                    dve.tensor_copy(m.sumv[:, b, :, :], vs_p[:, :].rearrange("p (h c) -> p h c", c=COL)[:, :, 0:VW]).then_inc(s_sv, 1)
                    wait(dve, s_st, b + 1)
                    dve.tensor_scalar(m.sd[:, b, :].rearrange("p (h t) -> p t h", t=TB),
                                      st_p[:, 0:TB * HEADS].rearrange("p (t h) -> p t h", t=TB), 0.0, None,
                                      ALU.max).then_inc(s_var, 1)

                batches(dve, emit)


SLOTS = 16
TILES = QUAD * TB
ROUNDS = 4
Z0 = 1.33
AIM = KEEP - 3.5
GAINS = (0.85, 0.5, 0.3)
SLOPE = 1.0 / (S * 0.3989423 * 2.718281828 ** (-Z0 * Z0 / 2))
ROUNDER = 12582912.0
FINALS = (0, 1, 1, 2, 1, 1, 2, 1, 1, 2, 1, 1, 2, 0, 0, 0)


def search_attention(nc, m, a):
    with ExitStack() as c:
        sb = lambda n, s, d=F32: c.enter_context(nc.sbuf_tensor("se_" + n, s, d))
        pb = lambda n, s: c.enter_context(nc.psum_tensor("se_" + n, s, F32))
        sem = lambda n: nc.alloc_semaphore("se_" + n)
        STAT = 6
        VALUES, SIDE_EXP, SIDE_MASK = TB * QUAD * COL, 0, 1
        stack_q = sb("stack_q", [P, 4, 2, S], BF16)
        stack_k = sb("stack_k", [P, 4, 2, 2, S], BF16)
        vq = sb("vq", [P, 2, TB, QUAD, COL])
        vpq = sb("vpq", [P, 2, TB, QUAD, COL], BF16)
        nt = sb("nt", [P, 2, TILES])
        sd = sb("sd", [P, 2, TILES])
        cs = sb("cs", [P, 2, ROUNDS, TILES])
        err = sb("err", [P, TILES])
        sq = sb("sq", [P, TILES])
        far = sb("far", [P, TILES])
        move = sb("move", [P, TILES])
        count = sb("count", [P, 2, TILES])
        fail = sb("fail", [P, 2, TILES])
        low = sb("low", [P, TILES])
        junk = sb("junk", [P, 2, S], BF16)
        one = sb("one", [P, 1])
        flags = sb("flags", [1, 1 + TILES], mybir.dt.int32)
        ranks = sb("ranks", [P, 1 + 8])
        score = sb("score", [P, 2, S])
        work = sb("work", [P, 2, S])
        ext = sb("ext", [P, 2, TILES, 1 + 8])
        top = sb("top", [P, 7, 8])
        rmax = sb("rmax", [P, TILES])
        pick = sb("pick", [P, 3, TILES, 1 + 8])
        thr = sb("thr", [P, TILES])
        largest = sb("largest", [P, TILES])
        stat = sb("stat", [P, 2, TB, QUAD, 2])
        stat_rest = sb("stat_rest", [P, TB, QUAD, 2])
        stat_part = sb("stat_part", [P, TB, QUAD, 2, 3], BF16)
        statT = sb("statT", [QUAD * STAT, 2, S], BF16)
        floor = sb("floor", [P, 2, TB, QUAD])
        e = sb("e", [P, QUAD, S])
        mask = sb("mask", [P, 2, QUAD, S], BF16)
        w = sb("w", [P, 2, QUAD, S])
        u_sb = sb("u_sb", [P, 2, S])
        tot = sb("tot", [P, TB, QUAD, VW])
        tot2 = sb("tot2", [P, TB, QUAD, VW])
        zr = sb("zr", [P, TB, QUAD, 1])
        cb = pb("cb", [P, 2, S])
        db = pb("db", [P, 2, S])
        h_p = pb("h_p", [P, S])
        g_p = pb("g_p", [P, S])
        u_p = [pb(f"u_p{i}", [P, S]) for i in range(2)]
        (s_load, s_init, s_ld0, s_ld1, s_vld0, s_vld1, s_st0, s_st1, s_cu, s_cf0, s_cf1, s_nt, s_po, s_cfin, s_du, s_df0, s_df1, s_flag, s_fin, s_top,
         s_sel, s_sp, s_fl, s_hp, s_gp, s_exp, s_mk, s_w, s_pv, s_u, s_f, s_tok, s_pass, s_pass2, s_pass3, s_split2) = map(sem, (
             "load", "init", "ld0", "ld1", "vld0", "vld1", "st0", "st1", "cu", "cf0", "cf1", "nt", "po", "cfin", "du", "df0", "df1", "flag", "fin", "top",
             "sel", "sp", "fl", "hp", "gp", "exp", "mk", "w", "pv", "u", "f", "tok", "pass", "pass2", "pass3", "split"))
        s_ld, s_vld, s_st = (s_ld0, s_ld1), (s_vld0, s_vld1), (s_st0, s_st1)
        s_cf, s_df = (s_cf0, s_cf1), (s_df0, s_df1)
        LD = 6 * 16
        TOPS = 7 + 6 + 4
        N = B * QUADS

        order = ["flag"] + [("D", j) for j in range(TILES)] + ["F0", "F1", "T"]

        def use(g, u):
            n = order.index(u)
            if isinstance(g, int) and g <= 2:
                return (len(order) - 2) * (g - 1) + (n - 2 if u == "T" else n)
            if isinstance(g, int) and g > N:
                return 2 * (len(order) - 2) + len(order) * (N - 2) + 2 * (g - N - 1) + n - order.index("F0")
            return 2 * (len(order) - 2) + len(order) * (g - 3) + n

        def half(g, u):
            n = order.index(u)
            if isinstance(g, int):
                return use(g, u) // 2, use(g, u) % 2
            return len(order) - 2 + len(order) // 2 * (g - 3) + n // 2, n % 2

        def to(pe, g, u):
            before, k = half(g, u)
            wait(pe, s_df[k], before)
            return db[:, k, :]

        def used(eng, g, u):
            wait(eng, s_du, use(g, u) + 1)
            return db[:, half(g, u)[1], :]

        def freed(g, u):
            return s_df[half(g, u)[1]]

        def released(eng, g, u):
            before, k = half(g, u)
            wait(eng, s_df[k], before + 1)

        counts = lambda g: not isinstance(g, int) or g < N
        finals = lambda g: not isinstance(g, int) or 1 <= g <= N
        keys = lambda g: not isinstance(g, int) or 2 <= g <= N + 1
        ends = lambda g: not isinstance(g, int) or g >= 3

        def steps(eng, emit, looped=B):
            for g in range(QUADS):
                emit(g, g, lambda back, g=g: (g - back) // QUADS)
            with eng.Fori(1, looped) as b:
                for r in range(QUADS):
                    emit(QUADS * b + r, r, lambda back, r=r: b + (r - back) // QUADS)
            for g in range(QUADS * looped, N + 3):
                emit(g, g % QUADS, lambda back, g=g: (g - back) // QUADS)

        def alike(r, batch, back):
            return QUADS // 2 * batch(0) + (r - back) // 2

        def rows_of(i, more=0):
            return slice(64 * (i % 2), 64 * (i % 2) + ROWS + more)

        with nc.Block() as blk:
            @blk.sync
            def _(sp):
                for slot in range(4):
                    for side in range(2):
                        for par in range(2):
                            sp.dma_start(stack_k[64 * par + ROWS:64 * par + ROWS + STAT, slot, side, :, :],
                                         a["c_stat2"][:, side, :, :]).then_inc(s_load, 16)
                sp.dma_start(ranks[:, :], a["c_ranks"]).then_inc(s_load, 16)

                def stacks(b, r):
                    s_ld_ = s_ld[r % 2]
                    for par in range(2):
                        heads = slice(QUAD * r + par, QUAD * r + QUAD, 2)
                        rows = slice(64 * par, 64 * par + ROWS)
                        sp.dma_start(stack_q[rows, r, :, :], m.parts[b, 0, heads, :, :].rearrange("h r s -> r h s")).then_inc(s_ld_, 16)
                        for side in range(2):
                            sp.dma_start(stack_k[rows, r, side, :, :],
                                         m.parts[b, 1 + side, heads, :, :].rearrange("h r s -> r h s")).then_inc(s_ld_, 16)

                stacks(0, 0)

                def emit(g, r, batch):
                    odd = (r - 1) % 2
                    if not isinstance(g, int) or g + 1 < N:
                        wait(sp, s_hp, TILES * (g - 2))
                        wait(sp, s_gp, TILES * (g - 2))
                        wait(sp, s_cu, 64 * (g - 1) + 1)
                        sp.sem_inc(s_pass3, 1)
                        stacks(batch(-1), (r + 1) % QUADS)
                    if finals(g):
                        wait(sp, s_pv, TB * (g - 2))
                        sp.sem_inc(s_pass3, 1)
                        q = (r - 1) % QUADS
                        sp.dma_start(vq[:, (r - 1) % 2, :, :, :].rearrange("p t i c -> p (t i c)"), m.v_store[batch(1), q]).then_inc(s_vld[odd], 16)
                        sp.dma_start(vpq[:, (r - 1) % 2, :, :, :].rearrange("p t i c -> p (t i c)"), m.vp_store[batch(1), q]).then_inc(s_vld[odd], 16)
                        released(sp, g, "T")
                        for i in range(QUAD):
                            sp.dma_start(stack_q[64 * (i % 2) + ROWS:64 * (i % 2) + ROWS + STAT, q, i // 2, :],
                                         statT[STAT * i:STAT * i + STAT, (r - 1) % 2, :]).then_inc(s_st[odd], 16)

                steps(sp, emit, B - 1)

            @blk.gpsimd
            def _(pool):
                pool.memset(one[:, :], 1.0).then_inc(s_init, 1)
                def emit(g, r, batch):
                    n = [0]
                    base = 38 * g + 1
                    par = r % 2

                    def did(ins, s_=None):
                        if s_ is None:
                            n[0] += 1
                            ins.then_inc(s_po, 1)
                        else:
                            ins.then_inc(s_, 1)

                    def wait_own():
                        wait(pool, s_po, base + n[0])
                        pool.sem_inc(s_pass, 1)

                    for s in range(SLOTS):
                        if counts(g) and s and s % 2 == 0 and s // 2 - 1 < 2 * (ROUNDS - 1):
                            block = s // 2 - 1
                            rnd, group = block // 2, block % 2
                            at = slice(8 * group, 8 * group + 8)
                            wait(pool, s_cf0, 32 * g + 4 * (block + 1))
                            wait(pool, s_cf1, 32 * g + 4 * (block + 1))
                            wait(pool, s_po, base + n[0])
                            pool.sem_inc(s_pass, 1)
                            did(pool.tensor_scalar(err[:, at], cs[:, par, rnd, at], 0.5, S / 2 - AIM, ALU.mult, ALU.add))
                            wait_own()
                            did(pool.tensor_tensor(sq[:, at], err[:, at], err[:, at], ALU.mult))
                            did(pool.tensor_tensor(move[:, at], err[:, at], sd[:, par, at], ALU.mult))
                            wait_own()
                            did(pool.tensor_scalar(far[:, at], sq[:, at], 12.96, -SLOPE * GAINS[rnd], ALU.is_gt, ALU.mult))
                            wait_own()
                            did(pool.tensor_tensor(err[:, at], move[:, at], far[:, at], ALU.mult))
                            wait_own()
                            did(pool.tensor_tensor(nt[:, par, at], nt[:, par, at], err[:, at], ALU.add), s_nt)
                        if keys(g) and s % 2 == 1:
                            ch, p = s // 4, s % 4 // 2
                            wait(pool, s_exp, TILES * (g - 2) + s + 1)
                            wait(pool, s_mk, TILES * (g - 2) + s + 1)
                            wait(pool, s_pv, TB * (g - 2) + ch - 1)
                            pool.tensor_tensor(w[:, ch % 2, 2 * p:2 * p + 2, :], mask[:, ch % 2, 2 * p:2 * p + 2, :],
                                               e[:, 2 * p:2 * p + 2, :], ALU.mult).then_inc(s_w, 1)
                        if s == 14 and (not isinstance(g, int) or g + 1 < N):
                            wait(pool, s_sp, g)
                            wait(pool, s_nt, 7 * g + 7)
                            nr = (r + 1) % QUADS
                            pool.sem_inc(s_pass, 1)
                            did(pool.tensor_copy(sd[:, 1 - par, :], m.sd[:, batch(-1), nr * TILES:(nr + 1) * TILES]))
                            wait_own()
                            did(pool.tensor_scalar(nt[:, 1 - par, :], sd[:, 1 - par, :], -Z0, None, ALU.mult), s_nt)
                    if counts(g):
                        wait(pool, s_cf0, 32 * (g + 1))
                        wait(pool, s_cf1, 32 * (g + 1))
                        wait(pool, s_po, base + n[0])
                        wait(pool, s_nt, 7 * g + 7)
                        pool.sem_inc(s_pass, 1)
                        did(pool.tensor_scalar(count[:, par, :], cs[:, par, ROUNDS - 1, :], 0.5, S / 2 + 0.25, ALU.mult, ALU.add))
                        did(pool.tensor_scalar(ext[:, par, :, 0], nt[:, par, :], -1.0, None, ALU.mult))
                        did(pool.tensor_scalar(low[:, :], nt[:, par, :], 0.0, None, ALU.is_ge))
                        wait_own()
                        did(pool.tensor_scalar(count[:, par, :], count[:, par, :], ROUNDER, -ROUNDER, ALU.add, ALU.add))
                        wait_own()
                        did(pool.tensor_scalar(err[:, :], count[:, par, :], -AIM, None, ALU.add))
                        wait_own()
                        did(pool.tensor_tensor(sq[:, :], err[:, :], err[:, :], ALU.mult))
                        wait_own()
                        did(pool.tensor_scalar(far[:, :], sq[:, :], 12.96, None, ALU.is_gt))
                        wait_own()
                        did(pool.tensor_tensor(fail[:, par, :], far[:, :], low[:, :], ALU.add), s_cfin)
                        if g_last(g):
                            n[0] += 1
                        assert n[0] == 38, n[0]

                g_last = lambda g: isinstance(g, int) and g == N - 1
                pool.tensor_copy(sd[:, 0, :], m.sd[:, 0, 0:TILES]).then_inc(s_po, 1)
                pool.wait_ge(s_po, 1)
                pool.tensor_scalar(nt[:, 0, :], sd[:, 0, :], -Z0, None, ALU.mult).then_inc(s_nt, 1)
                steps(pool, emit, B - 1)

            @blk.tensor
            def _(pe):
                pe.wait_ge(s_load, 16 * 17)
                pe.wait_ge(s_init, 1)

                def emit(g, r, batch):
                    def values(ch, back):
                        q, qr = g - back, (r - back) % 2
                        if ch == 0:
                            wait(pe, s_u, q)
                            wait(pe, s_vld[qr], 32 * (alike(r, batch, back) + 1))
                        wait(pe, s_w, 8 * q + 2 * ch + 2)
                        for i in range(QUAD):
                            pe.matmul(u_p[0][COL * i:COL * i + COL, :], vq[:, qr, ch, i, :], w[:, ch % 2, i, :],
                                      start=(ch == 0), stop=(ch == TB - 1))
                        for i in range(QUAD):
                            mm = pe.matmul(u_p[1][COL * i:COL * i + COL, :], vpq[:, qr, ch, i, :], mask[:, ch % 2, i, :],
                                           start=(ch == 0), stop=(ch == TB - 1))
                        mm.then_inc(s_pv, 1)

                    tile = 0
                    for s in range(SLOTS):
                        if counts(g):
                            if s == 0:
                                wait(pe, s_ld[r % 2], LD * (alike(r, batch, 0) + 1))
                            for n in range(4 * s, 4 * s + 4):
                                col = 8 * (n // 8 % 2) + n % 8
                                i, t = col // TB, col % TB
                                wait(pe, s_cf[n % 2], 32 * g + n // 2)
                                pe.matmul(cb[:, n % 2, :], stack_q[rows_of(i), r, i // 2, t * P:(t + 1) * P],
                                          stack_k[rows_of(i), r, SIDE_MASK, i // 2, :], start=True, stop=True).then_inc(s_cu, 1)
                        if finals(g):
                            q = (r - 1) % QUADS
                            if s == 0:
                                o = to(pe, g, "flag")
                                wait(pe, s_cfin, g)
                                pe.matmul(o[0:1, 0:TILES], one[:, :], fail[:, (r - 1) % 2, :], start=True, stop=True).then_inc(s_du, 1)
                            for _ in range(FINALS[s]):
                                i, t = tile // TB, tile % TB
                                o = to(pe, g, ("D", tile))
                                pe.matmul(o, stack_q[rows_of(i), q, i // 2, t * P:(t + 1) * P],
                                          stack_k[rows_of(i), q, SIDE_MASK, i // 2, :], start=True, stop=True).then_inc(s_du, 1)
                                tile += 1
                        if s == 1 and ends(g):
                            values(TB - 1, 3)
                        if keys(g):
                            q = (r - 2) % QUADS
                            ch, i = s // QUAD, s % QUAD
                            at = slice(ch * P, (ch + 1) * P)
                            if s == 0:
                                wait(pe, s_st[r % 2], 64 * (alike(r, batch, 2) + 1))
                            for side, dst, s_read, s_done in ((SIDE_EXP, h_p, s_exp, s_hp), (SIDE_MASK, g_p, s_mk, s_gp)):
                                wait(pe, s_read, TILES * (g - 2) + s)
                                pe.matmul(dst[:, :], stack_k[rows_of(i, STAT), q, side, i // 2, at],
                                          stack_q[rows_of(i, STAT), q, i // 2, :], start=True, stop=True).then_inc(s_done, 1)
                            if i == 2 and ch >= 1:
                                values(ch - 1, 2)
                        if s == 13 and ends(g):
                            for k in range(2):
                                o = to(pe, g, f"F{k}")
                                wait(pe, s_u, g - 2)
                                for t in range(TB):
                                    mm = pe.transpose(o[:, t * P:(t + 1) * P], u_sb[:, k, t * P:(t + 1) * P], m.ident[:, :])
                                mm.then_inc(s_du, 1)
                        if s == 14 and finals(g):
                            o = to(pe, g, "T").bitcast(BF16)
                            wait(pe, s_sp, g)
                            for t in range(TB):
                                mm = pe.transpose(o[0:QUAD * STAT, t * P:(t + 1) * P],
                                                  stat_part[:, t, :, :, :].rearrange("p i k j -> p (i k j)"), m.ident_b[:, :])
                            mm.then_inc(s_du, 1)

                steps(pe, emit)

            @blk.scalar
            def _(act):
                def emit(g, r, batch):
                    for s in range(SLOTS):
                        if counts(g):
                            for n in range(4 * s, 4 * s + 4):
                                rnd, group = n // 16, n // 8 % 2
                                col = 8 * group + n % 8
                                if n % 8 == 0:
                                    wait(act, s_nt, 7 * g + 1 + (2 * (rnd - 1) + group + 1 if rnd else 0))
                                wait(act, s_cu, 64 * g + n + 1)
                                act.activation(junk[:, n % 2, :], cb[:, n % 2, :], ACT.Sign, bias=nt[:, r % 2, col:col + 1],
                                               accum_out=cs[:, r % 2, rnd, col:col + 1]).then_inc(s_cf[n % 2], 1)
                        if keys(g):
                            ch, i = s // QUAD, s % QUAD
                            wait(act, s_hp, TILES * (g - 2) + s + 1)
                            wait(act, s_w, 8 * (g - 2) + 2 * ch + i // 2 - 1)
                            act.activation(e[:, i, :], h_p[:, :], ACT.Exp).then_inc(s_exp, 1)
                        if s == 2 and ends(g):
                            wait(act, s_pv, TB * (g - 2))
                            if not isinstance(g, int) or g >= 4:
                                wait(act, s_du, use(g - 1, "F1") + 1)
                            act.activation(u_sb[:, 0, :], u_p[0][:, :], ACT.Copy)
                            act.activation(u_sb[:, 1, :], u_p[1][:, :], ACT.Copy).then_inc(s_u, 1)
                        if s == 15 and finals(g):
                            q = (r - 1) % 2
                            wait(act, s_sp, g)
                            wait(act, s_tok, g - 2)
                            act.activation(floor[:, q, :, :], stat[:, q, :, :, 1], ACT.Exp).then_inc(s_fl, 1)
                            o = used(act, g, "T").bitcast(BF16)
                            wait(act, s_st[q], 64 * alike(r, batch, 1))
                            act.activation(statT[:, q, :], o[0:QUAD * STAT, 0:S], ACT.Copy).then_inc(freed(g, "T"), 1)

                steps(act, emit)

            @blk.vector
            def _(dve):
                dve.wait_ge(s_load, 16 * 17)

                def carry():
                    dve.sem_inc(s_pass2, 1)

                def middle(g, r, batch, general):
                    q = (r - 1) % 2

                    def copy(j):
                        o = used(dve, g, ("D", j))
                        carry()
                        dve.tensor_scalar(score[:, j % 2, :], o, 1.0, LOW, ALU.mult, ALU.max,
                                          accum_out=rmax[:, j:j + 1]).then_inc(freed(g, ("D", j)), 1)

                    def below(j):
                        released(dve, g, ("D", j))
                        dve.scalar_tensor_tensor(work[:, j % 2, :], score[:, j % 2, :], ext[:, q, j, 0:1], score[:, j % 2, :],
                                                 ALU.is_lt, ALU.mult).then_inc(s_fin, 1)

                    def eight(j):
                        wait(dve, s_fin, 2 * TILES * (g - 1) + (2 * j + 1 if j == 0 or general else 2 * j + 1))
                        carry()
                        dve.max(ext[:, q, j, 1:9], work[:, j % 2, :]).then_inc(s_fin, 1)

                    def take_out(j):
                        n = [0]

                        def did(ins):
                            n[0] += 1
                            ins.then_inc(s_top, 1)

                        def wait_own():
                            wait(dve, s_top, TOPS * (TILES * (g - 1) + j) + n[0])
                            carry()

                        wait(dve, s_fin, 2 * TILES * (g - 1) + 2 * j + 2)
                        for k in range(7):
                            wait_own()
                            did(dve.max(top[:, k, :], score[:, j % 2, :]))
                            if k < 6:
                                wait_own()
                                did(dve.match_replace(score[:, j % 2, :], top[:, k, :], score[:, j % 2, :], LOW))
                        wait_own()
                        last = KEEP - 1 - 48
                        did(dve.tensor_copy(ext[:, q, j, 0:2], top[:, 6, last:last + 2]))
                        did(dve.memset(count[:, q, j:j + 1], float(KEEP)))
                        n[0] += 2
                        dve.sem_inc(s_top, 2)

                    tile = 0
                    for s in range(13):
                        for _ in range(FINALS[s]):
                            copy(tile)
                            if general:
                                below(tile)
                                eight(tile)
                                flag = dve.value_load(flags[0:1, 1 + tile:2 + tile], min_val=0, max_val=2 * P)
                                with dve.If(flag > 0):
                                    take_out(tile)
                                with dve.Else():
                                    dve.sem_inc(s_top, TOPS)
                                wait(dve, s_top, TOPS * (TILES * (g - 1) + tile + 1))
                            else:
                                if tile:
                                    eight(tile - 1)
                                below(tile)
                            tile += 1
                        if keys(g):
                            masks(g, s)
                    if not general:
                        eight(TILES - 1)
                        dve.sem_inc(s_top, TOPS * TILES)

                def masks(g, s):
                    ch, i = s // QUAD, s % QUAD
                    wait(dve, s_gp, TILES * (g - 2) + s + 1)
                    wait(dve, s_pv, TB * (g - 2) + ch - 1)
                    dve.tensor_scalar(mask[:, ch % 2, i, :], g_p[:, :], 0.0, None, ALU.is_ge).then_inc(s_mk, 1)

                def emit(g, r, batch):
                    q = (r - 1) % 2
                    if finals(g):
                        o = used(dve, g, "flag")
                        dve.tensor_copy(flags[:, 1:], o[0:1, 0:TILES]).then_inc(s_flag, 1)
                        dve.tensor_reduce(flags[:, 0:1], o[0:1, 0:TILES], AX.X, ALU.max).then_inc(freed(g, "flag"), 1)
                        released(dve, g, "flag")
                        wait(dve, s_flag, g)
                        wait(dve, s_cfin, g)
                        carry()
                        any_flag = dve.value_load(flags[0:1, 0:1], min_val=0, max_val=2 * P)
                        with dve.If(any_flag > 0):
                            middle(g, r, batch, True)
                        with dve.Else():
                            middle(g, r, batch, False)
                        wait(dve, s_fin, 2 * TILES * g)
                        wait(dve, s_top, TOPS * TILES * g)
                        n = [0]

                        def did(ins):
                            n[0] += 1
                            ins.then_inc(s_sel, 1)

                        def wait_own():
                            wait(dve, s_sel, 9 * (g - 1) + n[0])

                        wait_own()
                        did(dve.tensor_tensor(pick[:, 0, :, :], ranks[:, :].unsqueeze(1).to_broadcast([P, TILES, 9]),
                                              count[:, q, :].unsqueeze(2).to_broadcast([P, TILES, 9]), ALU.add))
                        did(dve.tensor_tensor(largest[:, :], rmax[:, :], m.mean[:, batch(1), (r - 1) % QUADS * TILES:((r - 1) % QUADS + 1) * TILES], ALU.add))
                        wait_own()
                        did(dve.scalar_tensor_tensor(pick[:, 1, :, :], pick[:, 0, :, :], KEEP - 0.25, ext[:, q, :, :], ALU.is_gt, ALU.mult))
                        wait_own()
                        did(dve.scalar_tensor_tensor(pick[:, 2, :, :], pick[:, 0, :, :], KEEP + 1.25, pick[:, 1, :, :], ALU.is_lt, ALU.mult))
                        wait_own()
                        did(dve.tensor_reduce(thr[:, :], pick[:, 2, :, :], AX.X, ALU.add))
                        wait_own()
                        st, sr = stat[:, q, :, :, :], stat_rest[:, :, :, :]
                        wait(dve, s_fl, g - 2)
                        dve.tensor_scalar(stat[:, q, :, :, 0].rearrange("p t i -> p i t"), thr[:, :].rearrange("p (i t) -> p i t", t=TB),
                                          -0.5, None, ALU.mult).then_inc(s_sel, 1)
                        dve.tensor_scalar(stat[:, q, :, :, 1].rearrange("p t i -> p i t"), largest[:, :].rearrange("p (i t) -> p i t", t=TB),
                                          0.0, -1.0, ALU.max, ALU.mult).then_inc(s_sel, 1)
                        n[0] += 2
                        wait_own()
                        if not isinstance(g, int) or g >= 2:
                            wait(dve, s_du, use(g - 1, "T") + 1)
                        pt = [stat_part[:, :, :, :, k] for k in range(3)]
                        did(dve.tensor_copy(pt[0], st))
                        wait_own()
                        did(dve.tensor_tensor(sr, st, pt[0], ALU.subtract))
                        wait_own()
                        dve.tensor_copy(pt[1], sr).then_inc(s_split2, 1)
                        wait(dve, s_split2, g)
                        dve.tensor_tensor(pt[2], sr, pt[1], ALU.subtract).then_inc(s_sp, 1)
                    elif keys(g):
                        for s in range(13):
                            masks(g, s)
                    if keys(g):
                        masks(g, 13)
                    if ends(g):
                        finish(g, r, batch)
                    if keys(g):
                        masks(g, 14)
                        masks(g, 15)

                def finish(g, r, batch):
                    n = [0]
                    q = (r - 3) % QUADS

                    def did(ins):
                        n[0] += 1
                        ins.then_inc(s_f, 1)

                    def wait_own():
                        wait(dve, s_f, 5 * (g - 3) + n[0])

                    parts = lambda x: x.rearrange("p (t i c) -> p t i c", t=TB, i=QUAD)
                    uT = parts(used(dve, g, "F0"))
                    mT = parts(used(dve, g, "F1"))
                    wait(dve, s_tok, g - 3)
                    did(dve.tensor_copy(tot[:, :, :, :], mT[:, :, :, 0:VW]))
                    wait_own()
                    did(dve.tensor_tensor(tot2[:, :, :, :], mT[:, :, :, VW:2 * VW], tot[:, :, :, :], ALU.add))
                    wait_own()
                    dve.tensor_tensor(tot[:, :, :, :], mT[:, :, :, 2 * VW:3 * VW], tot2[:, :, :, :], ALU.add).then_inc(freed(g, "F1"), 1)
                    released(dve, g, "F1")
                    sv = m.sumv[:, batch(3), QUAD * q:QUAD * (q + 1), :].unsqueeze(1).to_broadcast([P, TB, QUAD, VW])
                    did(dve.tensor_tensor(tot2[:, :, :, :], sv, tot[:, :, :, :], ALU.subtract))
                    wait_own()
                    wait(dve, s_fl, g - 2)
                    fl = floor[:, (r - 3) % 2, :, :].unsqueeze(3).to_broadcast([P, TB, QUAD, VW])
                    did(dve.tensor_tensor(tot[:, :, :, :], tot2[:, :, :, :], fl, ALU.mult))
                    wait_own()
                    dve.tensor_tensor(tot2[:, :, :, :], uT[:, :, :, 0:VW], tot[:, :, :, :], ALU.add).then_inc(freed(g, "F0"), 1)
                    released(dve, g, "F0")
                    did(dve.reciprocal(zr[:, :, :, :], tot2[:, :, :, HD1:VW]))
                    wait_own()
                    dst = m.attn[:, batch(3), :, q * COL:(q + 1) * COL].rearrange("p t (i d) -> p t i d", d=HD1)
                    dve.tensor_tensor(dst, tot2[:, :, :, 0:HD1], zr[:, :, :, :].to_broadcast([P, TB, QUAD, HD1]),
                                      ALU.mult).then_inc(s_tok, 1)

                steps(dve, emit)


def attention_out(nc, m, a):
    with ExitStack() as c:
        sb = lambda n, s, d=F32: c.enter_context(nc.sbuf_tensor("ao_" + n, s, d))
        sem = lambda n: nc.alloc_semaphore("ao_" + n)
        w_o, bo = sb("w_o", [P, P]), sb("bo", [P, 1])
        aT, y = sb("aT", [P, 2, S]), sb("y", [P, 2, S])
        at_p = c.enter_context(nc.psum_tensor("ao_at_p", [P, 2, S], F32))
        y_p = c.enter_context(nc.psum_tensor("ao_y_p", [P, 2, S], F32))
        s_load, s_t, s_aT, s_mm, s_y = (sem(n) for n in ("load", "t", "aT", "mm", "y"))
        with nc.Block() as blk:
            @blk.sync
            def _(sp):
                sp.dma_start(w_o[:, :], a["L1_attn_Wo"]).then_inc(s_load, 16)
                sp.dma_start(bo[:, :], a["L1_attn_bo"].rearrange("(p o) -> p o", o=1)).then_inc(s_load, 16)

            @blk.tensor
            def _(pe):
                pe.wait_ge(s_load, 32)

                def turn(b):
                    if b >= 2:
                        pe.wait_ge(s_aT, b - 1)
                    for t in range(TB):
                        mm = pe.transpose(at_p[:, b % 2, t * P:(t + 1) * P], m.attn[:, b, t, :], m.ident[:, :])
                    mm.then_inc(s_t, 1)

                turn(0)
                for b in range(B):
                    if b + 1 < B:
                        turn(b + 1)
                    pe.wait_ge(s_aT, b + 1)
                    if b >= 2:
                        pe.wait_ge(s_y, b - 1)
                    pe.matmul(y_p[:, b % 2, :], w_o[:, :], aT[:, b % 2, :], start=True, stop=True).then_inc(s_mm, 1)

            @blk.scalar
            def _(act):
                for b in range(B):
                    act.wait_ge(s_t, b + 1)
                    if b >= 2:
                        act.wait_ge(s_mm, b - 1)
                    act.activation(aT[:, b % 2, :], at_p[:, b % 2, :], ACT.Copy).then_inc(s_aT, 1)

            @blk.vector
            def _(dve):
                dve.wait_ge(s_load, 32)
                for b in range(B):
                    dve.wait_ge(s_mm, b + 1)
                    dve.tensor_scalar(y[:, b % 2, :], y_p[:, b % 2, :], bo[:, 0:1], m.mod[:, 1, GATE, b:b + 1], ALU.add,
                                      ALU.mult).then_inc(s_y, 1)
                    dve.wait_ge(s_y, b + 1)
                    dve.tensor_tensor(m.xT[:, b, :], m.xT[:, b, :], y[:, b % 2, :], ALU.add)


def experts(nc, m, a, gelu):
    tag = "ge_" if gelu else "li_"
    layer = 0 if gelu else 1
    with ExitStack() as c:
        sb = lambda n, s, d=F32: c.enter_context(nc.sbuf_tensor(tag + n, s, d))
        pb = lambda n, s: c.enter_context(nc.psum_tensor(tag + n, s, F32))
        sem = lambda n: nc.alloc_semaphore(tag + n)
        hs = sb("hs", [P, 2, S])
        lg = sb("lg", [P, TB, EX])
        m8 = sb("m8", [P, TB, 8])
        sh = sb("sh", [P, TB, EX])
        ex = sb("ex", [P, TB, EX])
        mk = sb("mk", [P, TB, EX])
        exm = sb("exm", [P, TB, EX])
        tot = sb("tot", [P, TB])
        inv = sb("inv", [P, TB])
        share = sb("share", [P, TB, EX])
        acc = sb("acc", [P, TB, P])
        STAGE = EX if gelu else 2
        if gelu:
            w1 = sb("w1", [P, EX, FF])
            w2 = sb("w2", [P, EX, 2, P])
            act_ = sb("act", [P, 2, 2, S])
            gate_w = m.small_T[:, 2, :]
            up_p = pb("up_p", [P, 2, 2, S])
            loads = [(w1[:, :, :], a["L0_ffn_w1"].rearrange("e p f -> p e f")),
                     ] + [(w2[:, :, k, :], a["L0_ffn_w2"][:, k * P:(k + 1) * P, :].rearrange("e p f -> p e f")) for k in range(2)]
            NOUT = EX
        else:
            wexp = sb("wexp", [P, EX, P])
            gw = sb("gw", [P, EX])
            gb = sb("gb", [P, EX])
            bexp = sb("bexp", [EX, P])
            shareT = sb("shareT", [EX, S])
            gate_w = gw[:, :]
            loads = [(wexp[:, :, :], a["L1_ffn_W_experts"].rearrange("e p f -> p e f")),
                     (gw[:, :], a["L1_ffn_W_gate"]), (bexp[:, :], a["L1_ffn_b_experts"]),
                     (gb[:, :], a["L1_ffn_b_gate"].rearrange("(o d) -> o d", o=1).to_broadcast([P, EX]))]
            NOUT = 2 * TB
        out_p = pb("out_p", [P, 2, S])
        lg_p = pb("lg_p", [P, S])
        y_p = pb("y_p", [P, S])
        (s_load, s_hs, s_lg, s_out, s_g, s_ex, s_acc, s_tr, s_x, s_free, s_norm, s_pass) = map(
            sem, ("load", "hs", "lg", "out", "g", "ex", "acc", "tr", "x", "free", "norm", "pass"))
        if gelu:
            s_up, s_act = sem("up"), sem("act")
        else:
            s_sh, s_shT = sem("sh"), sem("shT")
        G = 9 if gelu else 10
        ACC = EX * TB

        with nc.Block() as block:
            @block.sync
            def _(sp):
                for dst, src in loads:
                    sp.dma_start(dst, src).then_inc(s_load, 16)

            @block.gpsimd
            def _(pool):
                with pool.Fori(0, B // 2) as i:
                    for j in range(2):
                        b = 2 * i + j
                        pool.wait_ge(s_free, b + 1)
                        pool.tensor_copy(hs[:, j, :], m.hT[:, b, WINDOW:]).then_inc(s_hs, 1)

            @block.tensor
            def _(pe):
                pe.sem_inc(s_free, 2)
                pe.wait_ge(s_load, 16 * len(loads))
                with pe.Fori(0, B // 2) as i:
                    for j in range(2):
                        b = 2 * i + j
                        pe.wait_ge(s_hs, b + 1)
                        pe.wait_ge(s_g, G * b)
                        for t in range(TB):
                            mm = pe.matmul(lg_p[:, t * EX:(t + 1) * EX], hs[:, j, t * P:(t + 1) * P], gate_w,
                                           start=True, stop=True)
                        mm.then_inc(s_lg, 1)
                        if gelu:
                            def up(e):
                                n = EX * b + e
                                if e >= 2:
                                    pe.wait_ge(s_act, n - 1)
                                for k in range(2):
                                    mm = pe.matmul(up_p[:, e % 2, k, :], w1[:, e, k * P:(k + 1) * P], hs[:, j, :],
                                                   start=True, stop=True)
                                mm.then_inc(s_up, 1)

                            up(0)
                            for e in range(EX):
                                n = EX * b + e
                                if e + 1 < EX:
                                    up(e + 1)
                                pe.wait_ge(s_act, n + 1)
                                if e >= 2:
                                    pe.wait_ge(s_acc, ACC * b + TB * (e - 1))
                                else:
                                    pe.wait_ge(s_acc, ACC * b)
                                for t in range(TB):
                                    for k in range(2):
                                        mm = pe.matmul(out_p[:, e % 2, t * P:(t + 1) * P], act_[:, e % 2, k, t * P:(t + 1) * P],
                                                       w2[:, e, k, :], start=(k == 0), stop=(k == 1))
                                mm.then_inc(s_out, 1)
                        else:
                            for n in range(NOUT):
                                t, k = n // 2, n % 2
                                if n >= 2:
                                    pe.wait_ge(s_acc, ACC * b + EX // 2 * (n - 1))
                                else:
                                    pe.wait_ge(s_acc, ACC * b)
                                pe.matmul(out_p[:, n % 2, :], hs[:, j, t * P:(t + 1) * P],
                                          wexp[:, 4 * k:4 * k + 4, :].rearrange("p e f -> p (e f)"),
                                          start=True, stop=True).then_inc(s_out, 1)
                            pe.wait_ge(s_g, G * (b + 1))
                            for t in range(TB):
                                mm = pe.transpose(lg_p[0:EX, t * P:(t + 1) * P], share[:, t, :], m.ident[:, :])
                            mm.then_inc(s_sh, 1)
                        pe.wait_ge(s_acc, ACC * (b + 1))
                        pe.wait_ge(s_x, b)
                        for t in range(TB):
                            mm = pe.matmul(y_p[:, t * P:(t + 1) * P], acc[:, t, :], m.ident[:, :],
                                           start=True, stop=gelu)
                            if t == 0:
                                mm.then_inc(s_free, 1)
                            if not gelu:
                                if t == 0:
                                    pe.wait_ge(s_shT, b + 1)
                                mm = pe.matmul(y_p[:, t * P:(t + 1) * P], bexp[:, :], shareT[:, t * P:(t + 1) * P],
                                               start=False, stop=True)
                        mm.then_inc(s_tr, 1)

            @block.scalar
            def _(act):
                with act.Fori(0, B // 2) as i:
                    for j in range(2):
                        b = 2 * i + j
                        act.wait_ge(s_g, G * b + (6 if gelu else 7))
                        act.activation(ex[:, :, :], sh[:, :, :], ACT.Exp).then_inc(s_ex, 1)
                        if gelu:
                            for e in range(EX):
                                n = EX * b + e
                                act.wait_ge(s_up, n + 1)
                                if e >= 2:
                                    act.wait_ge(s_out, n - 1)
                                act.activation(act_[:, e % 2, :, :], up_p[:, e % 2, :, :], ACT.Gelu).then_inc(s_act, 1)
                        else:
                            act.wait_ge(s_sh, b + 1)
                            act.activation(shareT[:, :], lg_p[0:EX, :], ACT.Copy).then_inc(s_shT, 1)

            @block.vector
            def _(dve):
                dve.wait_ge(s_load, 16 * len(loads))
                with dve.Fori(0, B // 2) as i:
                    for j in range(2):
                        b = 2 * i + j
                        g = [0]

                        def did(ins):
                            g[0] += 1
                            ins.then_inc(s_g, 1)

                        def wait_own():
                            dve.wait_ge(s_g, G * b + g[0])

                        flat = lambda x: x[:, :, :].rearrange("p t e -> p (t e)")
                        dve.wait_ge(s_lg, b + 1)
                        if not gelu:
                            dve.wait_ge(s_shT, b)
                        did(dve.tensor_copy(flat(lg), lg_p[:, 0:TB * EX]))
                        wait_own()
                        if not gelu:
                            did(dve.tensor_tensor(lg[:, :, :], lg[:, :, :], gb[:, :].unsqueeze(1).to_broadcast([P, TB, EX]), ALU.add))
                            wait_own()
                        dve.sem_inc(s_pass, 1)
                        for t in range(TB):
                            did(dve.max(m8[:, t, :], lg[:, t, :]))
                        wait_own()
                        did(dve.tensor_tensor(sh[:, :, :], lg[:, :, :], m8[:, :, 0:1].to_broadcast([P, TB, EX]), ALU.subtract))
                        did(dve.tensor_tensor(mk[:, :, :], lg[:, :, :], m8[:, :, 1:2].to_broadcast([P, TB, EX]), ALU.is_ge))
                        wait_own()
                        dve.wait_ge(s_ex, b + 1)
                        did(dve.tensor_tensor(exm[:, :, :], ex[:, :, :], mk[:, :, :], ALU.mult))
                        wait_own()
                        dve.tensor_reduce(tot[:, :], (exm if gelu else ex)[:, :, :], AX.X, ALU.add).then_inc(s_norm, 1)
                        dve.wait_ge(s_norm, 2 * b + 1)
                        dve.reciprocal(inv[:, :], tot[:, :]).then_inc(s_norm, 1)
                        dve.wait_ge(s_norm, 2 * b + 2)
                        if not gelu:
                            dve.wait_ge(s_sh, b)
                        did(dve.tensor_tensor(share[:, :, :], exm[:, :, :], inv[:, :].unsqueeze(2).to_broadcast([P, TB, EX]), ALU.mult))
                        wait_own()
                        assert g[0] == G, g[0]
                        first = 0
                        if not gelu:
                            dve.wait_ge(s_tr, b)
                        if gelu:
                            order = [(e, e, t) for e in range(EX) for t in range(TB)]
                            dve.wait_ge(s_tr, b)
                        else:
                            order = [(2 * t + e // 4, e, t) for t in range(TB) for e in range(EX)]
                        last = {}
                        for n, (use, e, t) in enumerate(order):
                            dve.wait_ge(s_out, NOUT * b + use + 1)
                            o = out_p[:, use % 2, (t * P if gelu else (e % 4) * P):][:, 0:P]
                            sc = share[:, t, e:e + 1]
                            if e == 0 and gelu:
                                ins = dve.tensor_scalar(acc[:, t, :], o, sc, None, ALU.mult)
                            else:
                                if t in last:
                                    dve.wait_ge(s_acc, ACC * b + last[t] + 1)
                                ins = dve.scalar_tensor_tensor(acc[:, t, :], o, sc, acc[:, t, :] if t in last else m.attn[:, b, t, :],
                                                               ALU.mult, ALU.add)
                            ins.then_inc(s_acc, 1)
                            last[t] = n
                        dve.wait_ge(s_tr, b + 1)
                        dve.scalar_tensor_tensor(m.xT[:, b, :], y_p[:, :], m.mod[:, layer, 3 + GATE, bass.ds(b, 1)], m.xT[:, b, :],
                                                 ALU.mult, ALU.add).then_inc(s_x, 1)


def store(nc, m, a, out):
    with ExitStack() as c:
        sem = lambda n: nc.alloc_semaphore("st_" + n)
        rows = c.enter_context(nc.sbuf_tensor("st_rows", [P, B, TB, P], F32))
        turned = c.enter_context(nc.psum_tensor("st_turned", [P, 4, S], F32))
        s_t, s_c, s_o = sem("t"), sem("c"), sem("o")
        with nc.Block() as block:
            @block.tensor
            def _(pe):
                for b in range(B):
                    if b >= 4:
                        pe.wait_ge(s_c, b - 3)
                    for t in range(TB):
                        mm = pe.transpose(turned[:, b % 4, t * P:(t + 1) * P], m.xT[:, b, t * P:(t + 1) * P], m.ident[:, :])
                    mm.then_inc(s_t, 1)

            @block.vector
            def _(dve):
                for b in range(B):
                    dve.wait_ge(s_t, b + 1)
                    dve.tensor_copy(rows[:, b, :, :].rearrange("p t d -> p (t d)"), turned[:, b % 4, :]).then_inc(s_c, 1)

            @block.sync
            def _(sp):
                for b in range(B):
                    sp.wait_ge(s_c, b + 1)
                    sp.dma_start(out[b].rearrange("(t p) d -> p t d", p=P), rows[:, b, :, :]).then_inc(s_o, 16)
                sp.wait_ge(s_o, 16 * B)


def program(nc, a, out, upto=99, dump=None):
    m = Memory()
    with ExitStack() as ctx:
        sb = lambda n, s, d=F32: ctx.enter_context(nc.sbuf_tensor(n, s, d))
        m.ident = sb("ident", [P, P])
        m.ident_b = sb("ident_b", [P, P], BF16)
        m.attn = sb("attn", [P, B, TB, P])
        m.mean_w = sb("mean_w", [P, P])
        m.xT = sb("xT", [P, B, S])
        m.hT = sb("hT", [P, B, WINDOW + S])
        m.small_T = sb("small_T", [P, 3, EX])
        m.wqT = sb("wqT", [P, HEADS * HD0])
        m.wkvT = sb("wkvT", [P, 2 * KV0 * HD0])
        m.woT = sb("woT", [P, PAIRS, P])
        m.mod = sb("mod", [P, 2, 6, B])
        m.qk_w = sb("qk_w", [P, 3])
        m.eps = sb("eps", [P, 2])
        m.mean = sb("mean", [P, B, HEADS * TB])
        m.sd = sb("sd", [P, B, HEADS * TB])
        m.sumv = sb("sumv", [P, B, HEADS, VW])
        m.parts = nc.dram_tensor("parts", (B, 3, HEADS, ROWS, S), BF16, kind="Internal").ap()
        m.v_store = nc.dram_tensor("v_store", (B, QUADS, P, TB * QUAD * COL), F32, kind="Internal").ap()
        m.vp_store = nc.dram_tensor("vp_store", (B, QUADS, P, TB * QUAD * COL), BF16, kind="Internal").ap()

        def phase(build, *args):
            with nc.cleanup_on_exit():
                build(nc, m, *args)

        phase(setup, a, ctx)
        phase(layer_norm, 0, 0, "ln0_")
        if upto >= 1:
            phase(window_attention, a)
        if upto >= 2:
            phase(layer_norm, 0, 1, "ln1_")
            phase(experts, a, True)
        if upto >= 3:
            phase(layer_norm, 1, 0, "ln2_")
            phase(project_sparse, a)
            phase(search_attention, a)
            phase(attention_out, a)
        if upto >= 4:
            phase(layer_norm, 1, 1, "ln3_")
            phase(head_attention, a, False)
            phase(experts, a, False)
            if out is not None:
                phase(store, a, out)
        if dump:
            dump(nc, m, ctx)


def constants():
    import numpy as np
    bf16 = mybir.dt.np(BF16)
    out = {"c_ident": np.eye(P, dtype=np.float32), "c_ident_b": np.eye(P).astype(bf16)}
    stat2 = np.zeros((6, 2, 2, S))
    stat2[3:6, 0] = 1.0
    stat2[0:3, 1] = 1.0
    out["c_stat2"] = stat2.astype(bf16)
    out["c_stat1"] = np.ones((3, 1, 2, S)).astype(bf16)
    of_head = np.arange(P) // HD1
    out["c_block"] = ((of_head[:, None] == of_head[None, :]) / S).astype(np.float32)
    out["c_heads"] = (of_head[:, None] == np.arange(HEADS)[None, :]).astype(np.float32)
    out["c_ranks"] = np.tile(np.arange(9, dtype=np.float32), (P, 1))
    half = np.zeros((P, P + 2), np.float32)
    for i in range(2):
        half[HD0 * i:HD0 * (i + 1), HD0 * i:HD0 * (i + 1)] = 1.0 / HD0
        half[HD0 * i:HD0 * (i + 1), P + i] = 1.0 / HD0
    out["c_half"] = half
    query, key = np.arange(P)[:, None], np.arange(WIN)[None, :]
    rel = key - WINDOW - query % SUB
    slopes = (2.0 ** (-0.5)) ** np.arange(1, HEADS + 1, dtype=np.float32)
    table = np.zeros((P, 2, HEADS, WIN), np.float32)
    for first in range(2):
        masked = (rel > 0) | (rel < -WINDOW)
        if first == 0:
            masked = masked | (query + rel < 0)
        for h in range(HEADS):
            table[:, first, h] = np.where(masked, -1e30, slopes[h] * rel.astype(np.float32))
    out["c_bias"] = table.reshape(P, 2, PAIRS, 2, WIN)
    return out


def kernel(**inputs):
    import numpy as _np
    import concourse.bacc as _bacc
    from concourse.bass_utils import run_bass_kernel_spmd as _run

    nc = _bacc.Bacc("TRN2", target_bir_lowering=False, num_devices=1)
    arrays, aps = {}, {}
    for name, x in list(inputs.items()) + list(constants().items()):
        x = _np.ascontiguousarray(x)
        arrays[f"in_{name}_dram"] = x
        aps[name] = nc.dram_tensor(f"in_{name}_dram", x.shape, mybir.dt.from_np(x.dtype), kind="ExternalInput").ap()
    out = nc.dram_tensor("out_dram", (B, S, P), F32, kind="ExternalOutput").ap()
    program(nc, aps, out)
    r = _run(nc, [arrays], core_ids=[0])
    return r.results[0]["out_dram"]
```

```python
from contextlib import ExitStack

import concourse.bass as bass
from concourse import mybir

F32 = mybir.dt.float32
BF16 = mybir.dt.bfloat16
ALU = mybir.AluOpType
ACT = mybir.ActivationFunctionType
AX = mybir.AxisListType

P = 128
B = 8
S = 512
TB = S // P
HEADS = 16

HD0 = 64
KV0 = 4
PAIRS = HEADS // 2
WINDOW = 16
SUB = 32
WIN = SUB + WINDOW
SLOT = 64
EPS0 = 0.01

EX = 8
FF = 256

HD1 = 8
KEEP = int(S * (1.0 - 0.9))
LN_EPS = 1e-5
GATE_MIN = 0.25
SHIFT_IN, SCALE_IN, GATE = 0, 1, 2


class Memory:
    pass


def setup(nc, m, a, ctx):
    with ExitStack() as c:
        sb = lambda n, s, d=F32: c.enter_context(nc.sbuf_tensor(n, s, d))
        sem = lambda n: nc.alloc_semaphore(n)
        x_rows = sb("x_rows", [P, B * TB, P])
        wq_rows = sb("wq_rows", [P, PAIRS, P])
        wkv_rows = sb("wkv_rows", [P, 4, P])
        wo_rows = sb("wo_rows", [P, PAIRS, P])
        small_rows = sb("small_rows", [EX, 3, P])
        wmod = sb("wmod", [P, 2, 6 * P])
        silu = sb("silu", [P, 2 * B])
        work = sb("silu_work", [P, 2 * B])
        absmod = sb("absmod", [P, 2, 6, B])
        turned = c.enter_context(nc.psum_tensor("turned", [P, 4, 512], F32))
        modp = c.enter_context(nc.psum_tensor("modp", [P, 2, 6, B], F32))
        loaded, x_loaded = sem("loaded"), sem("x_loaded")
        turn_done, turn_copied, mod_done, step, exps = (
            sem("turn_done"), sem("turn_copied"), sem("mod_done"), sem("setup_step"), sem("exp_done"))

        jobs = []
        jobs.append([(small_rows[:, i, :], EX) for i in range(3)])
        for g in range(2):
            jobs.append([(wq_rows[:, 4 * g + i, :], P) for i in range(4)])
        jobs.append([(wkv_rows[:, i, :], P) for i in range(4)])
        for g in range(2):
            jobs.append([(wo_rows[:, 4 * g + i, :], P) for i in range(4)])
        dests = [m.small_T[:, :, :].rearrange("p a b -> p (a b)"), m.wqT[:, 0:512], m.wqT[:, 512:1024], m.wkvT[:, :],
                 m.woT[:, 0:4, :].rearrange("p a b -> p (a b)"), m.woT[:, 4:8, :].rearrange("p a b -> p (a b)")]
        n_weights = len(jobs)
        for b in range(B):
            jobs.append([(x_rows[:, TB * b + i, :], P) for i in range(TB)])
            dests.append(m.xT[:, b, :])

        loads = [
            (m.ident[:, :], a["c_ident"]), (m.ident_b[:, :], a["c_ident_b"]),
            (small_rows[:, 0, :], a["L0_c"]), (small_rows[:, 1, :], a["L1_c"]),
            (small_rows[:, 2, :], a["L0_ffn_router_w"]),
            (wmod[:, 0, :], a["L0_wmod"]), (wmod[:, 1, :], a["L1_wmod"]),
            (wq_rows[:, :, :], a["L0_attn_wq"].rearrange("(g p) d -> p g d", p=P)),
            (wkv_rows[:, 0:2, :], a["L0_attn_wk"].rearrange("(g p) d -> p g d", p=P)),
            (wkv_rows[:, 2:4, :], a["L0_attn_wv"].rearrange("(g p) d -> p g d", p=P)),
            (wo_rows[:, :, :], a["L0_attn_wo"].rearrange("p (g d) -> p g d", d=P)),
            (m.qk_w[0:HD0, 0:1], a["L0_attn_q_norm_w"].rearrange("(p o) -> p o", o=1)),
            (m.qk_w[HD0:P, 0:1], a["L0_attn_q_norm_w"].rearrange("(p o) -> p o", o=1)),
            (m.qk_w[0:HD0, 1:2], a["L0_attn_k_norm_w"].rearrange("(p o) -> p o", o=1)),
            (m.qk_w[HD0:P, 1:2], a["L0_attn_k_norm_w"].rearrange("(p o) -> p o", o=1)),
        ]
        with nc.Block() as block:
            @block.sync
            def _(sp):
                for dst, src in loads:
                    sp.dma_start(dst, src).then_inc(loaded, 16)
                x_src = a["L0_attn_x"].rearrange("b (t p) d -> p (b t) d", p=P)
                for b in range(B):
                    sp.dma_start(x_rows[:, TB * b:TB * b + TB, :], x_src[:, TB * b:TB * b + TB, :]).then_inc(x_loaded, 16)

            @block.tensor
            def _(pe):
                pe.wait_ge(loaded, 16 * len(loads))
                for n, job in enumerate(jobs):
                    if n == n_weights:
                        pe.wait_ge(x_loaded, 16 * B)
                    if n == 1:
                        pe.wait_ge(step, 2)
                        for layer in range(2):
                            for j in range(6):
                                mm = pe.matmul(modp[:, layer, j, :], wmod[:, layer, j * P:(j + 1) * P],
                                               silu[:, layer * B:(layer + 1) * B], start=True, stop=True)
                        mm.then_inc(mod_done, 1)
                    if n >= 4:
                        pe.wait_ge(turn_copied, n - 3)
                    at = 0
                    for rows, k in job:
                        mm = pe.transpose(turned[:, n % 4, at:at + k], rows, m.ident[0:k, 0:k])
                        at += k
                    mm.then_inc(turn_done, 1)

            @block.scalar
            def _(act):
                act.wait_ge(turn_copied, 1)
                act.activation(work[:, :], m.small_T[:, 0:2, :].rearrange("p a b -> p (a b)"), ACT.Exp,
                               scale=-1.0).then_inc(exps, 1)

            @block.vector
            def _(dve):
                def copy(n):
                    dve.wait_ge(turn_done, n + 1)
                    width = sum(k for _, k in jobs[n])
                    dve.tensor_copy(dests[n], turned[:, n % 4, 0:width]).then_inc(turn_copied, 1)

                copy(0)
                dve.wait_ge(exps, 1)
                dve.tensor_scalar(silu[:, :], work[:, :], 1.0, None, ALU.add).then_inc(step, 1)
                dve.wait_ge(step, 1)
                dve.reciprocal(work[:, :], silu[:, :]).then_inc(exps, 1)
                dve.wait_ge(exps, 2)
                dve.tensor_tensor(silu[:, :], m.small_T[:, 0:2, :].rearrange("p a b -> p (a b)"), work[:, :],
                                  ALU.mult).then_inc(step, 1)
                for n in range(1, len(jobs)):
                    copy(n)
                dve.wait_ge(mod_done, 1)
                dve.tensor_copy(m.mod[:, :, :, :], modp[:, :, :, :]).then_inc(step, 1)
                dve.wait_ge(step, 3)
                dve.scalar_tensor_tensor(absmod[:, :, :, :].rearrange("p a b c -> p (a b c)"),
                                         m.mod[:, :, :, :].rearrange("p a b c -> p (a b c)"), -1.0,
                                         m.mod[:, :, :, :].rearrange("p a b c -> p (a b c)"),
                                         ALU.mult, ALU.max).then_inc(step, 1)
                dve.wait_ge(step, 4)
                n = 4
                for layer in range(2):
                    for j in (GATE, 3 + GATE):
                        g = m.mod[:, layer, j, :]
                        ab = absmod[:, layer, j, :]
                        dve.tensor_scalar(ab, ab, GATE_MIN, None, ALU.max).then_inc(step, 1)
                        dve.tensor_scalar(g, g, 0.0, 2.0, ALU.is_ge, ALU.mult).then_inc(step, 1)
                        n += 2
                        dve.wait_ge(step, n)
                        dve.scalar_tensor_tensor(g, g, -1.0, ab, ALU.add, ALU.mult).then_inc(step, 1)
                        n += 1
                    for j in (SCALE_IN, 3 + SCALE_IN):
                        g = m.mod[:, layer, j, :]
                        dve.tensor_scalar(g, g, 1.0, None, ALU.add).then_inc(step, 1)
                        n += 1
                dve.tensor_tensor(m.qk_w[:, 2:3], m.qk_w[:, 0:1], m.qk_w[:, 1:2], ALU.mult).then_inc(step, 1)
                n += 1
                dve.wait_ge(step, n)
                dve.tensor_scalar(m.qk_w[:, 2:3], m.qk_w[:, 2:3], float(HD0) ** -0.5, None, ALU.mult)
                dve.memset(m.hT[:, :, 0:WINDOW], 0.0)
                dve.memset(m.eps[:, 0:1], LN_EPS)
                dve.memset(m.eps[:, 1:2], EPS0)
                dve.memset(m.mean_w[:, :], 1.0 / P)


def layer_norm(nc, m, layer, part, name):
    BUFS = 4
    with ExitStack() as c:
        sb = lambda n, s, d=F32: c.enter_context(nc.sbuf_tensor(name + n, s, d))
        pb = lambda n, s: c.enter_context(nc.psum_tensor(name + n, s, F32))
        sem = lambda n: nc.alloc_semaphore(name + n)
        squared = sb("squared", [P, BUFS, S])
        std = sb("std", [P, B * TB])
        rstd = sb("rstd", [P, B * TB])
        diag = sb("diag", [P, BUFS, TB, P])
        wide_p = pb("wide_p", [P, BUFS, S])
        var_p = pb("var_p", [P, S])
        s_mean, s_cent, s_sq, s_var, s_std, s_rstd, s_diag, s_spread, s_norm, s_h = map(
            sem, ("mean", "cent", "sq", "var", "std", "rstd", "diag", "spread", "norm", "h"))
        done = lambda b: b + BUFS + 1
        free = lambda b: b + 1
        shift, scale = m.mod[:, layer, 3 * part + SHIFT_IN, :], m.mod[:, layer, 3 * part + SCALE_IN, :]
        with nc.Block() as block:
            @block.tensor
            def _(pe):
                pe.sem_inc(s_mean, BUFS)
                pe.sem_inc(s_var, BUFS)
                pe.sem_inc(s_spread, BUFS)
                with pe.Fori(0, B // BUFS) as i:
                    for j in range(BUFS):
                        b = BUFS * i + j
                        pe.wait_ge(s_cent, free(b))
                        pe.matmul(wide_p[:, j, :], m.mean_w[:, :], m.xT[:, b, :], start=True, stop=True).then_inc(s_mean, 1)
                    for j in range(BUFS):
                        b = BUFS * i + j
                        pe.wait_ge(s_sq, done(b))
                        for t in range(TB):
                            mm = pe.matmul(var_p[:, bass.ds(TB * b + t, 1)], squared[:, j, t * P:(t + 1) * P],
                                           m.mean_w[:, 0:1], start=True, stop=True)
                        mm.then_inc(s_var, 1)
                with pe.Fori(0, B // BUFS) as i:
                    for j in range(BUFS):
                        b = BUFS * i + j
                        pe.wait_ge(s_norm, free(b))
                        pe.wait_ge(s_diag, done(b))
                        for t in range(TB):
                            mm = pe.matmul(wide_p[:, j, t * P:(t + 1) * P], m.mean_w[:, :], diag[:, j, t, :],
                                           start=True, stop=True)
                        mm.then_inc(s_spread, 1)

            @block.scalar
            def _(act):
                act.sem_inc(s_sq, BUFS)
                with act.Fori(0, B // BUFS) as i:
                    for j in range(BUFS):
                        b = BUFS * i + j
                        act.wait_ge(s_cent, done(b))
                        act.wait_ge(s_var, free(b))
                        act.activation(squared[:, j, :], m.hT[:, b, WINDOW:], ACT.Square).then_inc(s_sq, 1)
                act.wait_ge(s_var, BUFS + B)
                act.activation(std[:, :], var_p[:, 0:B * TB], ACT.Sqrt, bias=m.eps[:, 0:1]).then_inc(s_std, 1)
                with act.Fori(0, B) as b:
                    act.wait_ge(s_norm, done(b))
                    act.activation(m.hT[:, b, WINDOW:], m.hT[:, b, WINDOW:], ACT.Identity, bias=shift[:, bass.ds(b, 1)],
                                   scale=scale[:, bass.ds(b, 1)]).then_inc(s_h, 1)

            @block.vector
            def _(dve):
                dve.sem_inc(s_cent, BUFS)
                dve.sem_inc(s_diag, BUFS)
                dve.sem_inc(s_norm, BUFS)
                with dve.Fori(0, B // BUFS) as i:
                    for j in range(BUFS):
                        b = BUFS * i + j
                        dve.wait_ge(s_mean, done(b))
                        dve.tensor_tensor(m.hT[:, b, WINDOW:], m.xT[:, b, :], wide_p[:, j, :], ALU.subtract).then_inc(s_cent, 1)
                dve.wait_ge(s_std, 1)
                dve.reciprocal(rstd[:, :], std[:, :]).then_inc(s_rstd, 1)
                dve.wait_ge(s_rstd, 1)
                with dve.Fori(0, B // BUFS) as i:
                    for j in range(BUFS):
                        b = BUFS * i + j
                        dve.wait_ge(s_spread, free(b))
                        for t in range(TB):
                            ins = dve.tensor_scalar(diag[:, j, t, :], m.ident[:, :], rstd[:, bass.ds(TB * b + t, 1)], float(P),
                                                    ALU.mult, ALU.mult)
                        ins.then_inc(s_diag, 1)
                    for j in range(BUFS):
                        b = BUFS * i + j
                        dve.wait_ge(s_spread, done(b))
                        dve.wait_ge(s_sq, done(b))
                        dve.tensor_tensor(m.hT[:, b, WINDOW:], m.hT[:, b, WINDOW:], wide_p[:, j, :], ALU.mult).then_inc(s_norm, 1)


def wait(eng, sem, value):
    if not (isinstance(value, int) and value <= 0):
        eng.wait_ge(sem, value)


def window_attention(nc, m, a):
    with ExitStack() as c:
        sb = lambda n, s, d=F32: c.enter_context(nc.sbuf_tensor("wa_" + n, s, d))
        pb = lambda n, s: c.enter_context(nc.psum_tensor("wa_" + n, s, F32))
        sem = lambda n: nc.alloc_semaphore("wa_" + n)
        hs = sb("hs", [P, 2, WINDOW + S + SLOT - WIN])
        q = sb("q", [P, 2, PAIRS, S])
        qsq = sb("qsq", [P, PAIRS, S])
        k = sb("k", [P, 2, S])
        ksq = sb("ksq", [P, 2, S])
        kstd = sb("kstd", [P, 2, S])
        krstd = sb("krstd", [P, 2, S])
        kT = sb("kT", [P, 2, 2, WINDOW + S])
        vw = sb("vw", [P, 2, S // SUB, P])
        qstd = sb("qstd", [P, TB, 2, PAIRS])
        qrstd = sb("qrstd", [P, 2, TB, 2, PAIRS])
        half = sb("half", [P, P + 2])
        bias = sb("bias", [P, 2, PAIRS, 2, WIN])
        sc = sb("sc", [P, 2, PAIRS, 2, WIN])
        pr = sb("pr", [P, 2, PAIRS, 2, SLOT])
        mx = sb("mx", [P, 2, PAIRS, 2])
        sm = sb("sm", [P, 2, PAIRS, 2])
        rs = sb("rs", [P, 2, PAIRS, 2])
        pT = sb("pT", [P, PAIRS, P])
        ao = sb("ao", [P, PAIRS, S])
        bank = pb("bank", [P, 2, S])
        sp = pb("sp", [P, 2, S])
        tp = pb("tp", [P, PAIRS, P])
        op = pb("op", [P, PAIRS, P])
        (s_const, s_zero, s_hs, s_use, s_free, s_kr, s_k, s_qr, s_S, s_mult, s_bias, s_max, s_sub, s_exp, s_sum,
         s_rs, s_p, s_t, s_pT, s_pv, s_ao, s_x, s_y, s_pass, s_pass2) = map(sem, (
             "const", "zero", "hs", "use", "free", "kr", "k", "qr", "S", "mult", "bias", "max", "sub", "exp",
             "sum", "rs", "p", "t", "pT", "pv", "ao", "x", "y", "pass", "pass2"))
        Q0, K0, M0, RQ, V0 = 0, PAIRS, PAIRS + 2, PAIRS + 4, PAIRS + 5
        USES = PAIRS + 9
        PIECES = (((0, 1, 2), (3, 4)), ((5, 6, 7), (K0, K0 + 1)), ((M0, M0 + 1), (RQ, V0)), ((V0 + 1, V0 + 2), (V0 + 3,)))
        wv = m.wkvT[:, 2 * P:].rearrange("p (a par d) -> p par a d", par=2, d=HD0)

        fixed = lambda b: isinstance(b, int)
        projects = lambda b: not fixed(b) or b + 1 < B
        attends = lambda b: not fixed(b) or 0 <= b < B
        follows = lambda b, t: not fixed(b) or 2 <= TB * b + t < TB * B + 2

        def slots(eng, emit):
            for b in (-1, 0):
                for t in range(TB):
                    emit(b, t, b % 2)
            with eng.Fori(0, B // 2 - 1) as i:
                for k_ in range(2):
                    for t in range(TB):
                        emit(2 * i + (k_ + 1), t, (k_ + 1) % 2)
            for b in (B - 1, B):
                for t in range(TB if b < B else 3):
                    emit(b, t, b % 2)

        with nc.Block() as block:
            @block.sync
            def _(sp_):
                sp_.dma_start(half[:, :], a["c_half"]).then_inc(s_const, 16)
                sp_.dma_start(bias[:, :, :, :, :], a["c_bias"]).then_inc(s_const, 16)

            @block.gpsimd
            def _(pool):
                pool.memset(hs[:, :, WINDOW + S:], 0.0).then_inc(s_zero, 1)
                pool.memset(kT[:, :, :, 0:WINDOW], 0.0).then_inc(s_zero, 1)
                pool.memset(pr[:, :, :, :, :], 0.0).then_inc(s_zero, 1)

                def slot(b, t, j):
                    if t == 0 and projects(b):
                        wait(pool, s_use, USES * b)
                        pool.sem_inc(s_pass2, 1)
                        pool.tensor_copy(hs[:, 1 - j, 0:WINDOW + S], m.hT[:, b + 1, :]).then_inc(s_hs, 1)

                slots(pool, slot)

            @block.tensor
            def _(pe):
                pe.wait_ge(s_const, 32)
                pe.wait_ge(s_zero, 3)

                def project(b, j, n):
                    wait(pe, s_free, USES * b + n - 1)
                    o = bank[:, (n + j) % 2, :]
                    if n < K0:
                        mm = pe.matmul(o, m.wqT[:, n * P:(n + 1) * P], hs[:, j, WINDOW:WINDOW + S], start=True, stop=True)
                    elif n < M0:
                        g = n - K0
                        mm = pe.matmul(o, m.wkvT[:, g * P:(g + 1) * P], hs[:, j, WINDOW:WINDOW + S], start=True, stop=True)
                    elif n < RQ:
                        mm = pe.matmul(o, half[:, 0:P], ksq[:, n - M0, :], start=True, stop=True)
                    elif n == RQ:
                        o = o[:, 0:TB * HEADS].rearrange("p (t par g) -> p t par g", t=TB, par=2)
                        for t in range(TB):
                            for g in range(PAIRS):
                                mm = pe.matmul(o[:, t, :, g], qsq[:, g, t * P:(t + 1) * P], half[:, P:P + 2], start=True, stop=True)
                    else:
                        for w in range(4):
                            at = (4 * (n - V0) + w) * SUB
                            for par in range(2):
                                mm = pe.matmul(o[SLOT * par:SLOT * par + SLOT, w * P:(w + 1) * P], hs[:, j, at:at + SLOT],
                                               wv[:, par, :, :], start=True, stop=True)
                    mm.then_inc(s_use, 1)

                def scores(b, t, j):
                    n = TB * b + t
                    if t == 0:
                        wait(pe, s_k, b + 1)
                    wait(pe, s_mult, n)
                    pe.sem_inc(s_pass, 1)
                    for par in range(2):
                        for g in range(PAIRS):
                            for sub in range(P // SUB):
                                at = t * P + SUB * sub
                                mm = pe.matmul(sp[SUB * sub:SUB * sub + SUB, par, g * WIN:(g + 1) * WIN],
                                               q[SLOT * par:SLOT * par + SLOT, j, g, at:at + SUB],
                                               kT[SLOT * par:SLOT * par + SLOT, j, g % 2, at:at + WIN],
                                               start=True, stop=True)
                    mm.then_inc(s_S, 1)

                def turn(n, t):
                    wait(pe, s_p, n + 1)
                    wait(pe, s_pT, n)
                    for g in range(PAIRS):
                        mm = pe.transpose(tp[:, g, :], pr[:, t % 2, g, :, :].rearrange("p a k -> p (a k)"), m.ident[:, :])
                    mm.then_inc(s_t, 1)

                def values(n, b, t, j):
                    wait(pe, s_pT, n + 1)
                    wait(pe, s_ao, n)
                    if t == 0:
                        wait(pe, s_x, b)
                    pe.sem_inc(s_pass, 1)
                    for kv in range(2):
                        for sub in range(P // SUB):
                            at = slice(SUB * sub, SUB * sub + SUB)
                            for par in range(2):
                                rows = slice(SLOT * par, SLOT * par + SLOT)
                                mm = pe.matmul(op[rows, 4 * kv:4 * kv + 4, at], vw[rows, j, 4 * t + sub, kv * HD0:(kv + 1) * HD0],
                                               pT[rows, kv::2, at], start=True, stop=True)
                    mm.then_inc(s_pv, 1)

                def slot(b, t, j):
                    if attends(b):
                        scores(b, t, j)
                    if projects(b):
                        if t == 0:
                            wait(pe, s_hs, b + 2)
                        for n in PIECES[t][0]:
                            project(b + 1, 1 - j, n)
                    n, late = TB * b + t - 2, t < 2
                    if follows(b, t):
                        turn(n, t)
                    if projects(b):
                        for k in PIECES[t][1]:
                            project(b + 1, 1 - j, k)
                    if follows(b, t):
                        values(n, b - 1 if late else b, (t - 2) % TB, 1 - j if late else j)
                        if t == 1:
                            wait(pe, s_ao, TB * b)
                            for g in range(PAIRS):
                                mm = pe.matmul(op[:, 0:TB, :].rearrange("p t d -> p (t d)"), m.woT[:, 2 * (g % 4) + g // 4, :],
                                               ao[:, g, :], start=(g == 0), stop=(g == PAIRS - 1))
                            mm.then_inc(s_y, 1)

                slots(pe, slot)

            @block.scalar
            def _(act):
                def read(b, j, n):
                    wait(act, s_use, USES * b + n + 1)
                    o = bank[:, (n + j) % 2, :]
                    if n < K0:
                        act.activation(q[:, j, n, :], o, ACT.Copy)
                        ins = act.activation(qsq[:, n, :], o, ACT.Square)
                    elif n < M0:
                        if n == K0:
                            wait(act, s_k, b)
                        act.activation(k[:, n - K0, :], o, ACT.Copy)
                        ins = act.activation(ksq[:, n - K0, :], o, ACT.Square)
                    elif n < RQ:
                        if n == M0:
                            wait(act, s_kr, b)
                        ins = act.activation(kstd[:, n - M0, :], o, ACT.Sqrt, bias=m.eps[:, 1:2])
                    elif n == RQ:
                        ins = act.activation(qstd[:, :, :, :].rearrange("p t a g -> p (t a g)"), o[:, 0:TB * HEADS], ACT.Sqrt,
                                             bias=m.eps[:, 1:2])
                    else:
                        g = n - V0
                        ins = act.activation(vw[:, j, 4 * g:4 * g + 4, :].rearrange("p a b -> p (a b)"), o, ACT.Copy)
                    ins.then_inc(s_free, 1)

                def slot(b, t, j):
                    n = TB * b + t
                    if projects(b):
                        for k_ in PIECES[t][0]:
                            read(b + 1, 1 - j, k_)
                    if follows(b, t):
                        wait(act, s_t, n - 1)
                        wait(act, s_pv, n - 2)
                        act.activation(pT[:, :, :], tp[:, :, :], ACT.Copy).then_inc(s_pT, 1)
                    if projects(b):
                        for k_ in PIECES[t][1]:
                            read(b + 1, 1 - j, k_)
                    if follows(b, t):
                        at = (t - 2) % TB
                        wait(act, s_pv, n - 1)
                        act.activation(ao[:, :, at * P:(at + 1) * P], op[:, :, :], ACT.Copy).then_inc(s_ao, 1)
                    if attends(b):
                        wait(act, s_sub, n + 1)
                        wait(act, s_t, n - 1)
                        act.activation(pr[:, t % 2, :, :, 0:WIN].rearrange("p g a k -> p (g a) k"),
                                       sc[:, t % 2, :, :, :].rearrange("p g a k -> p (g a) k"), ACT.Exp).then_inc(s_exp, 1)

                slots(act, slot)

            @block.vector
            def _(dve):
                dve.wait_ge(s_const, 32)

                def logits(b, t, j):
                    n, i = TB * b + t, t % 2
                    wait(dve, s_S, n + 1)
                    wait(dve, s_exp, n - 1)
                    s_ = sc[:, i, :, :, :].rearrange("p g a k -> p a g k")
                    for par in range(2):
                        ins = dve.tensor_tensor(s_[:, par], sp[:, par, 0:PAIRS * WIN].rearrange("p (g k) -> p g k", g=PAIRS),
                                                qrstd[:, j, t, par, :].unsqueeze(2).to_broadcast([P, PAIRS, WIN]), ALU.mult)
                    ins.then_inc(s_mult, 1)
                    wait(dve, s_mult, n + 1)
                    flat = sc[:, i, :, :, :].rearrange("p g a k -> p (g a k)")
                    dve.tensor_tensor(flat, flat, bias[:, 0 if t == 0 else 1, :, :, :].rearrange("p g a k -> p (g a k)"),
                                      ALU.add).then_inc(s_bias, 1)
                    wait(dve, s_bias, n + 1)
                    rows = sc[:, i, :, :, :].rearrange("p g a k -> p (g a) k")
                    m_ = mx[:, i, :, :].rearrange("p g a -> p (g a)")
                    dve.tensor_reduce(m_, rows, AX.X, ALU.max).then_inc(s_max, 1)
                    wait(dve, s_max, n + 1)
                    dve.tensor_tensor(rows, rows, m_.unsqueeze(2).to_broadcast([P, HEADS, WIN]), ALU.subtract).then_inc(s_sub, 1)

                def normalise(n, t):
                    i = t % 2
                    rows = pr[:, i, :, :, 0:WIN].rearrange("p g a k -> p (g a) k")
                    s_ = sm[:, i, :, :].rearrange("p g a -> p (g a)")
                    r_ = rs[:, i, :, :].rearrange("p g a -> p (g a)")
                    wait(dve, s_exp, n + 1)
                    dve.tensor_reduce(s_, rows, AX.X, ALU.add).then_inc(s_sum, 1)
                    wait(dve, s_sum, n + 1)
                    dve.reciprocal(r_, s_).then_inc(s_rs, 1)
                    wait(dve, s_rs, n + 1)
                    dve.tensor_tensor(rows, rows, r_.unsqueeze(2).to_broadcast([P, HEADS, WIN]), ALU.mult).then_inc(s_p, 1)

                def slot(b, t, j):
                    if t == 2 and attends(b - 1):
                        wait(dve, s_y, b)
                        dve.scalar_tensor_tensor(m.xT[:, b - 1, :], op[:, 0:TB, :].rearrange("p t d -> p (t d)"),
                                                 m.mod[:, 0, GATE, bass.ds(b - 1, 1)], m.xT[:, b - 1, :],
                                                 ALU.mult, ALU.add).then_inc(s_x, 1)
                    if attends(b):
                        logits(b, t, j)
                    if t == 0 and attends(b - 1) or t > 0 and attends(b):
                        normalise(TB * b + t - 1, (t - 1) % TB)
                    if t == 3 and projects(b):
                        nb, nj = b + 1, 1 - j
                        wait(dve, s_free, USES * nb + M0 + 2)
                        dve.reciprocal(krstd[:, :, :], kstd[:, :, :]).then_inc(s_kr, 1)
                        wait(dve, s_kr, nb + 1)
                        for g in range(2):
                            ins = dve.scalar_tensor_tensor(kT[:, nj, g, WINDOW:], k[:, g, :], m.qk_w[:, 2:3], krstd[:, g, :],
                                                           ALU.mult, ALU.mult)
                        ins.then_inc(s_k, 1)
                        wait(dve, s_free, USES * nb + RQ + 1)
                        dve.reciprocal(qrstd[:, nj, :, :, :], qstd[:, :, :, :]).then_inc(s_qr, 1)
                        wait(dve, s_qr, nb + 1)

                slots(dve, slot)


SPLIT_Q = (0, 0, 0, 1, 1, 2)
SPLIT_K = (0, 1, 2, 0, 1, 0)
GROUPS = len(SPLIT_Q)
ROWS = GROUPS * HD1
QUAD = 4
QUADS = HEADS // QUAD
COL = 32
VW = HD1 + 1
LOW = -3.0e38


def project(nc, m, a, sparse):
    tag = "ps_" if sparse else "pd_"
    KINDS = 3 if sparse else 2
    with ExitStack() as c:
        sb = lambda n, s, d=F32: c.enter_context(nc.sbuf_tensor(tag + n, s, d))
        pb = lambda n: c.enter_context(nc.psum_tensor(tag + n, [P, S], F32))
        sem = lambda n: nc.alloc_semaphore(tag + n)
        hs = sb("hs", [P, 2, S])
        w_q, w_k, w_v = (sb(n, [P, P]) for n in ("w_q", "w_k", "w_v"))
        cols = sb("cols", [P, 2])
        bq = sb("bq", [P, 1])
        bv = sb("bv", [P, P])
        ones = sb("ones", [P, P])
        block = sb("block", [P, P])
        heads = sb("heads", [P, HEADS])
        qkc = sb("qkc", [P, 2, 3, S])
        ksum = sb("ksum", [P, 2, 1])
        kbar = sb("kbar", [P, 2, 1])
        kbar_h = sb("kbar_h", [P, 2, HEADS])
        rest = sb("rest", [P, 2, 3, S])
        part = sb("part", [P, 2, 3, 3, S], BF16)
        v = sb("v", [P, 2, QUADS, TB, QUAD, COL])
        vrest = sb("vrest", [P, 2, 2, QUADS, TB, QUAD, HD1])
        vpart = sb("vpart", [P, 2, QUADS, TB, QUAD, COL], BF16)
        kT = sb("kT", [P, 2, TB, P])
        cov = sb("cov", [P, 2, P])
        z = sb("z", [P, 2, S])
        q_p, k_p, v_p, vs_p, kt_p, cov_p, y_p, st_p = (pb(n) for n in ("q_p", "k_p", "v_p", "vs_p", "kt_p", "cov_p", "y_p", "st_p"))
        names = ("load", "zero", "ones", "bq", "hs", "pq", "pk", "pv", "q", "k", "kbar", "kc", "p0", "rest", "p1", "p2", "wr0", "wr1",
                 "v", "vp", "vw0", "vw1", "vs", "sv", "kt", "kts", "cov", "covs", "y", "z", "st", "mean", "var", "sd", "kh", "split", "pass")
        (s_load, s_zero, s_ones, s_bq, s_hs, s_pq, s_pk, s_pv, s_q, s_k, s_kbar, s_kc, s_p0, s_rest, s_p1, s_p2, s_wr0, s_wr1,
         s_v, s_vp, s_vw0, s_vw1, s_vs, s_sv, s_kt, s_kts, s_cov, s_covs, s_y, s_z, s_st, s_mean, s_var, s_sd, s_kh, s_split,
         s_pass) = map(sem, names)
        VWR = 32 if sparse else 16
        s_wr, s_vw = (s_wr0, s_wr1), (s_vw0, s_vw1)
        WR = KINDS * GROUPS * 16
        if sparse:
            srcs = [a[f"L1_attn_W{x}"] for x in "qkv"], [a[f"L1_attn_b{x}"] for x in "qkv"]
        else:
            wqkv, bqkv = a["L1_ffn_W_qkv"], a["L1_ffn_b_qkv"]
            srcs = [wqkv[:, k * P:(k + 1) * P] for k in range(3)], [bqkv[k * P:(k + 1) * P] for k in range(3)]
        loads = [(w_q[:, :], srcs[0][0]), (w_k[:, :], srcs[0][1]), (w_v[:, :], srcs[0][2]),
                 (cols[:, 0:1], srcs[1][0].rearrange("(p o) -> p o", o=1)),
                 (cols[:, 1:2], srcs[1][1].rearrange("(p o) -> p o", o=1)),
                 (bv[:, :], srcs[1][2].rearrange("(o d) -> o d", o=1).to_broadcast([P, P])),
                 (block[:, :], a["c_block"]), (heads[:, :], a["c_heads"])]

        def batches(eng, emit):
            for j in range(2):
                emit(j, j, 0)
            with eng.Fori(1, B // 2) as i:
                for j in range(2):
                    emit(2 * i + j, j, i)

        with nc.Block() as blk:
            @blk.sync
            def _(sp):
                for dst, src in loads:
                    sp.dma_start(dst, src).then_inc(s_load, 16)

                def emit(b, j, pair):
                    wait(sp, s_p2, b + 1)
                    sp.sem_inc(s_pass, 1)
                    for kind, groups in ((0, SPLIT_Q), (1, SPLIT_K), (2, SPLIT_K))[:KINDS]:
                        for n, k in enumerate(groups):
                            sp.dma_start(m.parts[b, kind, :, HD1 * n:HD1 * n + HD1, :], part[:, j, k, kind, :]).then_inc(s_wr[j], 16)
                    wait(sp, s_vp if sparse else s_v, b + 1)
                    sp.sem_inc(s_pass, 1)
                    sp.dma_start(m.v_store[b].rearrange("q p n -> p q n"),
                                 v[:, j, :, :, :, :].rearrange("p q t i c -> p q (t i c)")).then_inc(s_vw[j], 16)
                    if not sparse:
                        return
                    sp.dma_start(m.vp_store[b].rearrange("q p n -> p q n"),
                                 vpart[:, j, :, :, :, :].rearrange("p q t i c -> p q (t i c)")).then_inc(s_vw[j], 16)

                batches(sp, emit)
                for j in range(2):
                    sp.wait_ge(s_wr[j], WR * B // 2)
                    sp.wait_ge(s_vw[j], VWR * B // 2)

            @blk.gpsimd
            def _(pool):
                pool.memset(v[:, :, :, :, :, :], 0.0).then_inc(s_zero, 1)
                pool.memset(vpart[:, :, :, :, :, :], 0.0).then_inc(s_zero, 1)
                pool.memset(ones[:, :], 1.0).then_inc(s_ones, 1)
                pool.wait_ge(s_zero, 2)
                pool.memset(v[:, :, :, :, :, HD1:VW], 1.0).then_inc(s_ones, 1)
                pool.memset(vpart[:, :, :, :, :, HD1:VW], 1.0).then_inc(s_ones, 1)

                def emit(b, j, pair):
                    wait(pool, s_pv, b - 1)
                    pool.sem_inc(s_pass, 1)
                    pool.tensor_copy(hs[:, j, :], m.hT[:, b, WINDOW:]).then_inc(s_hs, 1)

                batches(pool, emit)

            @blk.tensor
            def _(pe):
                pe.wait_ge(s_load, 16 * len(loads))
                pe.wait_ge(s_ones, 3)

                def emit(b, j, pair):
                    wait(pe, s_hs, b + 1)
                    wait(pe, s_q, b)
                    pe.matmul(q_p[:, :], w_q[:, :], hs[:, j, :], start=True, stop=True).then_inc(s_pq, 1)
                    wait(pe, s_k, b)
                    pe.matmul(k_p[:, :], w_k[:, :], hs[:, j, :], start=True, stop=True).then_inc(s_pk, 1)
                    wait(pe, s_v, b)
                    for t in range(TB):
                        mm = pe.matmul(v_p[:, t * P:(t + 1) * P], hs[:, j, t * P:(t + 1) * P], w_v[:, :], start=True, stop=True)
                    mm.then_inc(s_pv, 1)
                    if not sparse:
                        return
                    wait(pe, s_kc, b + 1)
                    wait(pe, s_kts, b)
                    for t in range(TB):
                        mm = pe.transpose(kt_p[:, t * P:(t + 1) * P], qkc[:, j, 2, t * P:(t + 1) * P], m.ident[:, :])
                    mm.then_inc(s_kt, 1)
                    wait(pe, s_v, b + 1)
                    wait(pe, s_sv, b)
                    for t in range(TB):
                        mm = pe.matmul(vs_p[:, :], ones[:, :], v[:, j, :, t, :, :], start=(t == 0), stop=(t == TB - 1))
                    mm.then_inc(s_vs, 1)
                    wait(pe, s_kts, b + 1)
                    wait(pe, s_covs, b)
                    for t in range(TB):
                        mm = pe.matmul(cov_p[:, 0:P], kT[:, j, t, :], kT[:, j, t, :], start=(t == 0), stop=(t == TB - 1))
                    mm.then_inc(s_cov, 1)
                    wait(pe, s_covs, b + 1)
                    wait(pe, s_z, b)
                    pe.matmul(y_p[:, :], cov[:, j, :], qkc[:, j, 0, :], start=True, stop=True).then_inc(s_y, 1)
                    wait(pe, s_z, b + 1)
                    wait(pe, s_kh, b + 1)
                    wait(pe, s_mean, b)
                    wait(pe, s_var, b)
                    for t in range(TB):
                        at = slice(t * P, (t + 1) * P)
                        pe.matmul(st_p[:, t * HEADS:(t + 1) * HEADS], z[:, j, at], heads[:, :], start=True, stop=True)
                        mm = pe.matmul(st_p[:, (TB + t) * HEADS:(TB + t + 1) * HEADS], qkc[:, j, 0, at], kbar_h[:, j, :],
                                       start=True, stop=True)
                    mm.then_inc(s_st, 1)

                batches(pe, emit)

            @blk.scalar
            def _(act):
                act.wait_ge(s_load, 16 * len(loads))
                act.activation(bq[:, :], cols[:, 0:1], ACT.Copy, scale=float(HD1) ** -0.5).then_inc(s_bq, 1)
                act.wait_ge(s_bq, 1)

                def emit(b, j, pair):
                    wait(act, s_pq, b + 1)
                    if sparse:
                        wait(act, s_st, b - 1)
                    wait(act, s_rest, b - 1)
                    act.activation(qkc[:, j, 0, :], q_p[:, :], ACT.Identity, bias=bq[:, 0:1],
                                   scale=float(HD1) ** -0.5).then_inc(s_q, 1)
                    wait(act, s_pk, b + 1)
                    act.activation(qkc[:, j, 1, :], k_p[:, :], ACT.Identity, bias=cols[:, 1:2],
                                   accum_out=ksum[:, j, :]).then_inc(s_k, 1)
                    if sparse:
                        wait(act, s_kc, b + 1)
                    wait(act, s_q, b + 1)
                    wait(act, s_k, b + 1)
                    wait(act, s_wr[j], WR * pair)
                    act.activation(part[:, j, 0, 0:KINDS, :], qkc[:, j, 0:KINDS, :], ACT.Copy).then_inc(s_p0, 1)
                    if sparse:
                        wait(act, s_kt, b + 1)
                        wait(act, s_cov, b - 1)
                        act.activation(kT[:, j, :, :], kt_p[:, :].rearrange("p (t d) -> p t d", t=TB), ACT.Copy).then_inc(s_kts, 1)
                    wait(act, s_rest, b + 1)
                    act.activation(part[:, j, 1, 0:KINDS, :], rest[:, j, 0:KINDS, :], ACT.Copy).then_inc(s_p1, 1)
                    if not sparse:
                        return
                    wait(act, s_st, b + 1)
                    wait(act, s_var, b + 1)
                    act.activation(m.mean[:, b, :].rearrange("p (h t) -> p t h", t=TB),
                                   st_p[:, TB * HEADS:2 * TB * HEADS].rearrange("p (t h) -> p t h", t=TB),
                                   ACT.Copy).then_inc(s_mean, 1)

                batches(act, emit)
                if sparse:
                    act.wait_ge(s_var, B)
                    act.activation(m.sd[:, :, :], m.sd[:, :, :], ACT.Sqrt).then_inc(s_sd, 1)

            @blk.vector
            def _(dve):
                dve.wait_ge(s_load, 16 * len(loads))
                dve.wait_ge(s_ones, 3)

                def emit(b, j, pair):
                    if sparse:
                        wait(dve, s_k, b + 1)
                        wait(dve, s_kh, b - 1)
                        dve.tensor_scalar(kbar[:, j, :], ksum[:, j, :], 1.0 / S, None, ALU.mult).then_inc(s_kbar, 1)
                        wait(dve, s_kbar, b + 1)
                        wait(dve, s_cov, b - 1)
                        dve.tensor_scalar(qkc[:, j, 2, :], qkc[:, j, 1, :], kbar[:, j, 0:1], None, ALU.subtract).then_inc(s_kc, 1)
                        wait(dve, s_st, b - 1)
                        dve.tensor_scalar(kbar_h[:, j, :], heads[:, :], kbar[:, j, 0:1], None, ALU.mult).then_inc(s_kh, 1)
                    wait(dve, s_pv, b + 1)
                    wait(dve, s_vw[j], VWR * pair)
                    for r in range(QUADS):
                        ins = dve.tensor_tensor(v[:, j, r, :, :, 0:HD1],
                                                v_p[:, :].rearrange("p (t q i d) -> p q t i d", t=TB, q=QUADS, i=QUAD)[:, r],
                                                bv[:, r * COL:(r + 1) * COL].rearrange("p (i d) -> p i d", i=QUAD).unsqueeze(1)
                                                .to_broadcast([P, TB, QUAD, HD1]), ALU.add)
                    ins.then_inc(s_v, 1)
                    wait(dve, s_p0, b + 1)
                    dve.tensor_tensor(rest[:, j, 0:KINDS, :], qkc[:, j, 0:KINDS, :], part[:, j, 0, 0:KINDS, :], ALU.subtract).then_inc(s_rest, 1)

                    def last_part():
                        wait(dve, s_p1, b + 1)
                        dve.tensor_tensor(part[:, j, 2, 0:KINDS, :], rest[:, j, 0:KINDS, :], part[:, j, 1, 0:KINDS, :],
                                          ALU.subtract).then_inc(s_p2, 1)

                    if not sparse:
                        last_part()
                        return
                    wait(dve, s_cov, b + 1)
                    wait(dve, s_y, b - 1)
                    dve.tensor_tensor(cov[:, j, :], cov_p[:, 0:P], block[:, :], ALU.mult).then_inc(s_covs, 1)
                    wait(dve, s_v, b + 1)
                    flat = lambda x: x.rearrange("p q t i d -> p (q t i) d")
                    vh = flat(v[:, j, :, :, :, :])[:, :, 0:HD1]
                    vp = [flat(vpart[:, j, :, :, :, :])[:, :, VW * k:VW * k + HD1] for k in range(3)]
                    vr = [flat(vrest[:, j, k, :, :, :, :]) for k in range(1)]
                    dve.tensor_copy(vp[0], vh).then_inc(s_split, 1)
                    wait(dve, s_split, 3 * b + 1)
                    dve.tensor_tensor(vr[0], vh, vp[0], ALU.subtract).then_inc(s_split, 1)
                    wait(dve, s_split, 3 * b + 2)
                    dve.tensor_copy(vp[1], vr[0]).then_inc(s_split, 1)
                    wait(dve, s_split, 3 * b + 3)
                    dve.tensor_tensor(vp[2], vr[0], vp[1], ALU.subtract).then_inc(s_vp, 1)
                    wait(dve, s_y, b + 1)
                    wait(dve, s_st, b - 1)
                    dve.tensor_tensor(z[:, j, :], y_p[:, :], qkc[:, j, 0, :], ALU.mult).then_inc(s_z, 1)
                    last_part()
                    wait(dve, s_vs, b + 1)
                    dve.tensor_copy(m.sumv[:, b, :, :], vs_p[:, :].rearrange("p (h c) -> p h c", c=COL)[:, :, 0:VW]).then_inc(s_sv, 1)
                    wait(dve, s_st, b + 1)
                    dve.tensor_scalar(m.sd[:, b, :].rearrange("p (h t) -> p t h", t=TB),
                                      st_p[:, 0:TB * HEADS].rearrange("p (t h) -> p t h", t=TB), 0.0, None,
                                      ALU.max).then_inc(s_var, 1)

                batches(dve, emit)


SLOTS = 16
TILES = QUAD * TB
ROUNDS = 4
Z0 = 1.33
AIM = KEEP - 3.5
GAINS = (0.85, 0.5, 0.3)
SLOPE = 1.0 / (S * 0.3989423 * 2.718281828 ** (-Z0 * Z0 / 2))
ROUNDER = 12582912.0
FINALS = (0, 1, 1, 2, 1, 1, 2, 1, 1, 2, 1, 1, 2, 0, 0, 0)


def search_attention(nc, m, a):
    with ExitStack() as c:
        sb = lambda n, s, d=F32: c.enter_context(nc.sbuf_tensor("se_" + n, s, d))
        pb = lambda n, s: c.enter_context(nc.psum_tensor("se_" + n, s, F32))
        sem = lambda n: nc.alloc_semaphore("se_" + n)
        STAT = 6
        VALUES, SIDE_EXP, SIDE_MASK = TB * QUAD * COL, 0, 1
        score_q = sb("score_q", [P, 2, 2, S], BF16)
        score_k = sb("score_k", [P, 2, 2, S], BF16)
        stack_q = sb("stack_q", [P, 2, 2, S], BF16)
        stack_k = sb("stack_k", [P, 2, 2, 2, S], BF16)
        vq = sb("vq", [P, 2, TB, QUAD, COL])
        vpq = sb("vpq", [P, 2, TB, QUAD, COL], BF16)
        nt = sb("nt", [P, 2, TILES])
        sd = sb("sd", [P, 2, TILES])
        cs = sb("cs", [P, 2, ROUNDS, TILES])
        err = sb("err", [P, TILES])
        sq = sb("sq", [P, TILES])
        far = sb("far", [P, TILES])
        move = sb("move", [P, TILES])
        count = sb("count", [P, 2, TILES])
        fail = sb("fail", [P, 2, TILES])
        low = sb("low", [P, 2, TILES])
        junk = sb("junk", [P, 2, S], BF16)
        one = sb("one", [P, 1])
        flags = sb("flags", [1, 1 + TILES], mybir.dt.int32)
        ranks = sb("ranks", [P, 1 + 8])
        score = sb("score", [P, 2, TILES, S])
        work = sb("work", [P, 2, S])
        ext = sb("ext", [P, 2, TILES, 1 + 8])
        top = sb("top", [P, 7, 8])
        rmax = sb("rmax", [P, 2, TILES])
        pick = sb("pick", [P, 3, TILES, 1 + 8])
        thr = sb("thr", [P, TILES])
        largest = sb("largest", [P, TILES])
        stat = sb("stat", [P, 2, TB, QUAD, 2])
        stat_rest = sb("stat_rest", [P, TB, QUAD, 2])
        stat_part = sb("stat_part", [P, TB, QUAD, 2, 3], BF16)
        statT = sb("statT", [QUAD * STAT, 2, S], BF16)
        floor = sb("floor", [P, 2, TB, QUAD])
        e = sb("e", [P, QUAD, S])
        mask = sb("mask", [P, 2, QUAD, S], BF16)
        w = sb("w", [P, 2, QUAD, S])
        u_sb = sb("u_sb", [P, 2, S])
        tot = sb("tot", [P, TB, QUAD, VW])
        tot2 = sb("tot2", [P, TB, QUAD, VW])
        zr = sb("zr", [P, TB, QUAD, 1])
        cb = pb("cb", [P, 2, S])
        db = pb("db", [P, 2, S])
        h_p = pb("h_p", [P, S])
        g_p = pb("g_p", [P, S])
        u_p = [pb(f"u_p{i}", [P, S]) for i in range(2)]
        (s_load, s_init, s_ld0, s_ld1, s_vld0, s_vld1, s_kl0, s_kl1, s_st0, s_st1, s_cu, s_cf0, s_cf1, s_cnt, s_nt, s_po, s_cfin, s_du, s_df0, s_df1, s_flag, s_fin, s_top,
         s_sel, s_sp, s_fl, s_hp, s_gp, s_exp, s_mk, s_w, s_pv, s_u, s_f, s_tok, s_pass, s_pass2, s_pass3, s_split2) = map(sem, (
             "load", "init", "ld0", "ld1", "vld0", "vld1", "kl0", "kl1", "st0", "st1", "cu", "cf0", "cf1", "cnt", "nt", "po", "cfin", "du", "df0", "df1", "flag", "fin", "top",
             "sel", "sp", "fl", "hp", "gp", "exp", "mk", "w", "pv", "u", "f", "tok", "pass", "pass2", "pass3", "split"))
        s_ld, s_kl, s_vld, s_st = (s_ld0, s_ld1), (s_kl0, s_kl1), (s_vld0, s_vld1), (s_st0, s_st1)
        s_cf, s_df = (s_cf0, s_cf1), (s_df0, s_df1)
        LD, KL = 4 * 16, 6 * 16
        TOPS = 7 + 6 + 4
        N = B * QUADS
        LAG = 1

        order = ["flag", "F0", "F1", "T"]

        def use(g, u):
            n = order.index(u)
            if isinstance(g, int) and g < 4:
                return 2 * (g - 2) + (n > 0)
            if isinstance(g, int) and g > N + 1:
                return 4 + 4 * (N - 2) + 2 * (g - N - 2) + n - 1
            return 4 + 4 * (g - 4) + n

        def half(g, u):
            n = order.index(u)
            if isinstance(g, int):
                return use(g, u) // 2, use(g, u) % 2
            return 2 + 2 * (g - 4) + n // 2, n % 2

        def to(pe, g, u):
            before, k = half(g, u)
            wait(pe, s_df[k], before)
            return db[:, k, :]

        def used(eng, g, u):
            wait(eng, s_du, use(g, u) + 1)
            return db[:, half(g, u)[1], :]

        def freed(g, u):
            return s_df[half(g, u)[1]]

        def released(eng, g, u):
            before, k = half(g, u)
            wait(eng, s_df[k], before + 1)

        scores = lambda g: not isinstance(g, int) or g < N
        counts = lambda g: not isinstance(g, int) or 1 <= g <= N
        finals = lambda g: not isinstance(g, int) or 2 <= g <= N + 1
        keys = lambda g, back: not isinstance(g, int) or 0 <= g - back < N
        unit = lambda s: (4, TILES - LAG + s) if s < LAG else (3, s - LAG)

        ends = lambda g: not isinstance(g, int) or g >= 4

        def steps(eng, emit, looped=B):
            for g in range(QUADS):
                emit(g, g, lambda back, g=g: (g - back) // QUADS)
            with eng.Fori(1, looped) as b:
                for r in range(QUADS):
                    emit(QUADS * b + r, r, lambda back, r=r: b + (r - back) // QUADS)
            for g in range(QUADS * looped, N + 4):
                emit(g, g % QUADS, lambda back, g=g: (g - back) // QUADS)

        def alike(r, batch, back):
            return QUADS // 2 * batch(0) + (r - back) // 2

        def rows_of(i, more=0):
            return slice(64 * (i % 2), 64 * (i % 2) + ROWS + more)

        with nc.Block() as blk:
            @blk.sync
            def _(sp):
                for slot in range(2):
                    for side in range(2):
                        for par in range(2):
                            sp.dma_start(stack_k[64 * par + ROWS:64 * par + ROWS + STAT, slot, side, :, :],
                                         a["c_stat2"][:, side, :, :]).then_inc(s_load, 16)
                sp.dma_start(ranks[:, :], a["c_ranks"]).then_inc(s_load, 16)

                def stacks(b, r, dests, s_done):
                    for par in range(2):
                        heads = slice(QUAD * r + par, QUAD * r + QUAD, 2)
                        for dst, kind in dests:
                            sp.dma_start(dst[64 * par:64 * par + ROWS],
                                         m.parts[b, kind, heads, :, :].rearrange("h r s -> r h s")).then_inc(s_done, 16)

                def for_scores(b, r):
                    stacks(b, r, [(score_q[:, r % 2, :, :], 0), (score_k[:, r % 2, :, :], 2)], s_ld[r % 2])

                for_scores(0, 0)

                def emit(g, r, batch):
                    p = r % 2
                    if not isinstance(g, int) or g + 1 < N:
                        wait(sp, s_cu, TILES * g)
                        sp.sem_inc(s_pass3, 1)
                        for_scores(batch(-1), (r + 1) % QUADS)
                    if finals(g):
                        q = (r - 2) % QUADS
                        wait(sp, s_hp, TILES * (g - 3))
                        wait(sp, s_gp, TILES * (g - 3))
                        sp.sem_inc(s_pass3, 1)
                        stacks(batch(2), q, [(stack_q[:, p, :, :], 0), (stack_k[:, p, SIDE_EXP, :, :], 1),
                                             (stack_k[:, p, SIDE_MASK, :, :], 2)], s_kl[p])
                        wait(sp, s_pv, TB * (g - 3))
                        sp.sem_inc(s_pass3, 1)
                        sp.dma_start(vq[:, p, :, :, :].rearrange("p t i c -> p (t i c)"), m.v_store[batch(2), q]).then_inc(s_vld[p], 16)
                        sp.dma_start(vpq[:, p, :, :, :].rearrange("p t i c -> p (t i c)"), m.vp_store[batch(2), q]).then_inc(s_vld[p], 16)
                        released(sp, g, "T")
                        for i in range(QUAD):
                            sp.dma_start(stack_q[64 * (i % 2) + ROWS:64 * (i % 2) + ROWS + STAT, p, i // 2, :],
                                         statT[STAT * i:STAT * i + STAT, p, :]).then_inc(s_st[p], 16)

                steps(sp, emit, B - 1)

            @blk.gpsimd
            def _(pool):
                pool.memset(one[:, :], 1.0).then_inc(s_init, 1)
                def emit(g, r, batch):
                    n = [0]
                    base = 37 * (g - 1) + 1
                    par = (r - 1) % 2

                    def did(ins, s_=None):
                        if s_ is None:
                            n[0] += 1
                            ins.then_inc(s_po, 1)
                        else:
                            ins.then_inc(s_, 1)

                    def wait_own():
                        wait(pool, s_po, base + n[0])
                        pool.sem_inc(s_pass, 1)

                    for s in range(SLOTS):
                        if counts(g) and s and s % 2 == 0 and s // 2 - 1 < 2 * (ROUNDS - 1):
                            block = s // 2 - 1
                            rnd, group = block // 2, block % 2
                            at = slice(8 * group, 8 * group + 8)
                            wait(pool, s_cnt, 64 * (g - 1) + 8 * (block + 1))
                            wait(pool, s_po, base + n[0])
                            pool.sem_inc(s_pass, 1)
                            did(pool.tensor_scalar(err[:, at], cs[:, par, rnd, at], 0.5, S / 2 - AIM, ALU.mult, ALU.add))
                            wait_own()
                            did(pool.tensor_tensor(sq[:, at], err[:, at], err[:, at], ALU.mult))
                            did(pool.tensor_tensor(move[:, at], err[:, at], sd[:, par, at], ALU.mult))
                            wait_own()
                            did(pool.tensor_scalar(far[:, at], sq[:, at], 12.96, -SLOPE * GAINS[rnd], ALU.is_gt, ALU.mult))
                            wait_own()
                            did(pool.tensor_tensor(err[:, at], move[:, at], far[:, at], ALU.mult))
                            wait_own()
                            did(pool.tensor_tensor(nt[:, par, at], nt[:, par, at], err[:, at], ALU.add), s_nt)
                        back, k = unit(s)
                        if keys(g, back) and k % 2 == 1:
                            ch, p = k // 4, k % 4 // 2
                            wait(pool, s_exp, TILES * (g - back) + k + 1)
                            wait(pool, s_mk, TILES * (g - back) + k + 1)
                            wait(pool, s_pv, TB * (g - back) + ch - 1)
                            pool.tensor_tensor(w[:, ch % 2, 2 * p:2 * p + 2, :], mask[:, ch % 2, 2 * p:2 * p + 2, :],
                                               e[:, 2 * p:2 * p + 2, :], ALU.mult).then_inc(s_w, 1)
                        if s == 14 and counts(g) and (not isinstance(g, int) or g < N):
                            wait(pool, s_sp, g - 1)
                            wait(pool, s_nt, 7 * (g - 1) + 7)
                            pool.sem_inc(s_pass, 1)
                            did(pool.tensor_copy(sd[:, 1 - par, :], m.sd[:, batch(0), r * TILES:(r + 1) * TILES]))
                            wait_own()
                            did(pool.tensor_scalar(nt[:, 1 - par, :], sd[:, 1 - par, :], -Z0, None, ALU.mult), s_nt)
                    if counts(g):
                        wait(pool, s_cnt, 64 * g)
                        wait(pool, s_po, base + n[0])
                        wait(pool, s_nt, 7 * (g - 1) + 7)
                        pool.sem_inc(s_pass, 1)
                        did(pool.tensor_scalar(err[:, :], cs[:, par, ROUNDS - 1, :], 0.5, S / 2 - AIM, ALU.mult, ALU.add))
                        did(pool.tensor_scalar(low[:, par, :], nt[:, par, :], 0.0, None, ALU.is_ge))
                        did(pool.tensor_scalar(count[:, par, :], cs[:, par, ROUNDS - 1, :], 0.5, S / 2 + 0.25, ALU.mult, ALU.add))
                        did(pool.tensor_scalar(ext[:, par, :, 0], nt[:, par, :], -1.0, None, ALU.mult))
                        wait_own()
                        did(pool.tensor_tensor(sq[:, :], err[:, :], err[:, :], ALU.mult))
                        did(pool.tensor_scalar(count[:, par, :], count[:, par, :], ROUNDER, -ROUNDER, ALU.add, ALU.add))
                        wait_own()
                        did(pool.tensor_scalar(fail[:, par, :], sq[:, :], 12.96, None, ALU.is_gt), s_cfin)
                        if g_last(g):
                            n[0] += 1
                        assert n[0] == 37, n[0]

                g_last = lambda g: isinstance(g, int) and g == N
                pool.tensor_copy(sd[:, 0, :], m.sd[:, 0, 0:TILES]).then_inc(s_po, 1)
                pool.wait_ge(s_po, 1)
                pool.tensor_scalar(nt[:, 0, :], sd[:, 0, :], -Z0, None, ALU.mult).then_inc(s_nt, 1)
                steps(pool, emit)

            @blk.tensor
            def _(pe):
                pe.wait_ge(s_load, 16 * 9)
                pe.wait_ge(s_init, 1)

                def emit(g, r, batch):
                    def values(ch, back):
                        q, qr = g - back, (r - back) % 2
                        if ch == 0:
                            wait(pe, s_u, 2 * q)
                            wait(pe, s_vld[qr], 32 * (alike(r, batch, back) + 1))
                        wait(pe, s_w, 8 * q + 2 * ch + 2)
                        for i in range(QUAD):
                            pe.matmul(u_p[0][COL * i:COL * i + COL, :], vq[:, qr, ch, i, :], w[:, ch % 2, i, :],
                                      start=(ch == 0), stop=(ch == TB - 1))
                        for i in range(QUAD):
                            mm = pe.matmul(u_p[1][COL * i:COL * i + COL, :], vpq[:, qr, ch, i, :], mask[:, ch % 2, i, :],
                                           start=(ch == 0), stop=(ch == TB - 1))
                        mm.then_inc(s_pv, 1)

                    tile = 0
                    for s in range(SLOTS):
                        if scores(g):
                            if s == 0:
                                wait(pe, s_ld[r % 2], LD * (alike(r, batch, 0) + 1))
                            for _ in range(FINALS[s]):
                                i, t = tile // TB, tile % TB
                                wait(pe, s_cf[tile % 2], TILES // 2 * g + tile // 2)
                                pe.matmul(cb[:, tile % 2, :], score_q[rows_of(i), r % 2, i // 2, t * P:(t + 1) * P],
                                          score_k[rows_of(i), r % 2, i // 2, :], start=True, stop=True).then_inc(s_cu, 1)
                                tile += 1
                        if finals(g) and s == 0:
                            o = to(pe, g, "flag")
                            wait(pe, s_cfin, g - 1)
                            pe.matmul(o[0:1, 0:TILES], one[:, :], fail[:, r % 2, :], start=True, stop=False)
                            pe.matmul(o[0:1, 0:TILES], one[:, :], low[:, r % 2, :], start=False, stop=True).then_inc(s_du, 1)
                        if s == LAG + 1 and ends(g):
                            values(TB - 1, 4)
                        back, k = unit(s)
                        if keys(g, back):
                            q = (r - back) % 2
                            ch, i = k // QUAD, k % QUAD
                            at = slice(ch * P, (ch + 1) * P)
                            if k == 0:
                                wait(pe, s_kl[q], KL * (alike(r, batch, 3) + 1))
                                wait(pe, s_st[q], 64 * (alike(r, batch, 3) + 1))
                            for side, dst, s_read, s_done in ((SIDE_EXP, h_p, s_exp, s_hp), (SIDE_MASK, g_p, s_mk, s_gp)):
                                wait(pe, s_read, TILES * (g - back) + k)
                                pe.matmul(dst[:, :], stack_k[rows_of(i, STAT), q, side, i // 2, at],
                                          stack_q[rows_of(i, STAT), q, i // 2, :], start=True, stop=True).then_inc(s_done, 1)
                            if i == 2 and ch >= 1:
                                values(ch - 1, back)
                        if s == 13 and ends(g):
                            for k in range(2):
                                o = to(pe, g, f"F{k}")
                                wait(pe, s_u, 2 * (g - 3))
                                for t in range(TB):
                                    mm = pe.transpose(o[:, t * P:(t + 1) * P], u_sb[:, k, t * P:(t + 1) * P], m.ident[:, :])
                                mm.then_inc(s_du, 1)
                        if s == 14 and finals(g):
                            o = to(pe, g, "T").bitcast(BF16)
                            wait(pe, s_sp, g - 1)
                            for t in range(TB):
                                mm = pe.transpose(o[0:QUAD * STAT, t * P:(t + 1) * P],
                                                  stat_part[:, t, :, :, :].rearrange("p i k j -> p (i k j)"), m.ident_b[:, :])
                            mm.then_inc(s_du, 1)

                steps(pe, emit)

            @blk.scalar
            def _(act):
                def emit(g, r, batch):
                    for s in range(SLOTS):
                        if counts(g):
                            for n in range(4 * s, 4 * s + 4):
                                rnd, group = n // 16, n // 8 % 2
                                col = 8 * group + n % 8
                                p, at = (r - 1) % 2, 64 * (g - 1) + n
                                if n % 8 == 0:
                                    wait(act, s_nt, 7 * (g - 1) + 1 + (2 * (rnd - 1) + group + 1 if rnd else 0))
                                if n in (0, 8):
                                    for k in range(2):
                                        wait(act, s_cf[k], TILES // 2 * (g - 1) + 4 * (group + 1))
                                wait(act, s_cnt, at - 1)
                                act.activation(junk[:, n % 2, :], score[:, p, col, :], ACT.Sign, bias=nt[:, p, col:col + 1],
                                               accum_out=cs[:, p, rnd, col:col + 1]).then_inc(s_cnt, 1)
                        back, k = unit(s)
                        if keys(g, back):
                            ch, i = k // QUAD, k % QUAD
                            wait(act, s_hp, TILES * (g - back) + k + 1)
                            wait(act, s_w, 8 * (g - back) + 2 * ch + i // 2 - 1)
                            act.activation(e[:, i, :], h_p[:, :], ACT.Exp).then_inc(s_exp, 1)
                        if s == 15 and finals(g):
                            q = r % 2
                            wait(act, s_sp, g - 1)
                            wait(act, s_tok, g - 3)
                            act.activation(floor[:, q, :, :], stat[:, q, :, :, 1], ACT.Exp).then_inc(s_fl, 1)

                steps(act, emit)

            @blk.vector
            def _(dve):
                dve.wait_ge(s_load, 16 * 9)

                SUMS_AT = LAG + 3

                def carry():
                    dve.sem_inc(s_pass2, 1)

                def copy(g, p, j):
                    wait(dve, s_cu, TILES * g + j + 1)
                    carry()
                    dve.tensor_scalar(score[:, p, j, :], cb[:, j % 2, :], 1.0, LOW, ALU.mult, ALU.max,
                                      accum_out=rmax[:, p, j:j + 1]).then_inc(s_cf[j % 2], 1)

                def middle(g, r, batch, general):
                    q = r % 2
                    base = 2 * TILES * (g - 2)

                    def below(j):
                        dve.scalar_tensor_tensor(work[:, j % 2, :], score[:, q, j, :], ext[:, q, j, 0:1], score[:, q, j, :],
                                                 ALU.is_lt, ALU.mult).then_inc(s_fin, 1)

                    def eight(j):
                        wait(dve, s_fin, base + (2 * j + 1 if general else max(2 * j, 1)))
                        carry()
                        dve.max(ext[:, q, j, 1:9], work[:, j % 2, :]).then_inc(s_fin, 1)

                    def take_out(j):
                        n = [0]

                        def did(ins):
                            n[0] += 1
                            ins.then_inc(s_top, 1)

                        def wait_own():
                            wait(dve, s_top, TOPS * (TILES * (g - 2) + j) + n[0])
                            carry()

                        wait(dve, s_fin, base + 2 * j + 2)
                        for k in range(7):
                            wait_own()
                            did(dve.max(top[:, k, :], score[:, q, j, :]))
                            if k < 6:
                                wait_own()
                                did(dve.match_replace(score[:, q, j, :], top[:, k, :], score[:, q, j, :], LOW))
                        wait_own()
                        last = KEEP - 1 - 48
                        did(dve.tensor_copy(ext[:, q, j, 0:2], top[:, 6, last:last + 2]))
                        did(dve.memset(count[:, q, j:j + 1], float(KEEP)))
                        n[0] += 2
                        dve.sem_inc(s_top, 2)

                    tile = 0
                    for s in range(1, 13):
                        for _ in range(FINALS[s]):
                            if general:
                                below(tile)
                                eight(tile)
                                flag = dve.value_load(flags[0:1, 1 + tile:2 + tile], min_val=0, max_val=2 * P)
                                with dve.If(flag > 0):
                                    take_out(tile)
                                with dve.Else():
                                    dve.sem_inc(s_top, TOPS)
                                wait(dve, s_top, TOPS * (TILES * (g - 2) + tile + 1))
                                wait(dve, s_fin, base + 2 * tile + 2)
                            else:
                                if tile >= 2:
                                    wait(dve, s_fin, base + 2 * tile - 1)
                                below(tile)
                                if tile:
                                    eight(tile - 1)
                                wait(dve, s_fin, base + max(2 * tile, 1))
                            if scores(g):
                                copy(g, q, tile)
                            tile += 1
                        if s == SUMS_AT and ends(g):
                            sums(g)
                        masks(g, s)
                    if not general:
                        eight(TILES - 1)
                        dve.sem_inc(s_top, TOPS * TILES)

                def masks(g, s):
                    back, k = unit(s)
                    if not keys(g, back):
                        return
                    ch, i = k // QUAD, k % QUAD
                    wait(dve, s_gp, TILES * (g - back) + k + 1)
                    wait(dve, s_pv, TB * (g - back) + ch - 1)
                    dve.tensor_scalar(mask[:, ch % 2, i, :], g_p[:, :], 0.0, None, ALU.is_ge).then_inc(s_mk, 1)

                def emit(g, r, batch):
                    q = r % 2
                    masks(g, 0)
                    if not finals(g):
                        tile = 0
                        for s in range(1, 13):
                            for _ in range(FINALS[s] if scores(g) else 0):
                                copy(g, q, tile)
                                tile += 1
                            if s == SUMS_AT and ends(g):
                                sums(g)
                            masks(g, s)
                    if finals(g):
                        n = [0]

                        def did(ins):
                            n[0] += 1
                            ins.then_inc(s_sel, 1)

                        def wait_own():
                            wait(dve, s_sel, 9 * (g - 2) + n[0])

                        o = used(dve, g, "flag")
                        dve.tensor_copy(flags[:, 1:], o[0:1, 0:TILES]).then_inc(s_flag, 1)
                        dve.tensor_reduce(flags[:, 0:1], o[0:1, 0:TILES], AX.X, ALU.max).then_inc(freed(g, "flag"), 1)
                        released(dve, g, "flag")
                        wait_own()
                        for k in range(2):
                            wait(dve, s_cf[k], TILES // 2 * (g - 1))
                        at = (r - 2) % QUADS * TILES
                        did(dve.tensor_tensor(largest[:, :], rmax[:, q, :], m.mean[:, batch(2), at:at + TILES], ALU.add))
                        wait_own()
                        wait(dve, s_flag, g - 1)
                        wait(dve, s_cfin, g - 1)
                        carry()
                        any_flag = dve.value_load(flags[0:1, 0:1], min_val=0, max_val=2 * P)
                        with dve.If(any_flag > 0):
                            middle(g, r, batch, True)
                        with dve.Else():
                            middle(g, r, batch, False)
                        wait(dve, s_fin, 2 * TILES * (g - 1))
                        wait(dve, s_top, TOPS * TILES * (g - 1))
                        did(dve.tensor_tensor(pick[:, 0, :, :], ranks[:, :].unsqueeze(1).to_broadcast([P, TILES, 9]),
                                              count[:, q, :].unsqueeze(2).to_broadcast([P, TILES, 9]), ALU.add))
                        wait_own()
                        did(dve.scalar_tensor_tensor(pick[:, 1, :, :], pick[:, 0, :, :], KEEP - 0.25, ext[:, q, :, :], ALU.is_gt, ALU.mult))
                        wait_own()
                        did(dve.scalar_tensor_tensor(pick[:, 2, :, :], pick[:, 0, :, :], KEEP + 1.25, pick[:, 1, :, :], ALU.is_lt, ALU.mult))
                        wait_own()
                        did(dve.tensor_reduce(thr[:, :], pick[:, 2, :, :], AX.X, ALU.add))
                        wait_own()
                        st, sr = stat[:, q, :, :, :], stat_rest[:, :, :, :]
                        wait(dve, s_fl, g - 3)
                        dve.tensor_scalar(stat[:, q, :, :, 0].rearrange("p t i -> p i t"), thr[:, :].rearrange("p (i t) -> p i t", t=TB),
                                          -0.5, None, ALU.mult).then_inc(s_sel, 1)
                        dve.tensor_scalar(stat[:, q, :, :, 1].rearrange("p t i -> p i t"), largest[:, :].rearrange("p (i t) -> p i t", t=TB),
                                          0.0, -1.0, ALU.max, ALU.mult).then_inc(s_sel, 1)
                        n[0] += 2
                        wait_own()
                        if not isinstance(g, int) or g >= 3:
                            wait(dve, s_du, use(g - 1, "T") + 1)
                        pt = [stat_part[:, :, :, :, k] for k in range(3)]
                        did(dve.tensor_copy(pt[0], st))
                        wait_own()
                        did(dve.tensor_tensor(sr, st, pt[0], ALU.subtract))
                        wait_own()
                        dve.tensor_copy(pt[1], sr).then_inc(s_split2, 1)
                        wait(dve, s_split2, g - 1)
                        dve.tensor_tensor(pt[2], sr, pt[1], ALU.subtract).then_inc(s_sp, 1)
                    masks(g, 13)
                    if ends(g):
                        finish(g, r, batch)
                    masks(g, 14)
                    masks(g, 15)
                    if finals(g):
                        o = used(dve, g, "T").bitcast(BF16)
                        wait(dve, s_st[q], 64 * alike(r, batch, 2))
                        dve.tensor_copy(statT[:, q, :], o[0:QUAD * STAT, 0:S]).then_inc(freed(g, "T"), 1)

                def sums(g):
                    wait(dve, s_pv, TB * (g - 3))
                    if not isinstance(g, int) or g >= 5:
                        wait(dve, s_du, use(g - 1, "F1") + 1)
                    dve.tensor_copy(u_sb[:, 0, :], u_p[0][:, :]).then_inc(s_u, 1)
                    dve.tensor_copy(u_sb[:, 1, :], u_p[1][:, :]).then_inc(s_u, 1)

                def finish(g, r, batch):
                    n = [0]
                    q = (r - 4) % QUADS

                    def did(ins):
                        n[0] += 1
                        ins.then_inc(s_f, 1)

                    def wait_own():
                        wait(dve, s_f, 5 * (g - 4) + n[0])

                    parts = lambda x: x.rearrange("p (t i c) -> p t i c", t=TB, i=QUAD)
                    uT = parts(used(dve, g, "F0"))
                    mT = parts(used(dve, g, "F1"))
                    did(dve.tensor_copy(tot[:, :, :, :], mT[:, :, :, 0:VW]))
                    wait_own()
                    did(dve.tensor_tensor(tot2[:, :, :, :], mT[:, :, :, VW:2 * VW], tot[:, :, :, :], ALU.add))
                    wait_own()
                    dve.tensor_tensor(tot[:, :, :, :], mT[:, :, :, 2 * VW:3 * VW], tot2[:, :, :, :], ALU.add).then_inc(freed(g, "F1"), 1)
                    released(dve, g, "F1")
                    sv = m.sumv[:, batch(4), QUAD * q:QUAD * (q + 1), :].unsqueeze(1).to_broadcast([P, TB, QUAD, VW])
                    did(dve.tensor_tensor(tot2[:, :, :, :], sv, tot[:, :, :, :], ALU.subtract))
                    wait_own()
                    wait(dve, s_fl, g - 3)
                    fl = floor[:, (r - 4) % 2, :, :].unsqueeze(3).to_broadcast([P, TB, QUAD, VW])
                    did(dve.tensor_tensor(tot[:, :, :, :], tot2[:, :, :, :], fl, ALU.mult))
                    wait_own()
                    dve.tensor_tensor(tot2[:, :, :, :], uT[:, :, :, 0:VW], tot[:, :, :, :], ALU.add).then_inc(freed(g, "F0"), 1)
                    released(dve, g, "F0")
                    did(dve.reciprocal(zr[:, :, :, :], tot2[:, :, :, HD1:VW]))
                    wait_own()
                    dst = m.attn[:, batch(4), :, q * COL:(q + 1) * COL].rearrange("p t (i d) -> p t i d", d=HD1)
                    dve.tensor_tensor(dst, tot2[:, :, :, 0:HD1], zr[:, :, :, :].to_broadcast([P, TB, QUAD, HD1]),
                                      ALU.mult).then_inc(s_tok, 1)
                    wait(dve, s_tok, g - 3)

                steps(dve, emit)


def dense_attention(nc, m, a):
    with ExitStack() as c:
        sb = lambda n, s, d=F32: c.enter_context(nc.sbuf_tensor("dn_" + n, s, d))
        pb = lambda n, s: c.enter_context(nc.psum_tensor("dn_" + n, s, F32))
        sem = lambda n: nc.alloc_semaphore("dn_" + n)
        STAT, SLOTS8, PAIR = 3, 8, 2
        stack_q = sb("stack_q", [P, 4, 2, S], BF16)
        stack_k = sb("stack_k", [P, 4, 2, S], BF16)
        vq = sb("vq", [P, 2, TB, QUAD, COL])
        stat = sb("stat", [P, 2, TB, QUAD])
        stat_rest = sb("stat_rest", [P, TB, QUAD])
        stat_part = sb("stat_part", [P, TB, QUAD, 3], BF16)
        statT = sb("statT", [QUAD * STAT, 2, S], BF16)
        e = sb("e", [P, 2, QUAD, S])
        u_sb = sb("u_sb", [P, S])
        zr = sb("zr", [P, TB, QUAD, 1])
        s_p = pb("s_p", [P, 2, S])
        h_p = pb("h_p", [P, 2, PAIR, S])
        u_p = pb("u_p", [P, S])
        f_p = pb("f_p", [P, S])
        (s_load, s_ld0, s_ld1, s_vld0, s_vld1, s_st0, s_st1, s_sc, s_max0, s_max1, s_sp, s_split, s_T, s_Tc, s_hp, s_exp,
         s_pv, s_u, s_F, s_zr, s_tok, s_pass) = map(sem, (
             "load", "ld0", "ld1", "vld0", "vld1", "st0", "st1", "sc", "max0", "max1", "sp", "split", "T", "Tc", "hp", "exp",
             "pv", "u", "F", "zr", "tok", "pass"))
        s_ld, s_vld, s_st, s_max = (s_ld0, s_ld1), (s_vld0, s_vld1), (s_st0, s_st1), (s_max0, s_max1)
        LD = 4 * 16
        N = B * QUADS

        maxima = lambda g: not isinstance(g, int) or g < N
        turns = lambda g: not isinstance(g, int) or 1 <= g <= N
        keys = lambda g: not isinstance(g, int) or 2 <= g <= N + 1
        ends = lambda g: not isinstance(g, int) or g >= 3

        def steps(eng, emit, looped=B):
            for g in range(QUADS):
                emit(g, g, lambda back, g=g: (g - back) // QUADS)
            with eng.Fori(1, looped) as b:
                for r in range(QUADS):
                    emit(QUADS * b + r, r, lambda back, r=r: b + (r - back) // QUADS)
            for g in range(QUADS * looped, N + 3):
                emit(g, g % QUADS, lambda back, g=g: (g - back) // QUADS)

        def alike(r, batch, back):
            return QUADS // 2 * batch(0) + (r - back) // 2

        def rows_of(i, more=0):
            return slice(64 * (i % 2), 64 * (i % 2) + ROWS + more)

        with nc.Block() as blk:
            @blk.sync
            def _(sp):
                for slot in range(4):
                    for par in range(2):
                        sp.dma_start(stack_k[64 * par + ROWS:64 * par + ROWS + STAT, slot, :, :],
                                     a["c_stat1"][:, 0, :, :]).then_inc(s_load, 16)

                def stacks(b, r):
                    for par in range(2):
                        heads = slice(QUAD * r + par, QUAD * r + QUAD, 2)
                        rows = slice(64 * par, 64 * par + ROWS)
                        for kind, stack in ((0, stack_q), (1, stack_k)):
                            sp.dma_start(stack[rows, r, :, :],
                                         m.parts[b, kind, heads, :, :].rearrange("h r s -> r h s")).then_inc(s_ld[r % 2], 16)

                stacks(0, 0)

                def emit(g, r, batch):
                    odd = (r - 1) % 2
                    if not isinstance(g, int) or g + 1 < N:
                        wait(sp, s_hp, SLOTS8 * (g - 2))
                        wait(sp, s_sc, TILES * (g - 1) + 1)
                        sp.sem_inc(s_pass, 1)
                        stacks(batch(-1), (r + 1) % QUADS)
                    if turns(g):
                        wait(sp, s_pv, TB * (g - 2))
                        sp.sem_inc(s_pass, 1)
                        q = (r - 1) % QUADS
                        sp.dma_start(vq[:, odd, :, :, :].rearrange("p t i c -> p (t i c)"), m.v_store[batch(1), q]).then_inc(s_vld[odd], 16)
                        wait(sp, s_Tc, g)
                        for i in range(QUAD):
                            sp.dma_start(stack_q[64 * (i % 2) + ROWS:64 * (i % 2) + ROWS + STAT, q, i // 2, :],
                                         statT[STAT * i:STAT * i + STAT, odd, :]).then_inc(s_st[odd], 16)

                steps(sp, emit, B - 1)

            @blk.tensor
            def _(pe):
                pe.wait_ge(s_load, 16 * 8)

                def emit(g, r, batch):
                    def values(ch, back):
                        q, qr = g - back, (r - back) % 2
                        if ch == 0:
                            wait(pe, s_u, q)
                            wait(pe, s_vld[qr], 16 * (alike(r, batch, back) + 1))
                        wait(pe, s_exp, SLOTS8 * q + 2 * ch + 2)
                        for i in range(QUAD):
                            mm = pe.matmul(u_p[COL * i:COL * i + COL, :], vq[:, qr, ch, i, :], e[:, ch % 2, i, :],
                                           start=(ch == 0), stop=(ch == TB - 1))
                        mm.then_inc(s_pv, 1)

                    for s in range(SLOTS8):
                        if keys(g):
                            q = (r - 2) % QUADS
                            ch, p = s // 2, s % 2
                            if s == 0:
                                wait(pe, s_st[r % 2], 64 * (alike(r, batch, 2) + 1))
                            wait(pe, s_exp, SLOTS8 * (g - 2) + s - 1)
                            for par in range(2):
                                mm = pe.matmul(h_p[:, s % 2, par, :], stack_k[rows_of(par, STAT), q, p, ch * P:(ch + 1) * P],
                                               stack_q[rows_of(par, STAT), q, p, :], start=True, stop=True)
                            mm.then_inc(s_hp, 1)
                        if maxima(g):
                            if s == 0:
                                wait(pe, s_ld[r % 2], LD * (alike(r, batch, 0) + 1))
                            for n in (2 * s, 2 * s + 1):
                                i, t = n // TB, n % TB
                                wait(pe, s_max[n % 2], TILES // 2 * g + n // 2)
                                pe.matmul(s_p[:, n % 2, :], stack_q[rows_of(i), r, i // 2, t * P:(t + 1) * P],
                                          stack_k[rows_of(i), r, i // 2, :], start=True, stop=True).then_inc(s_sc, 1)
                        if s == 0 and ends(g):
                            values(TB - 1, 3)
                        if keys(g) and s % 2 == 0 and s:
                            values(s // 2 - 1, 2)
                        if s == 3 and turns(g):
                            wait(pe, s_sp, g)
                            wait(pe, s_tok, g - 3)
                            o = f_p[:, :].bitcast(BF16)
                            for t in range(TB):
                                mm = pe.transpose(o[0:QUAD * STAT, t * P:(t + 1) * P],
                                                  stat_part[:, t, :, :].rearrange("p i j -> p (i j)"), m.ident_b[:, :])
                            mm.then_inc(s_T, 1)
                        if s == 6 and ends(g):
                            wait(pe, s_u, g - 2)
                            if not isinstance(g, int) or g <= N:
                                wait(pe, s_Tc, g)
                            else:
                                wait(pe, s_tok, g - 3)
                            for t in range(TB):
                                mm = pe.transpose(f_p[:, t * P:(t + 1) * P], u_sb[:, t * P:(t + 1) * P], m.ident[:, :])
                            mm.then_inc(s_F, 1)

                steps(pe, emit)

            @blk.scalar
            def _(act):
                def emit(g, r, batch):
                    for s in range(SLOTS8):
                        if s == 1 and ends(g):
                            wait(act, s_pv, TB * (g - 2))
                            wait(act, s_F, g - 3)
                            act.activation(u_sb[:, :], u_p[:, :], ACT.Copy).then_inc(s_u, 1)
                        if keys(g):
                            ch, p = s // 2, s % 2
                            wait(act, s_hp, SLOTS8 * (g - 2) + s + 1)
                            wait(act, s_pv, TB * (g - 2) + ch - 1)
                            act.activation(e[:, ch % 2, 2 * p:2 * p + 2, :], h_p[:, s % 2, :, :], ACT.Exp).then_inc(s_exp, 1)
                        if s == 4 and turns(g):
                            q = (r - 1) % 2
                            wait(act, s_T, g)
                            wait(act, s_st[q], 64 * alike(r, batch, 1))
                            act.activation(statT[:, q, :], f_p[:, :].bitcast(BF16)[0:QUAD * STAT, 0:S], ACT.Copy).then_inc(s_Tc, 1)

                steps(act, emit)

            @blk.vector
            def _(dve):
                dve.wait_ge(s_load, 16 * 8)

                def emit(g, r, batch):
                    for s in range(SLOTS8):
                        if maxima(g):
                            for n in (2 * s, 2 * s + 1):
                                i, t = n // TB, n % TB
                                wait(dve, s_sc, TILES * g + n + 1)
                                wait(dve, s_sp, g - 1)
                                dve.tensor_reduce(stat[:, r % 2, t, i:i + 1], s_p[:, n % 2, :], AX.X, ALU.max,
                                                  negate=True).then_inc(s_max[n % 2], 1)
                        if turns(g) and s < 3:
                            st, sr = stat[:, (r - 1) % 2, :, :], stat_rest[:, :, :]
                            pt = [stat_part[:, :, :, k] for k in range(3)]
                            if s == 0:
                                for k in range(2):
                                    wait(dve, s_max[k], TILES // 2 * g)
                                wait(dve, s_T, g - 1)
                                dve.tensor_copy(pt[0], st).then_inc(s_split, 1)
                                wait(dve, s_split, 3 * (g - 1) + 1)
                                dve.tensor_tensor(sr, st, pt[0], ALU.subtract).then_inc(s_split, 1)
                            if s == 1:
                                wait(dve, s_split, 3 * (g - 1) + 2)
                                dve.tensor_copy(pt[1], sr).then_inc(s_split, 1)
                            if s == 2:
                                wait(dve, s_split, 3 * g)
                                dve.tensor_tensor(pt[2], sr, pt[1], ALU.subtract).then_inc(s_sp, 1)
                        if s == 7 and ends(g):
                            q = (r - 3) % QUADS
                            wait(dve, s_F, g - 2)
                            wait(dve, s_tok, g - 3)
                            uT = f_p[:, :].rearrange("p (t i c) -> p t i c", t=TB, i=QUAD)
                            dve.reciprocal(zr[:, :, :, :], uT[:, :, :, HD1:VW]).then_inc(s_zr, 1)
                            wait(dve, s_zr, g - 2)
                            dst = m.attn[:, batch(3), :, q * COL:(q + 1) * COL].rearrange("p t (i d) -> p t i d", d=HD1)
                            dve.tensor_tensor(dst, uT[:, :, :, 0:HD1], zr[:, :, :, :].to_broadcast([P, TB, QUAD, HD1]),
                                              ALU.mult).then_inc(s_tok, 1)

                steps(dve, emit)


def attention_out(nc, m, a):
    with ExitStack() as c:
        sb = lambda n, s, d=F32: c.enter_context(nc.sbuf_tensor("ao_" + n, s, d))
        sem = lambda n: nc.alloc_semaphore("ao_" + n)
        w_o, bo = sb("w_o", [P, P]), sb("bo", [P, 1])
        aT, y = sb("aT", [P, 2, S]), sb("y", [P, 2, S])
        at_p = c.enter_context(nc.psum_tensor("ao_at_p", [P, 2, S], F32))
        y_p = c.enter_context(nc.psum_tensor("ao_y_p", [P, 2, S], F32))
        s_load, s_t, s_aT, s_mm, s_y = (sem(n) for n in ("load", "t", "aT", "mm", "y"))
        with nc.Block() as blk:
            @blk.sync
            def _(sp):
                sp.dma_start(w_o[:, :], a["L1_attn_Wo"]).then_inc(s_load, 16)
                sp.dma_start(bo[:, :], a["L1_attn_bo"].rearrange("(p o) -> p o", o=1)).then_inc(s_load, 16)

            @blk.tensor
            def _(pe):
                pe.wait_ge(s_load, 32)

                def turn(b):
                    if b >= 2:
                        pe.wait_ge(s_aT, b - 1)
                    for t in range(TB):
                        mm = pe.transpose(at_p[:, b % 2, t * P:(t + 1) * P], m.attn[:, b, t, :], m.ident[:, :])
                    mm.then_inc(s_t, 1)

                turn(0)
                for b in range(B):
                    if b + 1 < B:
                        turn(b + 1)
                    pe.wait_ge(s_aT, b + 1)
                    if b >= 2:
                        pe.wait_ge(s_y, b - 1)
                    pe.matmul(y_p[:, b % 2, :], w_o[:, :], aT[:, b % 2, :], start=True, stop=True).then_inc(s_mm, 1)

            @blk.scalar
            def _(act):
                for b in range(B):
                    act.wait_ge(s_t, b + 1)
                    if b >= 2:
                        act.wait_ge(s_mm, b - 1)
                    act.activation(aT[:, b % 2, :], at_p[:, b % 2, :], ACT.Copy).then_inc(s_aT, 1)

            @blk.vector
            def _(dve):
                dve.wait_ge(s_load, 32)
                for b in range(B):
                    dve.wait_ge(s_mm, b + 1)
                    dve.tensor_scalar(y[:, b % 2, :], y_p[:, b % 2, :], bo[:, 0:1], m.mod[:, 1, GATE, b:b + 1], ALU.add,
                                      ALU.mult).then_inc(s_y, 1)
                    dve.wait_ge(s_y, b + 1)
                    dve.tensor_tensor(m.xT[:, b, :], m.xT[:, b, :], y[:, b % 2, :], ALU.add)


def experts(nc, m, a, gelu):
    tag = "ge_" if gelu else "li_"
    layer = 0 if gelu else 1
    with ExitStack() as c:
        sb = lambda n, s, d=F32: c.enter_context(nc.sbuf_tensor(tag + n, s, d))
        pb = lambda n, s: c.enter_context(nc.psum_tensor(tag + n, s, F32))
        sem = lambda n: nc.alloc_semaphore(tag + n)
        hs = sb("hs", [P, 2, S])
        lg = sb("lg", [P, TB, EX])
        m8 = sb("m8", [P, TB, 8])
        sh = sb("sh", [P, TB, EX])
        ex = sb("ex", [P, TB, EX])
        mk = sb("mk", [P, TB, EX])
        exm = sb("exm", [P, TB, EX])
        tot = sb("tot", [P, TB])
        inv = sb("inv", [P, TB])
        share = sb("share", [P, 2, TB, EX])
        acc = sb("acc", [P, 2, TB, P])
        STAGE = EX if gelu else 2
        if gelu:
            w1 = sb("w1", [P, EX, FF])
            w2 = sb("w2", [P, EX, 2, P])
            act_ = sb("act", [P, 2, 2, S])
            gate_w = m.small_T[:, 2, :]
            up_p = pb("up_p", [P, 2, 2, S])
            loads = [(w1[:, :, :], a["L0_ffn_w1"].rearrange("e p f -> p e f")),
                     ] + [(w2[:, :, k, :], a["L0_ffn_w2"][:, k * P:(k + 1) * P, :].rearrange("e p f -> p e f")) for k in range(2)]
            NOUT = EX
        else:
            wexp = sb("wexp", [P, EX, P])
            gw = sb("gw", [P, EX])
            gb = sb("gb", [P, EX])
            bexp = sb("bexp", [EX, P])
            shareT = sb("shareT", [EX, S])
            gate_w = gw[:, :]
            loads = [(wexp[:, :, :], a["L1_ffn_W_experts"].rearrange("e p f -> p e f")),
                     (gw[:, :], a["L1_ffn_W_gate"]), (bexp[:, :], a["L1_ffn_b_experts"]),
                     (gb[:, :], a["L1_ffn_b_gate"].rearrange("(o d) -> o d", o=1).to_broadcast([P, EX]))]
            NOUT = 2 * TB
        OUTS = 2 if gelu else 4
        out_p = pb("out_p", [P, OUTS, S])
        lg_p = pb("lg_p", [P, S])
        y_p = pb("y_p", [P, S])
        (s_load, s_hs, s_lg, s_out, s_g, s_ex, s_acc, s_tr, s_x, s_norm, s_pass) = map(
            sem, ("load", "hs", "lg", "out", "g", "ex", "acc", "tr", "x", "norm", "pass"))
        if gelu:
            s_up, s_act = sem("up"), sem("act")
        else:
            s_sh, s_shT = sem("sh"), sem("shT")
        G = 9 if gelu else 10
        ACC = EX * TB

        def batches(eng, emit):
            for j in range(2):
                emit(j, j)
            with eng.Fori(1, B // 2 - 1) as i:
                for j in range(2):
                    emit(2 * i + j, j)
            for j in range(2):
                emit(B - 2 + j, j)

        more = lambda b: not isinstance(b, int) or b + 1 < B
        block_of = lambda u: (2 * (u // 4) + u % 2, u // 2 % 2)

        with nc.Block() as block:
            @block.sync
            def _(sp):
                for dst, src in loads:
                    sp.dma_start(dst, src).then_inc(s_load, 16)

            @block.gpsimd
            def _(pool):
                def emit(b, j):
                    wait(pool, s_out, NOUT * (b - 1))
                    pool.tensor_copy(hs[:, j, :], m.hT[:, b, WINDOW:]).then_inc(s_hs, 1)

                batches(pool, emit)

            @block.tensor
            def _(pe):
                pe.wait_ge(s_load, 16 * len(loads))

                def logits(b, j):
                    wait(pe, s_hs, b + 1)
                    wait(pe, s_g, G * b)
                    if not gelu:
                        wait(pe, s_shT, b - 1)
                    for t in range(TB):
                        mm = pe.matmul(lg_p[:, t * EX:(t + 1) * EX], hs[:, j, t * P:(t + 1) * P], gate_w,
                                       start=True, stop=True)
                    mm.then_inc(s_lg, 1)

                def finish(b, j):
                    if not gelu:
                        wait(pe, s_g, G * (b + 1))
                        for t in range(TB):
                            mm = pe.transpose(lg_p[0:EX, t * P:(t + 1) * P], share[:, j, t, :], m.ident[:, :])
                        mm.then_inc(s_sh, 1)
                    wait(pe, s_acc, ACC * (b + 1))
                    wait(pe, s_x, b)
                    for t in range(TB):
                        mm = pe.matmul(y_p[:, t * P:(t + 1) * P], acc[:, j, t, :], m.ident[:, :],
                                       start=True, stop=gelu)
                        if not gelu:
                            if t == 0:
                                wait(pe, s_shT, b + 1)
                            mm = pe.matmul(y_p[:, t * P:(t + 1) * P], bexp[:, :], shareT[:, t * P:(t + 1) * P],
                                           start=False, stop=True)
                    mm.then_inc(s_tr, 1)

                def between(b, j):
                    if not isinstance(b, int) or b >= 1:
                        finish(b - 1, 1 - j)
                    if more(b):
                        logits(b + 1, 1 - j)

                def emit(b, j):
                    if gelu:
                        def up(e):
                            n = EX * b + e
                            wait(pe, s_act, n - 1)
                            for k in range(2):
                                mm = pe.matmul(up_p[:, e % 2, k, :], w1[:, e, k * P:(k + 1) * P], hs[:, j, :],
                                               start=True, stop=True)
                            mm.then_inc(s_up, 1)

                        up(0)
                        for e in range(EX):
                            n = EX * b + e
                            if e + 1 < EX:
                                up(e + 1)
                            wait(pe, s_act, n + 1)
                            wait(pe, s_acc, ACC * b + TB * (e - 1))
                            for t in range(TB):
                                for k in range(2):
                                    mm = pe.matmul(out_p[:, e % 2, t * P:(t + 1) * P], act_[:, e % 2, k, t * P:(t + 1) * P],
                                                   w2[:, e, k, :], start=(k == 0), stop=(k == 1))
                            mm.then_inc(s_out, 1)
                            if e == 0:
                                between(b, j)
                    else:
                        for u in range(NOUT):
                            t, k = block_of(u)
                            wait(pe, s_acc, ACC * b + EX * ((u - OUTS) // 2 + 1))
                            pe.matmul(out_p[:, u % OUTS, :], hs[:, j, t * P:(t + 1) * P],
                                      wexp[:, 4 * k:4 * k + 4, :].rearrange("p e f -> p (e f)"),
                                      start=True, stop=True).then_inc(s_out, 1)
                            if u == 2:
                                between(b, j)

                logits(0, 0)
                batches(pe, emit)
                finish(B - 1, 1)

            @block.scalar
            def _(act):
                def exps(b):
                    wait(act, s_g, G * b + (6 if gelu else 7))
                    act.activation(ex[:, :, :], sh[:, :, :], ACT.Exp).then_inc(s_ex, 1)

                def emit(b, j):
                    if gelu:
                        for e in range(EX):
                            n = EX * b + e
                            wait(act, s_up, n + 1)
                            wait(act, s_out, n - 1)
                            act.activation(act_[:, e % 2, :, :], up_p[:, e % 2, :, :], ACT.Gelu).then_inc(s_act, 1)
                            if e == 3 and more(b):
                                exps(b + 1)
                    else:
                        if not isinstance(b, int) or b >= 1:
                            turned(b - 1)
                        if more(b):
                            exps(b + 1)

                def turned(b):
                    wait(act, s_sh, b + 1)
                    wait(act, s_tr, b)
                    act.activation(shareT[:, :], lg_p[0:EX, :], ACT.Copy).then_inc(s_shT, 1)

                exps(0)
                batches(act, emit)
                if not gelu:
                    turned(B - 1)

            @block.vector
            def _(dve):
                dve.wait_ge(s_load, 16 * len(loads))
                flat = lambda x: x[:, :, :].rearrange("p t e -> p (t e)")

                def own(b, n):
                    wait(dve, s_g, G * b + n)

                def gate(b, j, k):
                    n = 1 if gelu else 2
                    if k == 0:
                        wait(dve, s_lg, b + 1)
                        dve.tensor_copy(flat(lg), lg_p[:, 0:TB * EX]).then_inc(s_g, 1)
                    if k == 1 and not gelu:
                        own(b, 1)
                        dve.tensor_tensor(lg[:, :, :], lg[:, :, :], gb[:, :].unsqueeze(1).to_broadcast([P, TB, EX]),
                                          ALU.add).then_inc(s_g, 1)
                    if k == 2:
                        own(b, n)
                        dve.sem_inc(s_pass, 1)
                        for t in range(TB):
                            dve.max(m8[:, t, :], lg[:, t, :]).then_inc(s_g, 1)
                    if k == 3:
                        own(b, n + 4)
                        dve.tensor_tensor(sh[:, :, :], lg[:, :, :], m8[:, :, 0:1].to_broadcast([P, TB, EX]), ALU.subtract).then_inc(s_g, 1)
                        dve.tensor_tensor(mk[:, :, :], lg[:, :, :], m8[:, :, 1:2].to_broadcast([P, TB, EX]), ALU.is_ge).then_inc(s_g, 1)
                    if k == 4:
                        own(b, n + 6)
                        wait(dve, s_ex, b + 1)
                        dve.tensor_tensor(exm[:, :, :], ex[:, :, :], mk[:, :, :], ALU.mult).then_inc(s_g, 1)
                    if k == 5:
                        own(b, n + 7)
                        dve.tensor_reduce(tot[:, :], (exm if gelu else ex)[:, :, :], AX.X, ALU.add).then_inc(s_norm, 1)
                    if k == 6:
                        wait(dve, s_norm, 2 * b + 1)
                        dve.reciprocal(inv[:, :], tot[:, :]).then_inc(s_norm, 1)
                    if k == 7:
                        wait(dve, s_norm, 2 * b + 2)
                        if not gelu:
                            wait(dve, s_sh, b - 1)
                        dve.tensor_tensor(share[:, j, :, :], exm[:, :, :], inv[:, :].unsqueeze(2).to_broadcast([P, TB, EX]),
                                          ALU.mult).then_inc(s_g, 1)

                def add(b, j):
                    wait(dve, s_tr, b + 1)
                    dve.scalar_tensor_tensor(m.xT[:, b, :], y_p[:, :], m.mod[:, layer, 3 + GATE, bass.ds(b, 1)], m.xT[:, b, :],
                                             ALU.mult, ALU.add).then_inc(s_x, 1)

                if gelu:
                    order = [(e, e, t) for e in range(EX) for t in range(TB)]
                    GATE_AT = (4, 6, 8, 10, 22, 24, 26, 28)
                else:
                    order = [(4 * (t0 // 2) + 2 * k + t % 2, 4 * k + e, t) for t0 in (0, 2) for k in range(2)
                             for e in range(4) for t in (t0, t0 + 1)]
                    GATE_AT = (10, 12, 14, 16, 22, 24, 26, 28)

                def emit(b, j):
                    own(b, G)
                    last = {}
                    for n, (use, e, t) in enumerate(order):
                        if n in GATE_AT and more(b):
                            gate(b + 1, 1 - j, GATE_AT.index(n))
                        if n == 20:
                            if not isinstance(b, int) or b >= 1:
                                add(b - 1, 1 - j)
                        wait(dve, s_out, NOUT * b + use + 1)
                        o = out_p[:, use % OUTS, (t * P if gelu else (e % 4) * P):][:, 0:P]
                        sc = share[:, j, t, e:e + 1]
                        if t not in last:
                            wait(dve, s_tr, b - 1)
                        if e == 0 and gelu:
                            ins = dve.tensor_scalar(acc[:, j, t, :], o, sc, None, ALU.mult)
                        else:
                            if t in last:
                                wait(dve, s_acc, ACC * b + last[t] + 1)
                            ins = dve.scalar_tensor_tensor(acc[:, j, t, :], o, sc, acc[:, j, t, :] if t in last else m.attn[:, b, t, :],
                                                           ALU.mult, ALU.add)
                        ins.then_inc(s_acc, 1)
                        last[t] = n

                for k in range(8):
                    gate(0, 0, k)
                batches(dve, emit)
                add(B - 1, 1)


def store(nc, m, a, out):
    with ExitStack() as c:
        sem = lambda n: nc.alloc_semaphore("st_" + n)
        rows = c.enter_context(nc.sbuf_tensor("st_rows", [P, B, TB, P], F32))
        turned = c.enter_context(nc.psum_tensor("st_turned", [P, 4, S], F32))
        s_t, s_c, s_o = sem("t"), sem("c"), sem("o")
        with nc.Block() as block:
            @block.tensor
            def _(pe):
                for b in range(B):
                    if b >= 4:
                        pe.wait_ge(s_c, b - 3)
                    for t in range(TB):
                        mm = pe.transpose(turned[:, b % 4, t * P:(t + 1) * P], m.xT[:, b, t * P:(t + 1) * P], m.ident[:, :])
                    mm.then_inc(s_t, 1)

            @block.vector
            def _(dve):
                for b in range(B):
                    dve.wait_ge(s_t, b + 1)
                    dve.tensor_copy(rows[:, b, :, :].rearrange("p t d -> p (t d)"), turned[:, b % 4, :]).then_inc(s_c, 1)

            @block.sync
            def _(sp):
                for b in range(B):
                    sp.wait_ge(s_c, b + 1)
                    sp.dma_start(out[b].rearrange("(t p) d -> p t d", p=P), rows[:, b, :, :]).then_inc(s_o, 16)
                sp.wait_ge(s_o, 16 * B)


def program(nc, a, out, upto=99, dump=None):
    m = Memory()
    with ExitStack() as ctx:
        sb = sb1 = lambda n, s, d=F32: ctx.enter_context(nc.sbuf_tensor(n, s, d))
        m.ident = sb("ident", [P, P])
        m.ident_b = sb("ident_b", [P, P], BF16)
        m.mean_w = sb("mean_w", [P, P])
        m.xT = sb("xT", [P, B, S])
        m.small_T = sb("small_T", [P, 3, EX])
        m.mod = sb("mod", [P, 2, 6, B])
        m.qk_w = sb("qk_w", [P, 3])
        m.eps = sb("eps", [P, 2])
        m.parts = nc.dram_tensor("parts", (B, 3, HEADS, ROWS, S), BF16, kind="Internal").ap()
        m.v_store = nc.dram_tensor("v_store", (B, QUADS, P, TB * QUAD * COL), F32, kind="Internal").ap()
        m.vp_store = nc.dram_tensor("vp_store", (B, QUADS, P, TB * QUAD * COL), BF16, kind="Internal").ap()

        def phase(build, *args):
            with nc.cleanup_on_exit():
                build(nc, m, *args)

        with ExitStack() as layer0:
            sb = lambda n, s, d=F32: layer0.enter_context(nc.sbuf_tensor(n, s, d))
            m.hT = sb("h0T", [P, B, WINDOW + S])
            m.wqT = sb("wqT", [P, HEADS * HD0])
            m.wkvT = sb("wkvT", [P, 2 * KV0 * HD0])
            m.woT = sb("woT", [P, PAIRS, P])
            phase(setup, a, ctx)
            phase(layer_norm, 0, 0, "ln0_")
            if upto >= 1:
                phase(window_attention, a)
            if upto >= 2:
                phase(layer_norm, 0, 1, "ln1_")
                phase(experts, a, True)
        m.attn = sb1("attn", [P, B, TB, P])
        m.mean = sb1("mean", [P, B, HEADS * TB])
        m.sd = sb1("sd", [P, B, HEADS * TB])
        m.sumv = sb1("sumv", [P, B, HEADS, VW])
        if upto >= 3:
            with ExitStack() as attention:
                m.hT = attention.enter_context(nc.sbuf_tensor("h1T", [P, B, WINDOW + S], F32))
                phase(layer_norm, 1, 0, "ln2_")
                phase(project, a, True)
            phase(search_attention, a)
            phase(attention_out, a)
        if upto >= 4:
            with ExitStack() as last:
                m.hT = last.enter_context(nc.sbuf_tensor("h2T", [P, B, WINDOW + S], F32))
                phase(layer_norm, 1, 1, "ln3_")
                phase(project, a, False)
                phase(dense_attention, a)
                phase(experts, a, False)
            if out is not None:
                phase(store, a, out)
        if dump:
            dump(nc, m, ctx)


def constants():
    import numpy as np
    bf16 = mybir.dt.np(BF16)
    out = {"c_ident": np.eye(P, dtype=np.float32), "c_ident_b": np.eye(P).astype(bf16)}
    stat2 = np.zeros((6, 2, 2, S))
    stat2[3:6, 0] = 1.0
    stat2[0:3, 1] = 1.0
    out["c_stat2"] = stat2.astype(bf16)
    out["c_stat1"] = np.ones((3, 1, 2, S)).astype(bf16)
    of_head = np.arange(P) // HD1
    out["c_block"] = ((of_head[:, None] == of_head[None, :]) / S).astype(np.float32)
    out["c_heads"] = (of_head[:, None] == np.arange(HEADS)[None, :]).astype(np.float32)
    out["c_ranks"] = np.tile(np.arange(9, dtype=np.float32), (P, 1))
    half = np.zeros((P, P + 2), np.float32)
    for i in range(2):
        half[HD0 * i:HD0 * (i + 1), HD0 * i:HD0 * (i + 1)] = 1.0 / HD0
        half[HD0 * i:HD0 * (i + 1), P + i] = 1.0 / HD0
    out["c_half"] = half
    query, key = np.arange(P)[:, None], np.arange(WIN)[None, :]
    rel = key - WINDOW - query % SUB
    slopes = (2.0 ** (-0.5)) ** np.arange(1, HEADS + 1, dtype=np.float32)
    table = np.zeros((P, 2, HEADS, WIN), np.float32)
    for first in range(2):
        masked = (rel > 0) | (rel < -WINDOW)
        if first == 0:
            masked = masked | (query + rel < 0)
        for h in range(HEADS):
            table[:, first, h] = np.where(masked, -1e30, slopes[h] * rel.astype(np.float32))
    out["c_bias"] = table.reshape(P, 2, PAIRS, 2, WIN)
    return out


def kernel(**inputs):
    import numpy as _np
    import concourse.bacc as _bacc
    from concourse.bass_utils import run_bass_kernel_spmd as _run

    nc = _bacc.Bacc("TRN2", target_bir_lowering=False, num_devices=1)
    arrays, aps = {}, {}
    for name, x in list(inputs.items()) + list(constants().items()):
        x = _np.ascontiguousarray(x)
        arrays[f"in_{name}_dram"] = x
        aps[name] = nc.dram_tensor(f"in_{name}_dram", x.shape, mybir.dt.from_np(x.dtype), kind="ExternalInput").ap()
    out = nc.dram_tensor("out_dram", (B, S, P), F32, kind="ExternalOutput").ap()
    program(nc, aps, out)
    r = _run(nc, [arrays], core_ids=[0])
    return r.results[0]["out_dram"]
```
